# Optimizing a Trainium2 kernel written in Bass

```python
import numpy as np
import jax
import jax.numpy as jnp

def _softmax(x, axis=-1):
    return jax.nn.softmax(x, axis=axis)

def _gelu(x):
    return jax.nn.gelu(x, approximate=True)

def _silu(x):
    return jax.nn.silu(x)

def _sigmoid(x):
    return jax.nn.sigmoid(x)

def _layernorm(x, axis=-1, eps=1e-05):
    m = jnp.mean(x, axis=axis, keepdims=True)
    v = jnp.var(x, axis=axis, keepdims=True)
    return (x - m) / jnp.sqrt(v + eps)

def _scatter_add(tgt, idx, src, axis=0):
    return tgt.at[idx].add(src)

def _segment_sum(src, seg, n):
    return jax.ops.segment_sum(src, seg, n)
kernel_name = 'mk_decoder_preln_d2_seqx_r8_1e6664'

def setup_inputs(seed: int=0):
    np.random.seed(seed)
    _w = jnp.asarray

    def _rec_inputs():
        import jax
        import jax.numpy as jnp
        _rk = jax.random.key(seed)
        x = 7.22e-05 + 1 * jax.random.normal(jax.random.fold_in(_rk, 1), (16, 256, 128), jnp.float32)
        _lenS = 256 - jax.random.randint(jax.random.fold_in(_rk, 7), (16,), 0, max(1, 256 // 4) + 1, jnp.int32)
        _lenS2 = 1601 - jax.random.randint(jax.random.fold_in(_rk, 8), (16,), 0, max(1, 1601 // 4) + 1, jnp.int32)
        _ctx_768P = jax.random.normal(jax.random.fold_in(_rk, 11), (16, 16, 96), jnp.float32)
        _ctx_768c = jax.random.dirichlet(jax.random.fold_in(_rk, 511), 0.3 * jnp.ones((16,), jnp.float32), (16, 1601))
        _ctx_768t = jnp.einsum('bsk,bkd->bsd', _ctx_768c, _ctx_768P)
        _ctx_768t = _ctx_768t * jax.lax.rsqrt(jnp.mean(jnp.square(_ctx_768t)) + 1e-12) * 0.953939
        ctx_768 = -0.000191848 + 0.999787 * (_ctx_768t + 0.3 * jax.random.normal(jax.random.fold_in(_rk, 611), (16, 1601, 96), jnp.float32))
        return (x, ctx_768)
    x, ctx_768 = _rec_inputs()

    def _L0_attn_setup():
        import jax, jax.numpy as jnp
        import numpy as np
        B, L, D, H = (1, 256, 128, 16)
        d = D // H

        def _forward(x, Wqkv_w, Wqkv_b, out_w, out_b, W_static, Lambda_raw, Gamma, gate_w1, gate_b1, gate_w2, gate_b2):
            Bb, Ll, Dm = x.shape
            Hh = Gamma.shape[0]
            dd = Dm // Hh
            scale = 1.0 / np.sqrt(dd)
            qkv = (x @ Wqkv_w + Wqkv_b).reshape(Bb, Ll, 3, Hh, dd)
            q = jnp.transpose(qkv[:, :, 0], (0, 2, 1, 3))
            k = jnp.transpose(qkv[:, :, 1], (0, 2, 1, 3))
            v = jnp.transpose(qkv[:, :, 2], (0, 2, 1, 3))
            scores = jnp.einsum('bhid,bhjd->bhij', q, k) * scale
            causal_mask = jnp.triu(jnp.full((Ll, Ll), -10000.0, dtype=scores.dtype), 1)
            attn = jax.nn.softmax(scores + causal_mask, axis=-1)
            y_softmax = jnp.einsum('bhij,bhjd->bhid', attn, v)
            retention = 1.0 - jax.nn.sigmoid(Lambda_raw)
            k_stp = k * scale

            def step(state, inp):
                q_t, k_t, v_t = inp
                hebbian = v_t[..., :, None] * k_t[..., None, :]
                state = retention * state + Gamma * hebbian
                y_t = jnp.einsum('bhij,bhj->bhi', W_static + state, q_t)
                return (state, y_t)
            state0 = jnp.zeros((Bb, Hh, dd, dd), x.dtype)
            qT = jnp.moveaxis(q, 2, 0)
            kT = jnp.moveaxis(k_stp, 2, 0)
            vT = jnp.moveaxis(v, 2, 0)
            _, ys = jax.lax.scan(step, state0, (qT, kT, vT))
            y_stp = jnp.moveaxis(ys, 0, 2)
            g = jax.nn.gelu(x @ gate_w1 + gate_b1, approximate=False)
            alpha = jax.nn.sigmoid(g @ gate_w2 + gate_b2)
            alpha = jnp.transpose(alpha, (0, 2, 1))[..., None]
            y = alpha * y_softmax + (1.0 - alpha) * y_stp
            y = jnp.transpose(y, (0, 2, 1, 3)).reshape(Bb, Ll, Dm)
            return y @ out_w + out_b
        key = jax.random.key(seed)
        ks = jax.random.split(key, 8)
        s = 1.0 / np.sqrt(D)
        return {'x': jax.random.normal(ks[0], (B, L, D), jnp.float32), 'Wqkv_w': jax.random.normal(ks[1], (D, 3 * D), jnp.float32) * s, 'Wqkv_b': jnp.zeros((3 * D,), jnp.float32), 'out_w': jax.random.normal(ks[2], (D, D), jnp.float32) * s, 'out_b': jnp.zeros((D,), jnp.float32), 'W_static': jnp.zeros((H, d, d), jnp.float32), 'Lambda_raw': jax.random.uniform(ks[3], (H, d, d), jnp.float32, -3.0, 3.0), 'Gamma': jax.random.uniform(ks[4], (H, d, d), jnp.float32, -0.5 / np.sqrt(d), 0.5 / np.sqrt(d)), 'gate_w1': jax.random.normal(ks[5], (D, D // 2), jnp.float32) * s, 'gate_b1': jnp.zeros((D // 2,), jnp.float32), 'gate_w2': jax.random.normal(ks[6], (D // 2, H), jnp.float32) * (1.0 / np.sqrt(D // 2)), 'gate_b2': jnp.zeros((H,), jnp.float32)}
    _L0_attn_all = _L0_attn_setup()
    _L0_attn_in = {k: v for k, v in _L0_attn_all.items() if k in ('Wqkv_w', 'Wqkv_b', 'out_w', 'out_b', 'W_static', 'Lambda_raw', 'Gamma', 'gate_w1', 'gate_b1', 'gate_w2', 'gate_b2')}
    del _L0_attn_all

    def _L0_xattn_setup():
        import jax, jax.numpy as jnp
        import numpy as np
        NUM_HEADS = 16
        CLAMP = 10000.0
        key = jax.random.key(seed)
        ks = jax.random.split(key, 8)
        B, Nq, Nkv, Cq, Ckv = (4, 256, 256, 128, 96)
        s_q = 1.0 / np.sqrt(Cq)
        s_kv = 1.0 / np.sqrt(Ckv)
        return {'query': jax.random.normal(ks[0], (B, Nq, Cq), jnp.float32), 'key_value': jax.random.normal(ks[1], (B, Nkv, Ckv), jnp.float32), 'Wq': jax.random.normal(ks[2], (Cq, Cq), jnp.float32) * s_q, 'bq': jnp.zeros((Cq,), jnp.float32), 'Wk': jax.random.normal(ks[3], (Ckv, Cq), jnp.float32) * s_kv, 'bk': jnp.zeros((Cq,), jnp.float32), 'Wv': jax.random.normal(ks[4], (Ckv, Cq), jnp.float32) * s_kv, 'bv': jnp.zeros((Cq,), jnp.float32), 'Wo': jax.random.normal(ks[5], (Cq, Cq), jnp.float32) * s_q, 'bo': jnp.zeros((Cq,), jnp.float32)}
    _L0_xattn_all = _L0_xattn_setup()
    _L0_xattn_in = {k: v for k, v in _L0_xattn_all.items() if k in ('Wq', 'bq', 'Wk', 'bk', 'Wv', 'bv', 'Wo', 'bo')}
    del _L0_xattn_all

    def _L0_ffn_setup():
        import jax, jax.numpy as jnp
        import numpy as np
        N_EXPERTS = 32
        TOP_K = 8
        N_GROUP = 4
        TOPK_GROUP = 2
        ROUTED_SCALING = 2.5

        def _gate(x, gate_w, gate_bias):
            T, E = (x.shape[0], gate_w.shape[0])
            logits = jnp.einsum('th,eh->te', x, gate_w)
            scores = jax.nn.sigmoid(logits)
            scores_choice = scores + gate_bias[None, :]
            grp = scores_choice.reshape(T, N_GROUP, E // N_GROUP)
            top2, _ = jax.lax.top_k(grp, 2)
            group_scores = top2.sum(-1)
            _, grp_idx = jax.lax.top_k(group_scores, TOPK_GROUP)
            group_mask = jax.nn.one_hot(grp_idx, N_GROUP, dtype=scores.dtype).sum(1)
            expert_mask = jnp.repeat(group_mask, E // N_GROUP, axis=1)
            masked = jnp.where(expert_mask > 0, scores_choice, 0.0)
            _, topk_idx = jax.lax.top_k(masked, TOP_K)
            topk_w = jnp.take_along_axis(scores, topk_idx, axis=1)
            topk_w = topk_w / (topk_w.sum(-1, keepdims=True) + 1e-20)
            topk_w = topk_w * ROUTED_SCALING
            return (topk_idx, topk_w)

        def _mlp(x, wg, wu, wd):
            return jnp.einsum('...i,hi->...h', jax.nn.silu(jnp.einsum('...h,ih->...i', x, wg)) * jnp.einsum('...h,ih->...i', x, wu), wd)
        key = jax.random.key(seed)
        ks = jax.random.split(key, 9)
        B, S, H, I = (2, 64, 128, 64)
        w = 0.02
        return {'hidden_states': jax.random.normal(ks[0], (B, S, H), jnp.float32), 'gate_w': jax.random.normal(ks[1], (N_EXPERTS, H), jnp.float32) * w, 'gate_bias': jax.random.normal(ks[2], (N_EXPERTS,), jnp.float32) * w, 'expert_gate': jax.random.normal(ks[3], (N_EXPERTS, I, H), jnp.float32) * w, 'expert_up': jax.random.normal(ks[4], (N_EXPERTS, I, H), jnp.float32) * w, 'expert_down': jax.random.normal(ks[5], (N_EXPERTS, H, I), jnp.float32) * w, 'shared_gate': jax.random.normal(ks[6], (2 * I, H), jnp.float32) * w, 'shared_up': jax.random.normal(ks[7], (2 * I, H), jnp.float32) * w, 'shared_down': jax.random.normal(ks[8], (H, 2 * I), jnp.float32) * w}
    _L0_ffn_all = _L0_ffn_setup()
    _L0_ffn_in = {k: v for k, v in _L0_ffn_all.items() if k in ('gate_w', 'gate_bias', 'expert_gate', 'expert_up', 'expert_down', 'shared_gate', 'shared_up', 'shared_down')}
    del _L0_ffn_all

    def _L1_attn_setup():
        import jax, jax.numpy as jnp
        import numpy as np
        H, DK, DV = (8, 64, 128)
        DECAY, THR, SBETA = (0.9, 0.5, 10.0)
        EPS = 1e-06

        def _rms(h, w):
            return h * jax.lax.rsqrt(jnp.mean(h * h, axis=-1, keepdims=True) + EPS) * w

        def _forward(x, w_norm_in, conv_w, conv_b, wq, wk, wv, w_out, w_spike, w_au, b_au, w_ad, b_ad, alpha_spike, w_beta, b_beta, beta_spike, w_hn, w_u1, b_u1, w_u2, b_u2, w_ffn, w_ff1, w_ff3, w_ff2):
            B, T, D = x.shape
            h = _rms(x, w_norm_in)
            CK = conv_w.shape[-1]
            hp = jnp.pad(h, ((0, 0), (CK - 1, 0), (0, 0)))
            conv = conv_b + sum((hp[:, j:j + T, :] * conv_w[:, j] for j in range(CK)))
            h = jax.nn.silu(conv)
            q = (h @ wq).reshape(B, T, H, DK)
            k = (h @ wk).reshape(B, T, H, DK)
            v = (h @ wv).reshape(B, T, H, DV)
            q = q / (jnp.linalg.norm(q, axis=-1, keepdims=True) + EPS)
            k = k / (jnp.linalg.norm(k, axis=-1, keepdims=True) + EPS)
            sd = (h @ w_spike).reshape(B, T, H, DK)
            ab = (jax.nn.silu(h @ w_au + b_au) @ w_ad + b_ad).reshape(B, T, H, DK)
            bb = h @ w_beta + b_beta

            def step(carry, inp):
                s, mem = carry
                qt, kt, vt, sdt, abt, bbt = inp
                mem = DECAY * mem + sdt
                sur = jax.nn.sigmoid(SBETA * (mem - THR))
                hard = (mem > THR).astype(x.dtype)
                spike = sur + jax.lax.stop_gradient(hard - sur)
                mem = mem - spike * THR
                alpha = jax.nn.sigmoid(abt + alpha_spike * spike)
                beta = jax.nn.sigmoid(bbt[..., None] + jnp.sum(spike * beta_spike, axis=-1, keepdims=True))
                active = jax.lax.stop_gradient((jnp.sum(hard, axis=-1, keepdims=True) > 0).astype(x.dtype))
                alpha = jnp.where(active > 0, alpha, jnp.ones_like(alpha))
                beta = beta * active
                s = s * alpha[..., None]
                u = jnp.einsum('bhd,bhdv->bhv', kt, s)
                s = s - beta[..., None] * jnp.einsum('bhd,bhv->bhdv', kt, u)
                s = s + beta[..., None] * jnp.einsum('bhd,bhv->bhdv', kt, vt)
                out = jnp.einsum('bhdv,bhd->bhv', s, qt)
                return ((s, mem), out)
            s0 = jnp.zeros((B, H, DK, DV), x.dtype)
            m0 = jnp.zeros((B, H, DK), x.dtype)
            tmaj = lambda a: jnp.moveaxis(a, 1, 0)
            (s, mem), outs = jax.lax.scan(step, (s0, m0), (tmaj(q), tmaj(k), tmaj(v), tmaj(sd), tmaj(ab), tmaj(bb)))
            y = jnp.moveaxis(outs, 0, 1)
            y = y * jax.lax.rsqrt(jnp.mean(y * y, axis=-1, keepdims=True) + EPS) * w_hn
            y = y.reshape(B, T, H * DV)
            gate = jax.nn.sigmoid(jax.nn.silu(x @ w_u1 + b_u1) @ w_u2 + b_u2)
            y = x + y @ w_out * gate
            h2 = _rms(y, w_ffn)
            y = y + jax.nn.silu(h2 @ w_ff1) * (h2 @ w_ff3) @ w_ff2
            return (y, s, mem)

        def _reference_tuple_inner(x, w_norm_in, conv_w, conv_b, wq, wk, wv, w_out, w_spike, w_au, b_au, w_ad, b_ad, alpha_spike, w_beta, b_beta, beta_spike, w_hn, w_u1, b_u1, w_u2, b_u2, w_ffn, w_ff1, w_ff3, w_ff2):
            return _forward(x, w_norm_in, conv_w, conv_b, wq, wk, wv, w_out, w_spike, w_au, b_au, w_ad, b_ad, alpha_spike, w_beta, b_beta, beta_spike, w_hn, w_u1, b_u1, w_u2, b_u2, w_ffn, w_ff1, w_ff3, w_ff2)
        key = jax.random.key(seed)
        B, T, D = (8, 256, 128)
        R, F, CK = (64, 512, 4)
        ks = jax.random.split(key, 16)
        n = lambda k, shp, s=0.02: jax.random.normal(k, shp, jnp.float32) * s
        return {'x': jax.random.normal(ks[0], (B, T, D), jnp.float32), 'w_norm_in': jnp.ones((D,), jnp.float32), 'conv_w': n(ks[1], (D, CK), 0.2), 'conv_b': jnp.zeros((D,), jnp.float32), 'wq': n(ks[2], (D, H * DK)), 'wk': n(ks[3], (D, H * DK)), 'wv': n(ks[4], (D, H * DV)), 'w_out': n(ks[5], (H * DV, D)), 'w_spike': n(ks[6], (D, H * DK), 0.1), 'w_au': n(ks[7], (D, R)), 'b_au': jnp.zeros((R,), jnp.float32), 'w_ad': n(ks[8], (R, H * DK)), 'b_ad': jnp.zeros((H * DK,), jnp.float32), 'alpha_spike': jnp.zeros((1, H, DK), jnp.float32), 'w_beta': n(ks[9], (D, H)), 'b_beta': jnp.zeros((H,), jnp.float32), 'beta_spike': jnp.zeros((1, H, DK), jnp.float32), 'w_hn': jnp.ones((H, DV), jnp.float32), 'w_u1': n(ks[10], (D, R)), 'b_u1': jnp.zeros((R,), jnp.float32), 'w_u2': n(ks[11], (R, D)), 'b_u2': jnp.zeros((D,), jnp.float32), 'w_ffn': jnp.ones((D,), jnp.float32), 'w_ff1': n(ks[12], (D, F)), 'w_ff3': n(ks[13], (D, F)), 'w_ff2': n(ks[14], (F, D))}
    _L1_attn_all = _L1_attn_setup()
    _L1_attn_in = {k: v for k, v in _L1_attn_all.items() if k in ('w_norm_in', 'conv_w', 'conv_b', 'wq', 'wk', 'wv', 'w_out', 'w_spike', 'w_au', 'b_au', 'w_ad', 'b_ad', 'alpha_spike', 'w_beta', 'b_beta', 'beta_spike', 'w_hn', 'w_u1', 'b_u1', 'w_u2', 'b_u2', 'w_ffn', 'w_ff1', 'w_ff3', 'w_ff2')}
    del _L1_attn_all

    def _L1_xattn_setup():
        import jax, jax.numpy as jnp
        import numpy as np
        B, LQ, LKV = (4, 64, 256)
        DQ, DKV, H = (128, 96, 16)
        HD = DQ // H
        key = jax.random.key(seed)
        ks = jax.random.split(key, 12)
        s_q = 1.0 / np.sqrt(DQ)
        s_kv = 1.0 / np.sqrt(DKV)
        return {'q': jax.random.normal(ks[0], (B, LQ, DQ), jnp.float32), 'kv': jax.random.normal(ks[1], (B, LKV, DKV), jnp.float32), 'Wq': jax.random.normal(ks[2], (DQ, DQ), jnp.float32) * s_q, 'bq': jnp.zeros((DQ,), jnp.float32), 'Wk': jax.random.normal(ks[3], (DKV, DQ), jnp.float32) * s_kv, 'bk': jnp.zeros((DQ,), jnp.float32), 'Wv': jax.random.normal(ks[4], (DKV, DQ), jnp.float32) * s_kv, 'bv': jnp.zeros((DQ,), jnp.float32), 'Wo': jax.random.normal(ks[5], (DQ, DQ), jnp.float32) * s_q, 'bo': jnp.zeros((DQ,), jnp.float32), 'scale': jnp.ones((1,), jnp.float32) * DQ ** (-0.5)}
    _L1_xattn_all = _L1_xattn_setup()
    _L1_xattn_in = {k: v for k, v in _L1_xattn_all.items() if k in ('Wq', 'bq', 'Wk', 'bk', 'Wv', 'bv', 'Wo', 'bo', 'scale')}
    del _L1_xattn_all

    def _L1_ffn_setup():
        import math
        import jax, jax.numpy as jnp
        import numpy as np
        B, S, H = (4, 256, 128)
        E, K, I = (8, 2, 128)
        NSH = 2
        CF, RSF = (1.25, 1.0)
        key = jax.random.key(seed)
        ks = jax.random.split(key, 8)
        w = lambda k, sh: jax.random.normal(k, sh, dtype=jnp.float32) * 0.02
        return {'hidden_states': jax.random.normal(ks[0], (B, S, H), dtype=jnp.float32), 'gate_w': w(ks[1], (E, H)), 'we_gate': w(ks[2], (E, I, H)), 'we_up': w(ks[3], (E, I, H)), 'we_down': w(ks[4], (E, H, I)), 'ws_gate': w(ks[5], (NSH * I, H)), 'ws_up': w(ks[6], (NSH * I, H)), 'ws_down': w(ks[7], (H, NSH * I))}
    _L1_ffn_all = _L1_ffn_setup()
    _L1_ffn_in = {k: v for k, v in _L1_ffn_all.items() if k in ('gate_w', 'we_gate', 'we_up', 'we_down', 'ws_gate', 'ws_up', 'ws_down')}
    del _L1_ffn_all
    return {'x': x, 'ctx_768': ctx_768, 'L0_attn_Wqkv_w': _L0_attn_in['Wqkv_w'], 'L0_attn_Wqkv_b': _L0_attn_in['Wqkv_b'], 'L0_attn_out_w': _L0_attn_in['out_w'], 'L0_attn_out_b': _L0_attn_in['out_b'], 'L0_attn_W_static': _L0_attn_in['W_static'], 'L0_attn_Lambda_raw': _L0_attn_in['Lambda_raw'], 'L0_attn_Gamma': _L0_attn_in['Gamma'], 'L0_attn_gate_w1': _L0_attn_in['gate_w1'], 'L0_attn_gate_b1': _L0_attn_in['gate_b1'], 'L0_attn_gate_w2': _L0_attn_in['gate_w2'], 'L0_attn_gate_b2': _L0_attn_in['gate_b2'], 'L0_xattn_Wq': _L0_xattn_in['Wq'], 'L0_xattn_bq': _L0_xattn_in['bq'], 'L0_xattn_Wk': _L0_xattn_in['Wk'], 'L0_xattn_bk': _L0_xattn_in['bk'], 'L0_xattn_Wv': _L0_xattn_in['Wv'], 'L0_xattn_bv': _L0_xattn_in['bv'], 'L0_xattn_Wo': _L0_xattn_in['Wo'], 'L0_xattn_bo': _L0_xattn_in['bo'], 'L0_ffn_gate_w': _L0_ffn_in['gate_w'], 'L0_ffn_gate_bias': _L0_ffn_in['gate_bias'], 'L0_ffn_expert_gate': _L0_ffn_in['expert_gate'], 'L0_ffn_expert_up': _L0_ffn_in['expert_up'], 'L0_ffn_expert_down': _L0_ffn_in['expert_down'], 'L0_ffn_shared_gate': _L0_ffn_in['shared_gate'], 'L0_ffn_shared_up': _L0_ffn_in['shared_up'], 'L0_ffn_shared_down': _L0_ffn_in['shared_down'], 'L1_attn_w_norm_in': _L1_attn_in['w_norm_in'], 'L1_attn_conv_w': _L1_attn_in['conv_w'], 'L1_attn_conv_b': _L1_attn_in['conv_b'], 'L1_attn_wq': _L1_attn_in['wq'], 'L1_attn_wk': _L1_attn_in['wk'], 'L1_attn_wv': _L1_attn_in['wv'], 'L1_attn_w_out': _L1_attn_in['w_out'], 'L1_attn_w_spike': _L1_attn_in['w_spike'], 'L1_attn_w_au': _L1_attn_in['w_au'], 'L1_attn_b_au': _L1_attn_in['b_au'], 'L1_attn_w_ad': _L1_attn_in['w_ad'], 'L1_attn_b_ad': _L1_attn_in['b_ad'], 'L1_attn_alpha_spike': _L1_attn_in['alpha_spike'], 'L1_attn_w_beta': _L1_attn_in['w_beta'], 'L1_attn_b_beta': _L1_attn_in['b_beta'], 'L1_attn_beta_spike': _L1_attn_in['beta_spike'], 'L1_attn_w_hn': _L1_attn_in['w_hn'], 'L1_attn_w_u1': _L1_attn_in['w_u1'], 'L1_attn_b_u1': _L1_attn_in['b_u1'], 'L1_attn_w_u2': _L1_attn_in['w_u2'], 'L1_attn_b_u2': _L1_attn_in['b_u2'], 'L1_attn_w_ffn': _L1_attn_in['w_ffn'], 'L1_attn_w_ff1': _L1_attn_in['w_ff1'], 'L1_attn_w_ff3': _L1_attn_in['w_ff3'], 'L1_attn_w_ff2': _L1_attn_in['w_ff2'], 'L1_xattn_Wq': _L1_xattn_in['Wq'], 'L1_xattn_bq': _L1_xattn_in['bq'], 'L1_xattn_Wk': _L1_xattn_in['Wk'], 'L1_xattn_bk': _L1_xattn_in['bk'], 'L1_xattn_Wv': _L1_xattn_in['Wv'], 'L1_xattn_bv': _L1_xattn_in['bv'], 'L1_xattn_Wo': _L1_xattn_in['Wo'], 'L1_xattn_bo': _L1_xattn_in['bo'], 'L1_xattn_scale': _L1_xattn_in['scale'], 'L1_ffn_gate_w': _L1_ffn_in['gate_w'], 'L1_ffn_we_gate': _L1_ffn_in['we_gate'], 'L1_ffn_we_up': _L1_ffn_in['we_up'], 'L1_ffn_we_down': _L1_ffn_in['we_down'], 'L1_ffn_ws_gate': _L1_ffn_in['ws_gate'], 'L1_ffn_ws_up': _L1_ffn_in['ws_up'], 'L1_ffn_ws_down': _L1_ffn_in['ws_down']}

def reference(x, ctx_768, L0_attn_Wqkv_w, L0_attn_Wqkv_b, L0_attn_out_w, L0_attn_out_b, L0_attn_W_static, L0_attn_Lambda_raw, L0_attn_Gamma, L0_attn_gate_w1, L0_attn_gate_b1, L0_attn_gate_w2, L0_attn_gate_b2, L0_xattn_Wq, L0_xattn_bq, L0_xattn_Wk, L0_xattn_bk, L0_xattn_Wv, L0_xattn_bv, L0_xattn_Wo, L0_xattn_bo, L0_ffn_gate_w, L0_ffn_gate_bias, L0_ffn_expert_gate, L0_ffn_expert_up, L0_ffn_expert_down, L0_ffn_shared_gate, L0_ffn_shared_up, L0_ffn_shared_down, L1_attn_w_norm_in, L1_attn_conv_w, L1_attn_conv_b, L1_attn_wq, L1_attn_wk, L1_attn_wv, L1_attn_w_out, L1_attn_w_spike, L1_attn_w_au, L1_attn_b_au, L1_attn_w_ad, L1_attn_b_ad, L1_attn_alpha_spike, L1_attn_w_beta, L1_attn_b_beta, L1_attn_beta_spike, L1_attn_w_hn, L1_attn_w_u1, L1_attn_b_u1, L1_attn_w_u2, L1_attn_b_u2, L1_attn_w_ffn, L1_attn_w_ff1, L1_attn_w_ff3, L1_attn_w_ff2, L1_xattn_Wq, L1_xattn_bq, L1_xattn_Wk, L1_xattn_bk, L1_xattn_Wv, L1_xattn_bv, L1_xattn_Wo, L1_xattn_bo, L1_xattn_scale, L1_ffn_gate_w, L1_ffn_we_gate, L1_ffn_we_up, L1_ffn_we_down, L1_ffn_ws_gate, L1_ffn_ws_up, L1_ffn_ws_down):
    import jax
    import jax.numpy as jnp

    def _L0_attn_ref(x, Wqkv_w, Wqkv_b, out_w, out_b, W_static, Lambda_raw, Gamma, gate_w1, gate_b1, gate_w2, gate_b2):
        import jax, jax.numpy as jnp
        import numpy as np
        B, L, D, H = (1, 256, 128, 16)
        d = D // H

        def _forward(x, Wqkv_w, Wqkv_b, out_w, out_b, W_static, Lambda_raw, Gamma, gate_w1, gate_b1, gate_w2, gate_b2):
            Bb, Ll, Dm = x.shape
            Hh = Gamma.shape[0]
            dd = Dm // Hh
            scale = 1.0 / np.sqrt(dd)
            qkv = (x @ Wqkv_w + Wqkv_b).reshape(Bb, Ll, 3, Hh, dd)
            q = jnp.transpose(qkv[:, :, 0], (0, 2, 1, 3))
            k = jnp.transpose(qkv[:, :, 1], (0, 2, 1, 3))
            v = jnp.transpose(qkv[:, :, 2], (0, 2, 1, 3))
            scores = jnp.einsum('bhid,bhjd->bhij', q, k) * scale
            causal_mask = jnp.triu(jnp.full((Ll, Ll), -10000.0, dtype=scores.dtype), 1)
            attn = jax.nn.softmax(scores + causal_mask, axis=-1)
            y_softmax = jnp.einsum('bhij,bhjd->bhid', attn, v)
            retention = 1.0 - jax.nn.sigmoid(Lambda_raw)
            k_stp = k * scale

            def step(state, inp):
                q_t, k_t, v_t = inp
                hebbian = v_t[..., :, None] * k_t[..., None, :]
                state = retention * state + Gamma * hebbian
                y_t = jnp.einsum('bhij,bhj->bhi', W_static + state, q_t)
                return (state, y_t)
            state0 = jnp.zeros((Bb, Hh, dd, dd), x.dtype)
            qT = jnp.moveaxis(q, 2, 0)
            kT = jnp.moveaxis(k_stp, 2, 0)
            vT = jnp.moveaxis(v, 2, 0)
            _, ys = jax.lax.scan(step, state0, (qT, kT, vT))
            y_stp = jnp.moveaxis(ys, 0, 2)
            g = jax.nn.gelu(x @ gate_w1 + gate_b1, approximate=False)
            alpha = jax.nn.sigmoid(g @ gate_w2 + gate_b2)
            alpha = jnp.transpose(alpha, (0, 2, 1))[..., None]
            y = alpha * y_softmax + (1.0 - alpha) * y_stp
            y = jnp.transpose(y, (0, 2, 1, 3)).reshape(Bb, Ll, Dm)
            return y @ out_w + out_b
        return _forward(x, Wqkv_w, Wqkv_b, out_w, out_b, W_static, Lambda_raw, Gamma, gate_w1, gate_b1, gate_w2, gate_b2)

    def _L0_xattn_ref(query, key_value, Wq, bq, Wk, bk, Wv, bv, Wo, bo):
        import jax, jax.numpy as jnp
        import numpy as np
        NUM_HEADS = 16
        CLAMP = 10000.0
        B, Nq, Cq = query.shape
        Nkv = key_value.shape[1]
        H = NUM_HEADS
        D = Cq // H
        scale = D ** (-0.5)
        q = (query @ Wq + bq).reshape(B, Nq, H, D).transpose(0, 2, 1, 3)
        k = (key_value @ Wk + bk).reshape(B, Nkv, H, D).transpose(0, 2, 1, 3)
        v = (key_value @ Wv + bv).reshape(B, Nkv, H, D).transpose(0, 2, 1, 3)
        attn = jnp.einsum('bhqd,bhkd->bhqk', q, k) * scale
        attn = jnp.clip(attn, -CLAMP, CLAMP)
        attn = jax.nn.softmax(attn, axis=-1)
        attn = jnp.where(jnp.any(jnp.isnan(attn)), jnp.asarray(1.0 / Nkv, attn.dtype), attn)
        x = jnp.einsum('bhqk,bhkd->bqhd', attn, v).reshape(B, Nq, Cq)
        return x @ Wo + bo

    def _L0_ffn_ref(hidden_states, gate_w, gate_bias, expert_gate, expert_up, expert_down, shared_gate, shared_up, shared_down):
        import jax, jax.numpy as jnp
        import numpy as np
        N_EXPERTS = 32
        TOP_K = 8
        N_GROUP = 4
        TOPK_GROUP = 2
        ROUTED_SCALING = 2.5

        def _gate(x, gate_w, gate_bias):
            T, E = (x.shape[0], gate_w.shape[0])
            logits = jnp.einsum('th,eh->te', x, gate_w)
            scores = jax.nn.sigmoid(logits)
            scores_choice = scores + gate_bias[None, :]
            grp = scores_choice.reshape(T, N_GROUP, E // N_GROUP)
            top2, _ = jax.lax.top_k(grp, 2)
            group_scores = top2.sum(-1)
            _, grp_idx = jax.lax.top_k(group_scores, TOPK_GROUP)
            group_mask = jax.nn.one_hot(grp_idx, N_GROUP, dtype=scores.dtype).sum(1)
            expert_mask = jnp.repeat(group_mask, E // N_GROUP, axis=1)
            masked = jnp.where(expert_mask > 0, scores_choice, 0.0)
            _, topk_idx = jax.lax.top_k(masked, TOP_K)
            topk_w = jnp.take_along_axis(scores, topk_idx, axis=1)
            topk_w = topk_w / (topk_w.sum(-1, keepdims=True) + 1e-20)
            topk_w = topk_w * ROUTED_SCALING
            return (topk_idx, topk_w)

        def _mlp(x, wg, wu, wd):
            return jnp.einsum('...i,hi->...h', jax.nn.silu(jnp.einsum('...h,ih->...i', x, wg)) * jnp.einsum('...h,ih->...i', x, wu), wd)
        orig_shape = hidden_states.shape
        H = orig_shape[-1]
        residuals = hidden_states
        x = hidden_states.reshape(-1, H)
        topk_idx, topk_w = _gate(x, gate_w, gate_bias)
        g = jnp.einsum('th,eih->eti', x, expert_gate)
        u = jnp.einsum('th,eih->eti', x, expert_up)
        outs = jnp.einsum('eti,ehi->eth', jax.nn.silu(g) * u, expert_down)
        outs_t = jnp.transpose(outs, (1, 0, 2))
        gathered = jnp.take_along_axis(outs_t, topk_idx[:, :, None], axis=1)
        final = (gathered * topk_w[:, :, None]).sum(1)
        shared = _mlp(residuals, shared_gate, shared_up, shared_down)
        return final.reshape(orig_shape) + shared

    def _L1_attn_ref(x, w_norm_in, conv_w, conv_b, wq, wk, wv, w_out, w_spike, w_au, b_au, w_ad, b_ad, alpha_spike, w_beta, b_beta, beta_spike, w_hn, w_u1, b_u1, w_u2, b_u2, w_ffn, w_ff1, w_ff3, w_ff2):
        import jax, jax.numpy as jnp
        import numpy as np
        H, DK, DV = (8, 64, 128)
        DECAY, THR, SBETA = (0.9, 0.5, 10.0)
        EPS = 1e-06

        def _rms(h, w):
            return h * jax.lax.rsqrt(jnp.mean(h * h, axis=-1, keepdims=True) + EPS) * w

        def _forward(x, w_norm_in, conv_w, conv_b, wq, wk, wv, w_out, w_spike, w_au, b_au, w_ad, b_ad, alpha_spike, w_beta, b_beta, beta_spike, w_hn, w_u1, b_u1, w_u2, b_u2, w_ffn, w_ff1, w_ff3, w_ff2):
            B, T, D = x.shape
            h = _rms(x, w_norm_in)
            CK = conv_w.shape[-1]
            hp = jnp.pad(h, ((0, 0), (CK - 1, 0), (0, 0)))
            conv = conv_b + sum((hp[:, j:j + T, :] * conv_w[:, j] for j in range(CK)))
            h = jax.nn.silu(conv)
            q = (h @ wq).reshape(B, T, H, DK)
            k = (h @ wk).reshape(B, T, H, DK)
            v = (h @ wv).reshape(B, T, H, DV)
            q = q / (jnp.linalg.norm(q, axis=-1, keepdims=True) + EPS)
            k = k / (jnp.linalg.norm(k, axis=-1, keepdims=True) + EPS)
            sd = (h @ w_spike).reshape(B, T, H, DK)
            ab = (jax.nn.silu(h @ w_au + b_au) @ w_ad + b_ad).reshape(B, T, H, DK)
            bb = h @ w_beta + b_beta

            def step(carry, inp):
                s, mem = carry
                qt, kt, vt, sdt, abt, bbt = inp
                mem = DECAY * mem + sdt
                sur = jax.nn.sigmoid(SBETA * (mem - THR))
                hard = (mem > THR).astype(x.dtype)
                spike = sur + jax.lax.stop_gradient(hard - sur)
                mem = mem - spike * THR
                alpha = jax.nn.sigmoid(abt + alpha_spike * spike)
                beta = jax.nn.sigmoid(bbt[..., None] + jnp.sum(spike * beta_spike, axis=-1, keepdims=True))
                active = jax.lax.stop_gradient((jnp.sum(hard, axis=-1, keepdims=True) > 0).astype(x.dtype))
                alpha = jnp.where(active > 0, alpha, jnp.ones_like(alpha))
                beta = beta * active
                s = s * alpha[..., None]
                u = jnp.einsum('bhd,bhdv->bhv', kt, s)
                s = s - beta[..., None] * jnp.einsum('bhd,bhv->bhdv', kt, u)
                s = s + beta[..., None] * jnp.einsum('bhd,bhv->bhdv', kt, vt)
                out = jnp.einsum('bhdv,bhd->bhv', s, qt)
                return ((s, mem), out)
            s0 = jnp.zeros((B, H, DK, DV), x.dtype)
            m0 = jnp.zeros((B, H, DK), x.dtype)
            tmaj = lambda a: jnp.moveaxis(a, 1, 0)
            (s, mem), outs = jax.lax.scan(step, (s0, m0), (tmaj(q), tmaj(k), tmaj(v), tmaj(sd), tmaj(ab), tmaj(bb)))
            y = jnp.moveaxis(outs, 0, 1)
            y = y * jax.lax.rsqrt(jnp.mean(y * y, axis=-1, keepdims=True) + EPS) * w_hn
            y = y.reshape(B, T, H * DV)
            gate = jax.nn.sigmoid(jax.nn.silu(x @ w_u1 + b_u1) @ w_u2 + b_u2)
            y = x + y @ w_out * gate
            h2 = _rms(y, w_ffn)
            y = y + jax.nn.silu(h2 @ w_ff1) * (h2 @ w_ff3) @ w_ff2
            return (y, s, mem)

        def _reference_tuple_inner(x, w_norm_in, conv_w, conv_b, wq, wk, wv, w_out, w_spike, w_au, b_au, w_ad, b_ad, alpha_spike, w_beta, b_beta, beta_spike, w_hn, w_u1, b_u1, w_u2, b_u2, w_ffn, w_ff1, w_ff3, w_ff2):
            return _forward(x, w_norm_in, conv_w, conv_b, wq, wk, wv, w_out, w_spike, w_au, b_au, w_ad, b_ad, alpha_spike, w_beta, b_beta, beta_spike, w_hn, w_u1, b_u1, w_u2, b_u2, w_ffn, w_ff1, w_ff3, w_ff2)
        return _reference_tuple_inner(x, w_norm_in, conv_w, conv_b, wq, wk, wv, w_out, w_spike, w_au, b_au, w_ad, b_ad, alpha_spike, w_beta, b_beta, beta_spike, w_hn, w_u1, b_u1, w_u2, b_u2, w_ffn, w_ff1, w_ff3, w_ff2)[0]

    def _L1_xattn_ref(q, kv, Wq, bq, Wk, bk, Wv, bv, Wo, bo, scale):
        import jax, jax.numpy as jnp
        import numpy as np
        B, LQ, LKV = (4, 64, 256)
        DQ, DKV, H = (128, 96, 16)
        HD = DQ // H
        b, lq, _ = q.shape
        lkv = kv.shape[1]
        qh = (q @ Wq + bq).reshape(b, lq, H, HD).transpose(0, 2, 1, 3)
        kh = (kv @ Wk + bk).reshape(b, lkv, H, HD).transpose(0, 2, 1, 3)
        vh = (kv @ Wv + bv).reshape(b, lkv, H, HD).transpose(0, 2, 1, 3)
        scores = jnp.einsum('bhqd,bhkd->bhqk', qh, kh) * scale[0]
        attn = jax.nn.softmax(scores, axis=-1)
        out = jnp.einsum('bhqk,bhkd->bhqd', attn, vh)
        out = out.transpose(0, 2, 1, 3).reshape(b, lq, DQ)
        return out @ Wo + bo

    def _L1_ffn_ref(hidden_states, gate_w, we_gate, we_up, we_down, ws_gate, ws_up, ws_down):
        import math
        import jax, jax.numpy as jnp
        import numpy as np
        B, S, H = (4, 256, 128)
        E, K, I = (8, 2, 128)
        NSH = 2
        CF, RSF = (1.25, 1.0)
        orig_shape = hidden_states.shape
        x = hidden_states.reshape(-1, H)
        N = x.shape[0]
        logits = x.astype(jnp.float32) @ gate_w.astype(jnp.float32).T
        scores = jax.nn.softmax(logits, axis=-1)
        topk_w, topk_idx = jax.lax.top_k(scores, K)
        topk_w = topk_w / (topk_w.sum(-1, keepdims=True) + 1e-20) * RSF
        capacity = math.ceil(CF * N * K / E)
        flat = topk_idx.reshape(-1)
        one_hot = jax.nn.one_hot(flat, E, dtype=jnp.int32)
        pos = jnp.cumsum(one_hot, axis=0) - 1
        pos_tok = jnp.take_along_axis(pos, flat[:, None], axis=1)[:, 0]
        keep = (pos_tok < capacity).reshape(N, K)
        topk_w = topk_w * keep.astype(topk_w.dtype)
        comb = jnp.zeros((N, E), jnp.float32).at[jnp.arange(N)[:, None], topk_idx].add(topk_w)
        g = jnp.einsum('nh,eih->nei', x, we_gate)
        u = jnp.einsum('nh,eih->nei', x, we_up)
        eo = jnp.einsum('nei,ehi->neh', jax.nn.silu(g) * u, we_down)
        y = jnp.einsum('neh,ne->nh', eo, comb)
        sh = jax.nn.silu(x @ ws_gate.T) * (x @ ws_up.T) @ ws_down.T
        return (y + sh).reshape(orig_shape)
    x = x + _L0_attn_ref(_layernorm(x, axis=-1), L0_attn_Wqkv_w, L0_attn_Wqkv_b, L0_attn_out_w, L0_attn_out_b, L0_attn_W_static, L0_attn_Lambda_raw, L0_attn_Gamma, L0_attn_gate_w1, L0_attn_gate_b1, L0_attn_gate_w2, L0_attn_gate_b2)
    x = x + _L0_xattn_ref(_layernorm(x, axis=-1), ctx_768, L0_xattn_Wq, L0_xattn_bq, L0_xattn_Wk, L0_xattn_bk, L0_xattn_Wv, L0_xattn_bv, L0_xattn_Wo, L0_xattn_bo)
    x = x + _L0_ffn_ref(_layernorm(x, axis=-1), L0_ffn_gate_w, L0_ffn_gate_bias, L0_ffn_expert_gate, L0_ffn_expert_up, L0_ffn_expert_down, L0_ffn_shared_gate, L0_ffn_shared_up, L0_ffn_shared_down)
    x = x + _L1_attn_ref(_layernorm(x, axis=-1), L1_attn_w_norm_in, L1_attn_conv_w, L1_attn_conv_b, L1_attn_wq, L1_attn_wk, L1_attn_wv, L1_attn_w_out, L1_attn_w_spike, L1_attn_w_au, L1_attn_b_au, L1_attn_w_ad, L1_attn_b_ad, L1_attn_alpha_spike, L1_attn_w_beta, L1_attn_b_beta, L1_attn_beta_spike, L1_attn_w_hn, L1_attn_w_u1, L1_attn_b_u1, L1_attn_w_u2, L1_attn_b_u2, L1_attn_w_ffn, L1_attn_w_ff1, L1_attn_w_ff3, L1_attn_w_ff2)
    x = x + _L1_xattn_ref(_layernorm(x, axis=-1), ctx_768, L1_xattn_Wq, L1_xattn_bq, L1_xattn_Wk, L1_xattn_bk, L1_xattn_Wv, L1_xattn_bv, L1_xattn_Wo, L1_xattn_bo, L1_xattn_scale)
    x = x + _L1_ffn_ref(_layernorm(x, axis=-1), L1_ffn_gate_w, L1_ffn_we_gate, L1_ffn_we_up, L1_ffn_we_down, L1_ffn_ws_gate, L1_ffn_ws_up, L1_ffn_ws_down)
    return x

_drawn_inputs = setup_inputs


def setup_inputs(seed=0):
    import zlib

    import numpy as np

    out = dict(_drawn_inputs(seed))
    spreads = {'L0_attn_Wqkv_b': (0.0, 0.1),
     'L0_attn_out_b': (0.0, 0.1),
     'L0_attn_W_static': (0.0, 0.1),
     'L0_attn_gate_b1': (0.0, 0.8),
     'L0_attn_gate_b2': (0.0, 0.797),
     'L0_xattn_bq': (0.0, 0.365),
     'L0_xattn_bk': (0.0, 2.0),
     'L0_xattn_bv': (0.0, 0.1),
     'L0_xattn_bo': (0.0, 0.1),
     'L1_attn_w_norm_in': (1.0, 0.2),
     'L1_attn_conv_b': (0.0, 0.1),
     'L1_attn_b_au': (0.0, 0.8),
     'L1_attn_b_ad': (0.0, 0.8),
     'L1_attn_alpha_spike': (0.0, 0.8),
     'L1_attn_b_beta': (0.0, 0.8),
     'L1_attn_beta_spike': (0.0, 0.8),
     'L1_attn_w_hn': (1.0, 0.6),
     'L1_attn_b_u1': (0.0, 0.8),
     'L1_attn_b_u2': (0.0, 0.8),
     'L1_attn_w_ffn': (1.0, 0.6),
     'L1_xattn_bq': (0.0, 2.0),
     'L1_xattn_bk': (0.0, 2.0),
     'L1_xattn_bv': (0.0, 0.795),
     'L1_xattn_bo': (0.0, 0.8)}
    factors = {'L0_ffn_gate_w': 8.0,
     'L0_ffn_gate_bias': 8.0,
     'L0_ffn_expert_gate': 8.0,
     'L0_ffn_expert_up': 8.0,
     'L0_ffn_expert_down': 8.0,
     'L0_ffn_shared_gate': 8.0,
     'L0_ffn_shared_up': 8.0,
     'L0_ffn_shared_down': 8.0,
     'L1_attn_w_spike': 4.975,
     'L1_attn_w_au': 8.0,
     'L1_attn_w_ad': 8.0,
     'L1_attn_w_beta': 8.0,
     'L1_attn_w_u1': 8.0,
     'L1_attn_w_u2': 8.0,
     'L1_attn_w_ff1': 8.0,
     'L1_attn_w_ff3': 8.0,
     'L1_attn_w_ff2': 8.0,
     'L1_xattn_Wq': 2.932,
     'L1_xattn_Wk': 2.86,
     'L1_ffn_gate_w': 8.0,
     'L1_ffn_we_gate': 8.0,
     'L1_ffn_we_up': 8.0,
     'L1_ffn_we_down': 8.0,
     'L1_ffn_ws_gate': 8.0,
     'L1_ffn_ws_up': 8.0,
     'L1_ffn_ws_down': 8.0}
    for name, (base, spread) in spreads.items():
        noise = np.random.default_rng([zlib.crc32(name.encode()), seed]).standard_normal(out[name].shape)
        drawn = base * np.exp(spread * noise) if base else spread * noise
        out[name] = jnp.asarray(drawn.astype(out[name].dtype))
    for name, factor in factors.items():
        out[name] = (out[name] * factor).astype(out[name].dtype)
    return out
```

```python
from contextlib import ExitStack

import concourse.bass as bass
from concourse import mybir

ALU = mybir.AluOpType
ACT = mybir.ActivationFunctionType
AX = mybir.AxisListType
F32 = mybir.dt.float32
BF16 = mybir.dt.bfloat16
I32 = mybir.dt.int32

P = 128
B, L, D = 16, 256, 128
NT = B * L
TILES = NT // P
LC, DC = 1601, 96
H, HD = 16, 8
HG = 4
UNITS = B * H // HG
NEG = -10000.0
CLAMP = 10000.0


class Stage:

    def __init__(self, nc, name):
        self.nc, self.name, self.ctx, self.sems = nc, name, ExitStack(), []

    def __enter__(self):
        return self

    def sb(self, name, shape, dt=F32):
        return self.ctx.enter_context(self.nc.sbuf_tensor(f"{self.name}_{name}", shape, dt))

    def ps(self, name, shape, dt=F32):
        return self.ctx.enter_context(self.nc.psum_tensor(f"{self.name}_{name}", shape, dt))

    def sem(self, name):
        s = self.nc.alloc_semaphore(f"{self.name}_{name}")
        self.sems.append(s)
        return s

    def block(self):
        return self.nc.Block(f"{self.name}_block")

    def __exit__(self, *e):
        if e[0] is None:
            for s in self.sems:
                self.nc.gpsimd.sem_clear(s)
                self.nc.release_semaphore(s)
            self.nc.all_engine_barrier()
        self.ctx.close()
        return False


def over_pairs(eng, total, body):
    body(0, 0, 0)
    body(1, 1, 0)
    with eng.Fori(1, total // 2 - 1) as j:
        body(j * 2, 0, j)
        body(j * 2 + 1, 1, j)
    body(total - 2, 0, total // 2 - 1)
    body(total - 1, 1, total // 2 - 1)


def early(n, k):
    return isinstance(n, int) and n < k


def over(eng, total, body):
    body(0)
    with eng.Fori(1, total) as n:
        body(n)


class Chain:

    def __init__(self, eng, sem):
        self.eng, self.sem, self.count = eng, sem, 0

    def __call__(self, instruction):
        self.count += 1
        instruction.then_inc(self.sem, 1)
        self.eng.wait_ge(self.sem, self.count)


def setup_stage(nc, X, ident, x_in):
    with Stage(nc, "setup") as st:
        x_loaded = st.sem("x_loaded")
        ident_zeroed = st.sem("ident_zeroed")
        with st.block() as block:
            @block.sync
            def _(sp):
                sp.dma_start(X[:, :, :], x_in.rearrange("b (s p) d -> p (b s) d", p=P)).then_inc(x_loaded, 16)
                sp.wait_ge(x_loaded, 16)

            @block.gpsimd
            def _(pool):
                pool.memset(ident[:, :], 0.0).then_inc(ident_zeroed, 1)
                pool.wait_ge(ident_zeroed, 1)
                pool.affine_select(out=ident[:, :], in_=ident[:, :], compare_op=ALU.not_equal, fill=1.0,
                                   base=0, pattern=[[-1, P]], channel_multiplier=1)


def norm_stage(nc, name, X, XT, ident, eps=1e-5, centre=True, XN=None, weight=None):
    GROUPS = 4
    GT = TILES // GROUPS
    with Stage(nc, name) as st:
        xn = XN if XN is not None else st.sb("xn", [P, TILES, D])
        sq = st.sb("sq", [P, TILES, D])
        total = st.sb("total", [P, TILES])
        mean = st.sb("mean", [P, TILES])
        power = st.sb("power", [P, TILES])
        var = st.sb("var", [P, TILES])
        std = st.sb("std", [P, TILES])
        rstd = st.sb("rstd", [P, TILES])
        wcol = st.sb("wcol", [P, 1])
        tp = st.ps("tp", [P, 2, 4, P])
        summed = st.sem("summed")
        meaned = st.sem("meaned")
        centred = st.sem("centred")
        squared = st.sem("squared")
        powered = st.sem("powered")
        var_ready = st.sem("var_ready")
        std_ready = st.sem("std_ready")
        rstd_ready = st.sem("rstd_ready")
        xn_ready = st.sem("xn_ready")
        turned = st.sem("turned")
        copied = st.sem("copied")
        w_loaded = st.sem("w_loaded")
        src = xn if centre else X

        with st.block() as block:
            @block.sync
            def _(sp):
                if weight is not None:
                    sp.dma_start(wcol[:, :], weight.rearrange("(p a) -> p a", a=1)).then_inc(w_loaded, 16)
                    sp.wait_ge(w_loaded, 16)

            @block.vector
            def _(dve):
                for g in range(GROUPS):
                    s = slice(g * GT, (g + 1) * GT)
                    if centre:
                        dve.tensor_reduce(total[:, s], X[:, s, :], AX.X, ALU.add).then_inc(summed, 1)
                        dve.wait_ge(summed, g + 1)
                        dve.tensor_scalar(mean[:, s], total[:, s], 1.0 / D, None, ALU.mult).then_inc(meaned, 1)
                        dve.wait_ge(meaned, g + 1)
                        dve.tensor_tensor(xn[:, s, :], X[:, s, :],
                                          mean[:, s].unsqueeze(2).to_broadcast([P, GT, D]),
                                          ALU.subtract).then_inc(centred, 1)
                for g in range(GROUPS):
                    s = slice(g * GT, (g + 1) * GT)
                    dve.wait_ge(squared, g + 1)
                    dve.tensor_reduce(power[:, s], sq[:, s, :], AX.X, ALU.add).then_inc(powered, 1)
                    dve.wait_ge(powered, g + 1)
                    dve.tensor_scalar(var[:, s], power[:, s], 1.0 / D, eps, ALU.mult, ALU.add).then_inc(var_ready, 1)
                for g in range(GROUPS):
                    s = slice(g * GT, (g + 1) * GT)
                    dve.wait_ge(std_ready, g + 1)
                    dve.reciprocal(rstd[:, s], std[:, s]).then_inc(rstd_ready, 1)
                    dve.wait_ge(rstd_ready, g + 1)
                    dve.tensor_tensor(xn[:, s, :], src[:, s, :], rstd[:, s].unsqueeze(2).to_broadcast([P, GT, D]),
                                      ALU.mult).then_inc(xn_ready, 1)

            @block.gpsimd
            def _(pool):
                for g in range(GROUPS):
                    s = slice(g * GT, (g + 1) * GT)
                    if centre:
                        pool.wait_ge(centred, g + 1)
                    pool.tensor_tensor(sq[:, s, :], src[:, s, :], src[:, s, :], ALU.mult).then_inc(squared, 1)

            @block.tensor
            def _(pe):
                for n in range(TILES):
                    pe.wait_ge(xn_ready, n // GT + 1)
                    if n % 4 == 0 and n >= 8:
                        pe.wait_ge(copied, n // 4 - 1)
                    ins = pe.transpose(tp[:, (n // 4) % 2, n % 4, :], xn[:, n, :], ident[:, :])
                    if n % 4 == 3:
                        ins.then_inc(turned, 1)

            @block.scalar
            def _(act):
                for g in range(GROUPS):
                    s = slice(g * GT, (g + 1) * GT)
                    act.wait_ge(var_ready, g + 1)
                    act.activation(std[:, s], var[:, s], ACT.Sqrt).then_inc(std_ready, 1)
                if weight is not None:
                    act.wait_ge(w_loaded, 16)
                for q in range(TILES // 4):
                    act.wait_ge(turned, q + 1)
                    act.activation(XT[:, q * 4 * P:(q + 1) * 4 * P], tp[:, q % 2, :, :].rearrange("p a b -> p (a b)"),
                                   ACT.Copy if weight is None else ACT.Identity,
                                   scale=1.0 if weight is None else wcol[:, 0:1]).then_inc(copied, 1)


def column(vec, base=0, n=P):
    return vec[base:base + n].rearrange("(p a) -> p a", a=1)


def project_stage(nc, name, XT, w, bias, factor, dst, wcols=0, factor_dram=None):
    with Stage(nc, name) as st:
        w_sb = st.sb("w", [P, P])
        b_sb = st.sb("b", [P, 1])
        f_sb = st.sb("f", [P, 1])
        full = st.sb("full", [P, 2, L])
        rest = st.sb("rest", [P, 2, L])
        rest2 = st.sb("rest2", [P, 2, L])
        parts = st.sb("parts", [P, 2, 3, L], BF16)
        proj = st.ps("proj", [P, 2, 512])
        loaded = st.sem("loaded")
        projected = st.sem("projected")
        biased = st.sem("biased")
        evacuated = st.sem("evacuated")
        hi_ready = st.sem("hi_ready")
        rest_ready = st.sem("rest_ready")
        mid_ready = st.sem("mid_ready")
        rest2_ready = st.sem("rest2_ready")
        lo_ready = st.sem("lo_ready")
        stored = [st.sem("stored0"), st.sem("stored1")]

        with st.block() as block:
            @block.sync
            def _(sp):
                sp.dma_start(w_sb[:, :], w[:, wcols:wcols + P]).then_inc(loaded, 16)
                sp.dma_start(b_sb[:, :], column(bias, wcols)).then_inc(loaded, 16)
                if factor_dram is not None:
                    sp.dma_start(f_sb[:, :], factor_dram.partition_broadcast(P)).then_inc(loaded, 16)

                def unit(n, u, j):
                    sp.wait_ge(lo_ready, n + 1)
                    sp.dma_start(dst[bass.ds(n, 1), :, :, :].rearrange("a p c t -> (a p) c t"),
                                 parts[:, u, :, :]).then_inc(stored[u], 16)
                over_pairs(sp, B, unit)
                sp.wait_ge(stored[0], 16 * B // 2)
                sp.wait_ge(stored[1], 16 * B // 2)

            @block.tensor
            def _(pe):
                pe.wait_ge(loaded, 48 if factor_dram is not None else 32)

                def unit(n, u, j):
                    if not early(n, 2):
                        pe.wait_ge(evacuated, n - 1)
                    pe.matmul(proj[:, u, 0:L], w_sb[:, :], XT[:, bass.ds(n * L, L)],
                              start=True, stop=True).then_inc(projected, 1)
                over_pairs(pe, B, unit)

            @block.vector
            def _(dve):
                dve.wait_ge(loaded, 48 if factor_dram is not None else 32)

                def unit(n, u, j):
                    dve.wait_ge(projected, n + 1)
                    if not early(n, 2):
                        dve.wait_ge(rest_ready, n - 1)
                    dve.tensor_scalar(full[:, u, :], proj[:, u, 0:L], b_sb[:, 0:1],
                                      f_sb[:, 0:1] if factor_dram is not None else float(factor),
                                      ALU.add, ALU.mult).then_inc(evacuated, 1)
                    dve.wait_ge(evacuated, n + 1)
                    if not early(n, 2):
                        dve.wait_ge(stored[u], j * 16)
                    dve.tensor_copy(parts[:, u, 0, :], full[:, u, :]).then_inc(hi_ready, 1)
                    dve.wait_ge(hi_ready, n + 1)
                    dve.tensor_tensor(rest[:, u, :], full[:, u, :], parts[:, u, 0, :],
                                      ALU.subtract).then_inc(rest_ready, 1)
                    dve.wait_ge(rest_ready, n + 1)
                    dve.tensor_copy(parts[:, u, 1, :], rest[:, u, :]).then_inc(mid_ready, 1)
                    dve.wait_ge(mid_ready, n + 1)
                    dve.tensor_tensor(rest2[:, u, :], rest[:, u, :], parts[:, u, 1, :],
                                      ALU.subtract).then_inc(rest2_ready, 1)
                    dve.wait_ge(rest2_ready, n + 1)
                    dve.tensor_copy(parts[:, u, 2, :], rest2[:, u, :]).then_inc(lo_ready, 1)
                over_pairs(dve, B, unit)


def value_stage(nc, name, XT, w, bias, dst):
    wcols = 2 * P
    with Stage(nc, name) as st:
        w_sb = st.sb("w", [P, P])
        b_sb = st.sb("b", [P, P])
        xs = st.sb("xs", [P, 2, 2, P])
        vt = st.sb("vt", [P, 2, 2, P])
        vp = st.ps("vp", [P, 2, 512])
        loaded = st.sem("loaded")
        x_copied = st.sem("x_copied")
        projected = st.sem("projected")
        biased = st.sem("biased")
        stored = [st.sem("stored0"), st.sem("stored1")]

        with st.block() as block:
            @block.sync
            def _(sp):
                sp.dma_start(w_sb[:, :], w[:, wcols:wcols + P]).then_inc(loaded, 16)
                sp.dma_start(b_sb[:, :], bias[wcols:wcols + P].partition_broadcast(P)).then_inc(loaded, 16)

                def unit(n, u, j):
                    sp.wait_ge(biased, n + 1)
                    for s in range(2):
                        sp.dma_start(dst[bass.ds(n, 1), :, s * P:(s + 1) * P, :].rearrange("a g p c -> (a p) g c"),
                                     vt[:, u, s, :].rearrange("p (g c) -> p g c", g=H // HG)).then_inc(stored[u], 16)
                over_pairs(sp, B, unit)
                sp.wait_ge(stored[0], 16 * B)
                sp.wait_ge(stored[1], 16 * B)

            @block.scalar
            def _(act):
                def unit(n, u, j):
                    if not early(n, 2):
                        act.wait_ge(projected, n - 1)
                    act.activation(xs[:, u, :, :].rearrange("p s t -> p (s t)"), XT[:, bass.ds(n * L, L)],
                                   ACT.Copy).then_inc(x_copied, 1)
                over_pairs(act, B, unit)

            @block.tensor
            def _(pe):
                pe.wait_ge(loaded, 32)

                def unit(n, u, j):
                    pe.wait_ge(x_copied, n + 1)
                    if not early(n, 2):
                        pe.wait_ge(biased, n - 1)
                    for s in range(2):
                        ins = pe.matmul(vp[:, u, s * P:(s + 1) * P], xs[:, u, s, :], w_sb[:, :], start=True, stop=True)
                    ins.then_inc(projected, 1)
                over_pairs(pe, B, unit)

            @block.vector
            def _(dve):
                dve.wait_ge(loaded, 32)

                def unit(n, u, j):
                    dve.wait_ge(projected, n + 1)
                    if not early(n, 2):
                        dve.wait_ge(stored[u], j * 32)
                    dve.tensor_tensor(vt[:, u, :, :], vp[:, u, 0:2 * P].rearrange("p (s t) -> p s t", s=2),
                                      b_sb[:, :].unsqueeze(1).to_broadcast([P, 2, P]),
                                      ALU.add).then_inc(biased, 1)
                over_pairs(dve, B, unit)


def context_stage(nc, name, ctx_in, ident, wk, bk, wv, bv, k_dst, v_dst):
    KT = -(-LC // P)
    TAIL = LC - (KT - 1) * P
    QUADS = [(q * 4, min(4, KT - q * 4)) for q in range(-(-KT // 4))]
    NQ = len(QUADS)
    with Stage(nc, name) as st:
        wk_sb = st.sb("wk", [DC, P])
        bk_sb = st.sb("bk", [P, 1])
        wv_sb = st.sb("wv", [DC, P])
        bv_sb = st.sb("bv", [P, P])
        cin = st.sb("cin", [P, 2, KT, DC])
        cT = st.sb("cT", [DC, 2, KT * P])
        full = st.sb("full", [P, 2, LC])
        rest = st.sb("rest", [P, 2, LC])
        parts = st.sb("parts", [P, 2, 3, LC], BF16)
        vt = st.sb("vt", [P, 2, KT, P])
        tp = st.ps("tp", [P, 2, 512])
        kp = st.ps("kp", [P, 2, 512])
        vp = st.ps("vp", [P, 2, 512])
        loaded = st.sem("loaded")
        cin_loaded = [st.sem("cin_loaded0"), st.sem("cin_loaded1")]
        turned = st.sem("turned")
        cT_ready = st.sem("cT_ready")
        k_projected = st.sem("k_projected")
        k_biased = st.sem("k_biased")
        v_projected = st.sem("v_projected")
        v_biased = st.sem("v_biased")
        hi_ready = st.sem("hi_ready")
        rest_ready = st.sem("rest_ready")
        mid_ready = st.sem("mid_ready")
        rest2_ready = st.sem("rest2_ready")
        lo_ready = st.sem("lo_ready")
        k_stored = [st.sem("k_stored0"), st.sem("k_stored1")]
        v_stored = [st.sem("v_stored0"), st.sem("v_stored1")]

        def keys_of(q):
            t0, n = QUADS[q]
            return t0 * P, min(LC, (t0 + n) * P)

        with st.block() as block:
            @block.sync
            def _(sp):
                sp.dma_start(wk_sb[:, :], wk).then_inc(loaded, 16)
                sp.dma_start(bk_sb[:, :], column(bk)).then_inc(loaded, 16)
                sp.dma_start(wv_sb[:, :], wv).then_inc(loaded, 16)
                sp.dma_start(bv_sb[:, :], bv.partition_broadcast(P)).then_inc(loaded, 16)

                def store(n, u):
                    sp.wait_ge(lo_ready, n + 1)
                    sp.dma_start(k_dst[bass.ds(n, 1), :, :, :].rearrange("a p c t -> (a p) c t"),
                                 parts[:, u, :, :]).then_inc(k_stored[u], 16)
                    sp.wait_ge(v_biased, (n + 1) * NQ)
                    for t in range(KT):
                        rows = P if t < KT - 1 else TAIL
                        sp.dma_start(v_dst[bass.ds(n, 1), :, t * P:t * P + rows, :].rearrange("a g p c -> (a p) g c"),
                                     vt[0:rows, u, t, :].rearrange("p (g c) -> p g c", g=H // HG)
                                     ).then_inc(v_stored[u], 16)

                def unit(n, u, j):
                    if not early(n, 2):
                        sp.wait_ge(turned, (n - 1) * NQ)
                    whole = (KT - 1) * P
                    sp.dma_start(cin[:, u, 0:KT - 1, :],
                                 ctx_in[bass.ds(n, 1), 0:whole, :].rearrange("a (k p) d -> p (a k) d", p=P)
                                 ).then_inc(cin_loaded[u], 16)
                    sp.dma_start(cin[0:TAIL, u, KT - 1, :],
                                 ctx_in[bass.ds(n, 1), whole:LC, :].rearrange("a p d -> (a p) d")
                                 ).then_inc(cin_loaded[u], 16)
                    if not early(n, 1):
                        store(n - 1, 1 - u)
                over_pairs(sp, B, unit)
                store(B - 1, 1)
                for u in range(2):
                    sp.wait_ge(k_stored[u], 16 * B // 2)
                    sp.wait_ge(v_stored[u], 16 * KT * B // 2)

            @block.gpsimd
            def _(pool):
                def unit(n, u, j):
                    pool.wait_ge(hi_ready, n + 1)
                    if not early(n, 2):
                        pool.wait_ge(rest2_ready, n - 1)
                        pool.wait_ge(lo_ready, n - 1)
                    pool.tensor_tensor(rest[:, u, :], full[:, u, :], parts[:, u, 0, :],
                                       ALU.subtract).then_inc(rest_ready, 1)
                    pool.wait_ge(mid_ready, n + 1)
                    pool.tensor_tensor(full[:, u, :], rest[:, u, :], parts[:, u, 1, :],
                                       ALU.subtract).then_inc(rest2_ready, 1)
                over_pairs(pool, B, unit)

            @block.tensor
            def _(pe):
                pe.wait_ge(loaded, 64)

                def unit(n, u, j):
                    pe.wait_ge(cin_loaded[u], (j + 1) * 32)
                    for q, (t0, count) in enumerate(QUADS):
                        if not (early(n, 1) and q < 2):
                            pe.wait_ge(cT_ready, n * NQ + q - 1)
                        for t in range(t0, t0 + count):
                            rows = P if t < KT - 1 else TAIL
                            ins = pe.transpose(tp[0:DC, q % 2, (t - t0) * P:(t - t0) * P + rows],
                                               cin[0:rows, u, t, :], ident[0:rows, 0:rows])
                        ins.then_inc(turned, 1)
                    for q, (t0, count) in enumerate(QUADS):
                        a, b = keys_of(q)
                        pe.wait_ge(cT_ready, n * NQ + q + 1)
                        if not (early(n, 1) and q < 2):
                            pe.wait_ge(k_biased, n * NQ + q - 1)
                        pe.matmul(kp[:, q % 2, 0:b - a], wk_sb[:, :], cT[:, u, a:b],
                                  start=True, stop=True).then_inc(k_projected, 1)
                        if not (early(n, 1) and q < 2):
                            pe.wait_ge(v_biased, n * NQ + q - 1)
                        for t in range(t0, t0 + count):
                            rows = P if t < KT - 1 else TAIL
                            ins = pe.matmul(vp[0:rows, q % 2, (t - t0) * P:(t - t0 + 1) * P],
                                            cT[:, u, t * P:t * P + rows], wv_sb[:, :], start=True, stop=True)
                        ins.then_inc(v_projected, 1)
                over_pairs(pe, B, unit)

            @block.scalar
            def _(act):
                def unit(n, u, j):
                    if not early(n, 2):
                        act.wait_ge(v_projected, (n - 1) * NQ)
                    for q in range(NQ):
                        a, b = keys_of(q)
                        act.wait_ge(turned, n * NQ + q + 1)
                        act.activation(cT[:, u, a:b], tp[0:DC, q % 2, 0:b - a], ACT.Copy).then_inc(cT_ready, 1)
                    act.wait_ge(k_biased, (n + 1) * NQ)
                    if not early(n, 2):
                        act.wait_ge(k_stored[u], j * 16)
                    act.activation(parts[:, u, 0, :], full[:, u, :], ACT.Copy).then_inc(hi_ready, 1)
                    act.wait_ge(rest_ready, n + 1)
                    act.activation(parts[:, u, 1, :], rest[:, u, :], ACT.Copy).then_inc(mid_ready, 1)
                    act.wait_ge(rest2_ready, n + 1)
                    act.activation(parts[:, u, 2, :], full[:, u, :], ACT.Copy).then_inc(lo_ready, 1)
                over_pairs(act, B, unit)

            @block.vector
            def _(dve):
                dve.wait_ge(loaded, 64)

                def unit(n, u, j):
                    if not early(n, 2):
                        dve.wait_ge(lo_ready, n - 1)
                        dve.wait_ge(v_stored[u], j * 16 * KT)
                    for q, (t0, count) in enumerate(QUADS):
                        a, b = keys_of(q)
                        dve.wait_ge(k_projected, n * NQ + q + 1)
                        dve.tensor_scalar(full[:, u, a:b], kp[:, q % 2, 0:b - a], bk_sb[:, 0:1], None,
                                          ALU.add).then_inc(k_biased, 1)
                        dve.wait_ge(v_projected, n * NQ + q + 1)
                        rows = TAIL if t0 == KT - 1 else P
                        dve.tensor_tensor(vt[0:rows, u, t0:t0 + count, :],
                                          vp[0:rows, q % 2, 0:count * P].rearrange("p (s t) -> p s t", s=count),
                                          bv_sb[0:rows, :].unsqueeze(1).to_broadcast([rows, count, P]),
                                          ALU.add).then_inc(v_biased, 1)
                over_pairs(dve, B, unit)


def attention_stage(nc, name, q_parts, k_parts, v_units, y_units, ident, keys, causal=False, clip=False):
    PAIRS = [(0, 0), (1, 0), (0, 1), (1, 1), (2, 0), (0, 2)]
    MROW = HD * len(PAIRS)
    KR = MROW + 3
    QW = min(512, keys)
    KT = -(-keys // P)
    PIECES = -(-keys // QW)
    PER = 4 if KT > 2 else KT
    CH = -(-KT // PER)
    NC = HG * CH
    NA = HG * 2 * PIECES
    NV = 32
    EACH = -(-NA // max(1, NC - 3))

    with Stage(nc, name) as st:
        K = st.sb("K", [KR, 2, HG, keys], BF16)
        Q = st.sb("Q", [KR, 2, HG, L], BF16)
        V = st.sb("V", [P, 2, KT, NV])
        VG = st.sb("VG", [P, 2, KT, HG, NV])
        prob = st.sb("prob", [P, 4, PER, L])
        pmax = st.sb("pmax", [P, 2, HG * 2, PIECES])
        negm = st.sb("negm", [P, 2, HG * 2])
        mfull = st.sb("mfull", [HG * 2, 2, P])
        mrest = st.sb("mrest", [HG * 2, 2, P])
        mrest2 = st.sb("mrest2", [HG * 2, 2, P])
        mparts = st.sb("mparts", [HG * 2, 2, 3, P], BF16)
        osb = st.sb("osb", [P, 2, L])
        rsum = st.sb("rsum", [P, 2, 2, HG])
        yout = st.sb("yout", [P, 2, 2, HG, HD])
        if causal:
            maskA = st.sb("maskA", [P, 2, L])
            maskB = st.sb("maskB", [P, 2, L])
            masked = st.sb("masked", [P, 2, L])
        if causal or clip:
            shifted = st.sb("shifted", [P, 2, PER, L])
        if clip:
            pick = st.sb("pick", [KR, P], BF16)
            low = st.sb("low", [P, 2, HG, L])
        sa = st.ps("sa", [P, 2, 512])
        sb_ = st.ps("sb", [P, 2, PER, L])
        pv = st.ps("pv", [P, 2, L])
        misc = st.ps("misc", [P, 512])

        K_loaded = [st.sem("K_loaded0"), st.sem("K_loaded1")]
        m_loaded = [st.sem("m_loaded0"), st.sem("m_loaded1")]
        V_loaded = [st.sem("V_loaded0"), st.sem("V_loaded1")]
        zeroed = st.sem("zeroed")
        ones_set = st.sem("ones_set")
        masks_ready = st.sem("masks_ready")
        VG_ready = st.sem("VG_ready")
        a_scored = st.sem("a_scored")
        a_masked = st.sem("a_masked")
        a_reduced = st.sem("a_reduced")
        negm_ready = st.sem("negm_ready")
        m_turned = st.sem("m_turned")
        m_copied = st.sem("m_copied")
        m_step = st.sem("m_step")
        mparts_ready = st.sem("mparts_ready")
        b_scored = st.sem("b_scored")
        b_shifted = st.sem("b_shifted")
        b_exp = st.sem("b_exp")
        b_used = st.sem("b_used")
        low_spread = st.sem("low_spread")
        low_ready = st.sem("low_ready")
        o_copied = st.sem("o_copied")
        o_turned = st.sem("o_turned")
        r_ready = st.sem("r_ready")
        y_ready = st.sem("y_ready")
        y_stored = [st.sem("y_stored0"), st.sem("y_stored1")]

        def tiles_of(k):
            t0 = k * PER
            ts = list(range(t0, min(KT, t0 + PER)))
            return ts, [min(P, keys - t * P) for t in ts]

        with st.block() as block:
            @block.sync
            def _(sp):
                sp.wait_ge(zeroed, 3)

                def unit(n, u, j):
                    if not early(n, 2):
                        sp.wait_ge(b_used, (n - 1) * NC)
                        sp.wait_ge(VG_ready, n - 1)
                    kd = k_parts.rearrange("b (x g d) c t -> (b x) g d c t", g=HG, d=HD)
                    qd = q_parts.rearrange("b (x g d) c t -> (b x) g d c t", g=HG, d=HD)
                    for r, (ck, cq) in enumerate(PAIRS):
                        sp.dma_start(K[r * HD:(r + 1) * HD, u, :, :],
                                     kd[bass.ds(n, 1), :, :, ck, :].rearrange("a g d t -> (a d) g t")
                                     ).then_inc(K_loaded[u], 16)
                        sp.dma_start(Q[r * HD:(r + 1) * HD, u, :, :],
                                     qd[bass.ds(n, 1), :, :, cq, :].rearrange("a g d t -> (a d) g t")
                                     ).then_inc(K_loaded[u], 16)
                    vd = v_units.rearrange("b x t c -> (b x) t c")
                    whole = keys // P
                    sp.dma_start(V[:, u, 0:whole, :],
                                 vd[bass.ds(n, 1), 0:whole * P, :].rearrange("a (k p) c -> p (a k) c", p=P)
                                 ).then_inc(V_loaded[u], 16)
                    if keys % P:
                        sp.dma_start(V[0:keys % P, u, whole, :],
                                     vd[bass.ds(n, 1), whole * P:keys, :].rearrange("a p c -> (a p) c")
                                     ).then_inc(V_loaded[u], 16)
                over_pairs(sp, UNITS, unit)

            @block.gpsimd
            def _(pool):
                pool.memset(K[:, :, :, :], 1.0).then_inc(zeroed, 1)
                pool.memset(Q[:, :, :, :], 0.0).then_inc(zeroed, 1)
                pool.memset(V[:, :, :, :], 0.0).then_inc(zeroed, 1)
                pool.memset(VG[:, :, :, :, :], 0.0).then_inc(ones_set, 1)
                pool.wait_ge(ones_set, 1)
                pool.memset(VG[:, :, :, :, HD:HD + 1], 1.0).then_inc(ones_set, 1)
                pool.wait_ge(ones_set, 2)
                if causal:
                    pool.memset(maskA[:, :, :], 0.0).then_inc(masks_ready, 1)
                    pool.memset(maskB[:, :, :], 0.0).then_inc(masks_ready, 1)
                    pool.wait_ge(masks_ready, 2)
                    for s in range(2):
                        pool.affine_select(out=maskA[:, s, :], in_=maskA[:, s, :], compare_op=ALU.is_ge, fill=NEG,
                                           base=s * P, pattern=[[-1, L]], channel_multiplier=1).then_inc(masks_ready, 1)
                        pool.affine_select(out=maskB[:, s, :], in_=maskB[:, s, :], compare_op=ALU.is_ge, fill=NEG,
                                           base=-s * P, pattern=[[1, L]], channel_multiplier=-1).then_inc(masks_ready, 1)
                if clip:
                    pool.memset(pick[:, :], 1.0).then_inc(masks_ready, 1)
                    pool.wait_ge(masks_ready, 1)
                    pool.affine_select(out=pick[:, :], in_=pick[:, :], compare_op=ALU.is_ge, fill=0.0,
                                       base=-MROW, pattern=[[0, P]], channel_multiplier=1).then_inc(masks_ready, 1)

            def piece_of(i):
                hq, k = divmod(i, PIECES)
                return hq // 2, hq % 2, k * QW, min(keys, (k + 1) * QW), k

            def slots(c):
                return range(min(NA, c * EACH), min(NA, (c + 1) * EACH))

            M_SLOT = -(-NA // EACH)
            assert M_SLOT < NC

            @block.tensor
            def _(pe):
                def a_piece(n, u, i):
                    g, s, a, b, k = piece_of(i)
                    if i == 0:
                        pe.wait_ge(K_loaded[u], 16 * 2 * len(PAIRS))
                    if not (early(n, 1) and i < 2):
                        pe.wait_ge(a_reduced, n * NA + (i - 1))
                    pe.matmul(sa[:, i % 2, 0:b - a], Q[0:MROW, u, g, s * P:(s + 1) * P], K[0:MROW, u, g, a:b],
                              start=True, stop=True).then_inc(a_scored, 1)

                def m_turn(n, u):
                    pe.wait_ge(negm_ready, n + 1)
                    if not early(n, 1):
                        pe.wait_ge(m_copied, n)
                    pe.transpose(misc[0:HG * 2, 256:256 + P], negm[:, u, :], ident[:, :]).then_inc(m_turned, 1)

                def spread_low(n, u, i):
                    pe.matmul(sa[:, i, :], pick[:, :], Q[:, u, 2 * i:2 * i + 2, :].rearrange("r g t -> r (g t)"),
                              start=True, stop=True).then_inc(low_spread, 1)

                def b_scores(n, u, c):
                    g, k = divmod(c, CH)
                    ts, rows = tiles_of(k)
                    if not (early(n, 1) and c < 2):
                        pe.wait_ge(b_shifted if causal or clip else b_exp, n * NC + (c - 1))
                    for x, (t, r) in enumerate(zip(ts, rows)):
                        ins = pe.matmul(sb_[0:r, c % 2, x, :], K[:, u, g, t * P:t * P + r], Q[:, u, g, :],
                                        start=True, stop=True)
                    ins.then_inc(b_scored, 1)

                def b_values(n, u, c):
                    g, k = divmod(c, CH)
                    ts, rows = tiles_of(k)
                    if c == 0:
                        pe.wait_ge(VG_ready, n + 1)
                        if not early(n, 2):
                            pe.wait_ge(o_copied, n - 1)
                    pe.wait_ge(b_exp, n * NC + (c + 1))
                    for x, (t, r) in enumerate(zip(ts, rows)):
                        ins = pe.matmul(pv[g * NV:(g + 1) * NV, u, :], VG[0:r, u, t, g, :], prob[0:r, c % 4, x, :],
                                        start=(t == 0), stop=(t == KT - 1), tile_position=(0, g * NV),
                                        skip_group_check=True)
                    ins.then_inc(b_used, 1)

                def o_turn(n, u):
                    pe.wait_ge(o_copied, n + 1)
                    if not early(n, 1):
                        pe.wait_ge(y_ready, n)
                    for s in range(2):
                        ins = pe.transpose(misc[:, s * P:(s + 1) * P], osb[:, u, s * P:(s + 1) * P], ident[:, :])
                    ins.then_inc(o_turned, 1)

                pe.wait_ge(zeroed, 3)
                if causal or clip:
                    pe.wait_ge(masks_ready, 6 if causal else 2)
                for i in range(NA):
                    a_piece(0, 0, i)
                m_turn(0, 0)

                def unit(n, u, j):
                    last = isinstance(n, int) and n == UNITS - 1
                    pe.wait_ge(m_loaded[u], (j + 1) * 48)
                    if clip:
                        pe.wait_ge(a_reduced, (n + 1) * NA)
                        spread_low(n, u, 0)
                        spread_low(n, u, 1)
                        pe.wait_ge(low_ready, n + 1)
                    b_scores(n, u, 0)
                    b_scores(n, u, 1)
                    if not early(n, 1):
                        o_turn(n - 1, 1 - u)
                    for c in range(NC):
                        if not last:
                            for i in slots(c):
                                a_piece_next(n, u, j, i)
                            if c == M_SLOT:
                                m_turn(n + 1, 1 - u)
                        b_values(n, u, c)
                        if c + 2 < NC:
                            b_scores(n, u, c + 2)

                def a_piece_next(n, u, j, i):
                    g, s, a, b, k = piece_of(i)
                    if i == 0:
                        pe.wait_ge(K_loaded[1 - u], (j + 1 + u) * 16 * 2 * len(PAIRS))
                    pe.wait_ge(a_reduced, (n + 1) * NA + (i - 1))
                    pe.matmul(sa[:, i % 2, 0:b - a], Q[0:MROW, 1 - u, g, s * P:(s + 1) * P], K[0:MROW, 1 - u, g, a:b],
                              start=True, stop=True).then_inc(a_scored, 1)
                over_pairs(pe, UNITS, unit)
                o_turn(UNITS - 1, 1)

            @block.vector
            def _(dve):
                def a_reduce(n, u, i):
                    g, s, a, b, k = piece_of(i)
                    dve.wait_ge(a_scored, n * NA + (i + 1))
                    if causal:
                        dve.wait_ge(a_reduced, n * NA + i) if not (early(n, 1) and i == 0) else None
                        dve.tensor_tensor(masked[:, i % 2, 0:b - a], sa[:, i % 2, 0:b - a], maskA[:, s, a:b],
                                          ALU.add).then_inc(a_masked, 1)
                        dve.wait_ge(a_masked, n * NA + (i + 1))
                        src = masked[:, i % 2, 0:b - a]
                    else:
                        src = sa[:, i % 2, 0:b - a]
                    dve.tensor_reduce(pmax[:, u, 2 * g + s, k:k + 1], src, AX.X, ALU.max).then_inc(a_reduced, 1)

                def m_find(n, u):
                    dve.wait_ge(a_reduced, (n + 1) * NA)
                    if not early(n, 2):
                        dve.wait_ge(m_turned, n - 1)
                    dve.tensor_reduce(negm[:, u, :], pmax[:, u, :, :], AX.X, ALU.max, negate=True
                                      ).then_inc(negm_ready, 1)

                def m_split(n, u, stored):
                    dve.wait_ge(m_turned, n + 1)
                    if clip:
                        dve.tensor_scalar(mfull[:, u, :], misc[0:HG * 2, 256:256 + P], CLAMP, -CLAMP, ALU.min, ALU.max
                                          ).then_inc(m_copied, 1)
                    else:
                        dve.tensor_copy(mfull[:, u, :], misc[0:HG * 2, 256:256 + P]).then_inc(m_copied, 1)
                    dve.wait_ge(m_copied, n + 1)
                    if stored is not None:
                        dve.wait_ge(m_loaded[u], stored)
                    dve.tensor_copy(mparts[:, u, 0, :], mfull[:, u, :]).then_inc(m_step, 1)
                    dve.wait_ge(m_step, n * 4 + 1)
                    dve.tensor_tensor(mrest[:, u, :], mfull[:, u, :], mparts[:, u, 0, :], ALU.subtract).then_inc(m_step, 1)
                    dve.wait_ge(m_step, n * 4 + 2)
                    dve.tensor_copy(mparts[:, u, 1, :], mrest[:, u, :]).then_inc(m_step, 1)
                    dve.wait_ge(m_step, n * 4 + 3)
                    dve.tensor_tensor(mrest2[:, u, :], mrest[:, u, :], mparts[:, u, 1, :], ALU.subtract).then_inc(m_step, 1)
                    dve.wait_ge(m_step, n * 4 + 4)
                    dve.tensor_copy(mparts[:, u, 2, :], mrest2[:, u, :]).then_inc(mparts_ready, 1)

                def b_shift(n, u, c):
                    g, k = divmod(c, CH)
                    ts, rows = tiles_of(k)
                    r, m = rows[0], len(ts)
                    dve.wait_ge(b_scored, n * NC + (c + 1))
                    if not (early(n, 1) and c < 2):
                        dve.wait_ge(b_exp, n * NC + (c - 1))
                    if causal:
                        dve.tensor_tensor(shifted[0:r, c % 2, 0:m, :], sb_[0:r, c % 2, 0:m, :],
                                          maskB[0:r, ts[0]:ts[0] + m, :], ALU.add).then_inc(b_shifted, 1)
                    else:
                        dve.scalar_tensor_tensor(shifted[0:r, c % 2, 0:m, :], sb_[0:r, c % 2, 0:m, :], 0.0,
                                                 low[0:r, u, g, :].unsqueeze(1).to_broadcast([r, m, L]),
                                                 ALU.min, ALU.max).then_inc(b_shifted, 1)

                def o_copy(n, u):
                    dve.wait_ge(b_used, (n + 1) * NC)
                    if not early(n, 2):
                        dve.wait_ge(o_turned, n - 1)
                    dve.tensor_copy(osb[:, u, :], pv[:, u, :]).then_inc(o_copied, 1)

                def o_norm(n, u, stored):
                    dve.wait_ge(o_turned, n + 1)
                    o = misc[:, 0:2 * P].rearrange("p (s g c) -> p s g c", s=2, g=HG)
                    dve.reciprocal(rsum[:, u, :, :], o[:, :, :, HD]).then_inc(r_ready, 1)
                    dve.wait_ge(r_ready, n + 1)
                    if stored is not None:
                        dve.wait_ge(y_stored[u], stored)
                    dve.tensor_tensor(yout[:, u, :, :, :], o[:, :, :, 0:HD],
                                      rsum[:, u, :, :].unsqueeze(3).to_broadcast([P, 2, HG, HD]),
                                      ALU.mult).then_inc(y_ready, 1)

                if causal:
                    dve.wait_ge(masks_ready, 6)
                for i in range(NA):
                    a_reduce(0, 0, i)
                m_find(0, 0)
                m_split(0, 0, None)

                def unit(n, u, j):
                    last = isinstance(n, int) and n == UNITS - 1
                    first = early(n, 1)
                    if clip:
                        dve.wait_ge(low_spread, (n + 1) * 2)
                        for i in range(2):
                            ins = dve.tensor_scalar(low[:, u, 2 * i:2 * i + 2, :].rearrange("p g t -> p (g t)"),
                                                    sa[:, i, :], -CLAMP, None, ALU.add)
                        ins.then_inc(low_ready, 1)
                        dve.wait_ge(low_ready, n + 1)
                    for c in range(NC):
                        if causal or clip:
                            if c == 0:
                                b_shift(n, u, 0)
                                b_shift(n, u, 1)
                        if c == 0 and not first:
                            before = None if early(n, 3) else (j - 1 + u) * 32
                            o_norm(n - 1, 1 - u, before)
                        if not last:
                            for i in slots(c):
                                a_reduce(n + 1, 1 - u, i)
                            if c == M_SLOT - 1:
                                m_find(n + 1, 1 - u)
                            if c == M_SLOT:
                                m_split(n + 1, 1 - u, None if early(n, 1) else (j + u) * 48)
                        if (causal or clip) and c + 2 < NC:
                            b_shift(n, u, c + 2)
                    o_copy(n, u)
                over_pairs(dve, UNITS, unit)
                o_norm(UNITS - 1, 1, (UNITS // 2 - 1) * 32)

            @block.scalar
            def _(act):
                def put_maxima(n, u):
                    act.wait_ge(mparts_ready, n + 1)
                    for c in range(3):
                        act.dma_start(Q[MROW + c:MROW + c + 1, u, :, :].rearrange("r g (s t) -> r (g s) t", s=2),
                                      mparts[:, u, c, :]).then_inc(m_loaded[u], 16)

                def put_y(n, u):
                    act.wait_ge(y_ready, n + 1)
                    for s in range(2):
                        act.dma_start(y_units[bass.ds(n, 1), s * P:(s + 1) * P, :].rearrange("a p c -> (a p) c"),
                                      yout[:, u, s, :, :].rearrange("p g d -> p (g d)")).then_inc(y_stored[u], 16)

                put_maxima(0, 0)
                act.wait_ge(ones_set, 2)

                def unit(n, u, j):
                    last = isinstance(n, int) and n == UNITS - 1
                    act.wait_ge(V_loaded[u], (j + 1) * 16 * (2 if keys % P else 1))
                    if not early(n, 2):
                        act.wait_ge(b_used, (n - 1) * NC)
                    act.activation(VG[:, u, :, :, 0:HD],
                                   V[:, u, :, :].rearrange("p k (g d) -> p k g d", g=HG), ACT.Copy
                                   ).then_inc(VG_ready, 1)
                    for c in range(NC):
                        g, k = divmod(c, CH)
                        ts, rows = tiles_of(k)
                        r, m = rows[0], len(ts)
                        act.wait_ge(b_shifted if causal or clip else b_scored, n * NC + (c + 1))
                        if not (early(n, 1) and c < 4):
                            act.wait_ge(b_used, n * NC + (c - 3))
                        src = shifted if causal or clip else sb_
                        act.activation(prob[0:r, c % 4, 0:m, :], src[0:r, c % 2, 0:m, :], ACT.Exp).then_inc(b_exp, 1)
                        if c == min(2, NC - 2) and not early(n, 1):
                            put_y(n - 1, 1 - u)
                        if c == min(M_SLOT + 1, NC - 1) and not last:
                            put_maxima(n + 1, 1 - u)
                over_pairs(act, UNITS, unit)
                put_y(UNITS - 1, 1)
                act.wait_ge(y_stored[0], UNITS // 2 * 32)
                act.wait_ge(y_stored[1], UNITS // 2 * 32)


def out_stage(nc, name, X, ident, y_units, wo, bo):
    with Stage(nc, name) as st:
        w_sb = st.sb("w", [P, P])
        b_sb = st.sb("b", [P, P])
        y = st.sb("y", [P, 2, P])
        yT = st.sb("yT", [P, 2, P])
        new = st.sb("new", [P, 2, P])
        tp = st.ps("tp", [P, 2, 512])
        op = st.ps("op", [P, 2, 512])
        loaded = st.sem("loaded")
        y_loaded = [st.sem("y_loaded0"), st.sem("y_loaded1")]
        turned = st.sem("turned")
        yT_ready = st.sem("yT_ready")
        projected = st.sem("projected")
        biased = st.sem("biased")
        added = st.sem("added")

        with st.block() as block:
            @block.sync
            def _(sp):
                sp.dma_start(w_sb[:, :], wo).then_inc(loaded, 16)
                sp.dma_start(b_sb[:, :], bo.partition_broadcast(P)).then_inc(loaded, 16)

                def unit(n, u, j):
                    if not early(n, 2):
                        sp.wait_ge(turned, n - 1)
                    yb = y_units.rearrange("(b x) t c -> b x t c", x=H // HG)
                    sp.dma_start(y[:, u, :].rearrange("p (x c) -> p x c", x=H // HG),
                                 yb[bass.ds(j, 1), :, u * P:(u + 1) * P, :].rearrange("b x p c -> (b p) x c")
                                 ).then_inc(y_loaded[u], 16)
                over_pairs(sp, TILES, unit)

            @block.tensor
            def _(pe):
                pe.wait_ge(loaded, 32)

                def unit(n, u, j):
                    pe.wait_ge(y_loaded[u], (j + 1) * 16)
                    if not early(n, 2):
                        pe.wait_ge(yT_ready, n - 1)
                    pe.transpose(tp[:, u, 0:P], y[:, u, :], ident[:, :]).then_inc(turned, 1)
                    pe.wait_ge(yT_ready, n + 1)
                    if not early(n, 2):
                        pe.wait_ge(biased, n - 1)
                    pe.matmul(op[:, u, 0:P], yT[:, u, :], w_sb[:, :], start=True, stop=True).then_inc(projected, 1)
                over_pairs(pe, TILES, unit)

            @block.scalar
            def _(act):
                def unit(n, u, j):
                    act.wait_ge(turned, n + 1)
                    if not early(n, 2):
                        act.wait_ge(projected, n - 1)
                    act.activation(yT[:, u, :], tp[:, u, 0:P], ACT.Copy).then_inc(yT_ready, 1)
                over_pairs(act, TILES, unit)

            @block.vector
            def _(dve):
                dve.wait_ge(loaded, 32)

                def unit(n, u, j):
                    dve.wait_ge(projected, n + 1)
                    if not early(n, 2):
                        dve.wait_ge(added, n - 1)
                    dve.tensor_tensor(new[:, u, :], op[:, u, 0:P], b_sb[:, :], ALU.add).then_inc(biased, 1)
                    dve.wait_ge(biased, n + 1)
                    xs = X[:, bass.ds(n, 1), :].rearrange("p a d -> p (a d)")
                    dve.tensor_tensor(xs, xs, new[:, u, :], ALU.add).then_inc(added, 1)
                over_pairs(dve, TILES, unit)


def cross(nc, name, X, ident, t, key, q_parts, k_ctx, v_ctx, y_units, clip):
    with nc.sbuf_tensor(f"{name}_XT", [P, NT], F32) as XT:
        norm_stage(nc, name + "n", X, XT, ident)
        scale = None if clip else t[f"{key}_scale"]
        project_stage(nc, name + "q", XT, t[f"{key}_Wq"], t[f"{key}_bq"], HD ** -0.5, q_parts, factor_dram=scale)
    context_stage(nc, name + "k", t["ctx_768"], ident, t[f"{key}_Wk"], t[f"{key}_bk"], t[f"{key}_Wv"],
                  t[f"{key}_bv"], k_ctx, v_ctx)
    attention_stage(nc, name + "a", q_parts, k_ctx, v_ctx, y_units, ident, LC, clip=clip)
    out_stage(nc, name + "o", X, ident, y_units, t[f"{key}_Wo"], t[f"{key}_bo"])


def mix_stage(nc, name, X, XT, ident, t, y_units):
    with Stage(nc, name) as st:
        wq = st.sb("wq", [P, P])
        wk = st.sb("wk", [P, P])
        wv = st.sb("wv", [P, P])
        wve = st.sb("wve", [P, HD, P])
        bq = st.sb("bq", [P, 1])
        bk = st.sb("bk", [P, 1])
        bve = st.sb("bve", [P, HD])
        gamma = st.sb("gamma", [P, HD])
        lam = st.sb("lam", [P, HD])
        retain = st.sb("retain", [P, HD])
        static = st.sb("static", [P, HD])
        bias_g = st.sb("bias_g", [P, HD])
        select = st.sb("select", [P, HD, P])
        same = st.sb("same", [P, P])
        gw1 = st.sb("gw1", [P, D // 2])
        gb1 = st.sb("gb1", [D // 2, 1])
        gw2 = st.sb("gw2", [D // 2, H])
        gw2e = st.sb("gw2e", [D // 2, P])
        gb2 = st.sb("gb2", [P, 1])
        wo = st.sb("wo", [P, P])
        bo = st.sb("bo", [P, P])
        qT = st.sb("qT", [P, 2, L])
        kT = st.sb("kT", [P, 2, L])
        gT = st.sb("gT", [D // 2, 2, L])
        alpha = st.sb("alpha", [P, 2, L])
        beta = st.sb("beta", [P, 2, L])
        vG = st.sb("vG", [P, 2, L])
        hebb = st.sb("hebb", [P, 2, L])
        state = st.sb("state", [P, 2, L])
        read = st.sb("read", [P, 2, L])
        y = st.sb("y", [P, 2, 2, P])
        soft = st.sb("soft", [P, 2, L])
        stp = st.sb("stp", [P, 2, L])
        mixed = st.sb("mixed", [P, 2, L])
        new = st.sb("new", [P, 2, 2, P])
        qk = st.ps("qk", [P, 2, L])
        gp = st.ps("gp", [P, 2, L])
        vp = st.ps("vp", [P, 2, 512])
        yp = st.ps("yp", [P, 2, 512])
        tp = st.ps("tp", [P, 2, P])
        op = st.ps("op", [P, 2, P])

        loaded = st.sem("loaded")
        built = st.sem("built")
        lam_squashed = st.sem("lam_squashed")
        y_loaded = [st.sem("y_loaded0"), st.sem("y_loaded1")]
        qk_projected = st.sem("qk_projected")
        q_ready = st.sem("q_ready")
        k_ready = st.sem("k_ready")
        g_projected = st.sem("g_projected")
        g_ready = st.sem("g_ready")
        a_projected = st.sem("a_projected")
        a_ready = st.sem("a_ready")
        v_projected = st.sem("v_projected")
        v_ready = st.sem("v_ready")
        hebb_ready = st.sem("hebb_ready")
        state_ready = st.sem("state_ready")
        read_ready = st.sem("read_ready")
        summed = st.sem("summed")
        y_turned = st.sem("y_turned")
        mix_step = st.sem("mix_step")
        mixed_ready = st.sem("mixed_ready")
        out_projected = st.sem("out_projected")
        biased = st.sem("biased")
        added = st.sem("added")

        with st.block() as block:
            @block.sync
            def _(sp):
                w = t["L0_attn_Wqkv_w"]
                b = t["L0_attn_Wqkv_b"]
                for dst, src in [
                        (wq[:, :], w[:, 0:P]), (wk[:, :], w[:, P:2 * P]), (wv[:, :], w[:, 2 * P:3 * P]),
                        (bq[:, :], column(b, 0)), (bk[:, :], column(b, P)),
                        (gw1[:, :], t["L0_attn_gate_w1"]), (gb1[:, :], column(t["L0_attn_gate_b1"], 0, D // 2)),
                        (gw2[:, :], t["L0_attn_gate_w2"]),
                        (wo[:, :], t["L0_attn_out_w"]), (bo[:, :], t["L0_attn_out_b"].partition_broadcast(P))]:
                    sp.dma_start(dst, src).then_inc(loaded, 16)
                for h in range(H):
                    rows = slice(h * HD, (h + 1) * HD)
                    for dst, src in ((gamma, t["L0_attn_Gamma"]), (lam, t["L0_attn_Lambda_raw"]),
                                     (static, t["L0_attn_W_static"])):
                        with nc.allow_non_contiguous_dma(reason="8 x 8 matrices, transposed"):
                            sp.dma_start(dst[rows, :], src[h].rearrange("i j -> j i")).then_inc(loaded, 16)
                    sp.dma_start(bve[rows, :], b[2 * P + h * HD:2 * P + (h + 1) * HD].partition_broadcast(HD)
                                 ).then_inc(loaded, 16)
                    sp.dma_start(gb2[rows, :], t["L0_attn_gate_b2"][h:h + 1].partition_broadcast(HD)
                                 ).then_inc(loaded, 16)

                def unit(n, u, j):
                    if not early(n, 2):
                        sp.wait_ge(y_turned, n - 1)
                    yb = y_units.rearrange("(b x) t c -> b x t c", x=H // HG)
                    for s in range(2):
                        sp.dma_start(y[:, u, s, :].rearrange("p (x c) -> p x c", x=H // HG),
                                     yb[bass.ds(n, 1), :, s * P:(s + 1) * P, :].rearrange("b x p c -> (b p) x c")
                                     ).then_inc(y_loaded[u], 16)
                over_pairs(sp, B, unit)

            LOADS = 16 * (10 + 5 * H)

            @block.gpsimd
            def _(pool):
                pool.memset(same[:, :], 1.0).then_inc(built, 1)
                pool.memset(select[:, :, :], 0.0).then_inc(built, 1)
                pool.wait_ge(built, 2)
                sv = same[:, :].rearrange("p (h c) -> p h c", h=H)
                pool.affine_select(out=sv, in_=sv, compare_op=ALU.is_ge, fill=0.0, base=0,
                                   pattern=[[-HD, H], [0, HD]], channel_multiplier=1).then_inc(built, 1)
                pool.wait_ge(built, 3)
                pool.affine_select(out=sv, in_=sv, compare_op=ALU.is_ge, fill=0.0, base=HD - 1,
                                   pattern=[[HD, H], [0, HD]], channel_multiplier=-1).then_inc(built, 1)
                pool.wait_ge(built, 4)
                for i in range(HD):
                    pool.tensor_copy(select[:, i, i:P:HD], same[:, i:P:HD]).then_inc(built, 1)

                def unit(n, u, j):
                    for i in range(HD):
                        pool.wait_ge(v_ready, n * HD + (i + 1))
                        if i == 0:
                            pool.wait_ge(k_ready, n + 1)
                        if not (early(n, 1) and i < 2):
                            pool.wait_ge(state_ready, n * HD + (i - 1))
                        pool.tensor_tensor(hebb[:, i % 2, :], vG[:, i % 2, :], kT[:, u, :], ALU.mult
                                           ).then_inc(hebb_ready, 1)
                over_pairs(pool, B, unit)

            @block.tensor
            def _(pe):
                pe.wait_ge(loaded, LOADS)
                pe.wait_ge(built, 4 + HD)
                pe.wait_ge(mix_step, 5)

                def unit(n, u, j):
                    x = XT[:, bass.ds(n * L, L)]
                    if not early(n, 1):
                        pe.wait_ge(q_ready, n)
                        pe.wait_ge(k_ready, n)
                        pe.wait_ge(a_ready, n)
                    pe.matmul(qk[:, 0, :], wq[:, :], x, start=True, stop=True)
                    pe.matmul(qk[:, 1, :], wk[:, :], x, start=True, stop=True).then_inc(qk_projected, 1)
                    pe.matmul(gp[0:D // 2, 0, :], gw1[:, :], x, start=True, stop=True).then_inc(g_projected, 1)
                    for i in range(HD):
                        if not (early(n, 1) and i < 2):
                            pe.wait_ge(v_ready, n * HD + (i - 1))
                        pe.matmul(vp[:, i % 2, 0:L], wve[:, i, :], x, start=True, stop=True).then_inc(v_projected, 1)
                        if i == 1:
                            pe.wait_ge(g_ready, n + 1)
                            pe.matmul(gp[:, 1, :], gw2e[:, :], gT[:, u, :], start=True, stop=True
                                      ).then_inc(a_projected, 1)
                        if i >= 2:
                            plasticity_sum(n, u, i - 2)
                    plasticity_sum(n, u, HD - 2)
                    plasticity_sum(n, u, HD - 1)
                    pe.wait_ge(y_loaded[u], (j + 1) * 32)
                    if not early(n, 1):
                        pe.wait_ge(mixed_ready, n)
                    for s in range(2):
                        ins = pe.transpose(tp[:, s, :], y[:, u, s, :], ident[:, :])
                    ins.then_inc(y_turned, 1)
                    pe.wait_ge(mixed_ready, n + 1)
                    if not early(n, 1):
                        pe.wait_ge(biased, n)
                    for s in range(2):
                        ins = pe.matmul(op[:, s, :], mixed[:, u, s * P:(s + 1) * P], wo[:, :], start=True, stop=True)
                    ins.then_inc(out_projected, 1)

                def plasticity_sum(n, u, i):
                    pe.wait_ge(read_ready, n * HD + (i + 1))
                    if i == 0 and not early(n, 2):
                        pe.wait_ge(mixed_ready, n - 1)
                    pe.matmul(yp[:, u, 0:L], select[:, i, :], read[:, i % 2, :], start=(i == 0), stop=(i == HD - 1)
                              ).then_inc(summed, 1)
                over_pairs(pe, B, unit)

            @block.scalar
            def _(act):
                act.wait_ge(loaded, LOADS)
                act.activation(retain[:, :], lam[:, :], ACT.Sigmoid).then_inc(lam_squashed, 1)
                act.wait_ge(mix_step, 5)

                def unit(n, u, j):
                    act.wait_ge(qk_projected, n + 1)
                    if not early(n, 2):
                        act.wait_ge(read_ready, (n - 1) * HD)
                        act.wait_ge(hebb_ready, (n - 1) * HD)
                    act.activation(qT[:, u, :], qk[:, 0, :], ACT.Identity, bias=bq[:, 0:1]).then_inc(q_ready, 1)
                    act.activation(kT[:, u, :], qk[:, 1, :], ACT.Identity, bias=bk[:, 0:1], scale=HD ** -0.5
                                   ).then_inc(k_ready, 1)
                    act.wait_ge(g_projected, n + 1)
                    if not early(n, 2):
                        act.wait_ge(a_projected, n - 1)
                    act.activation(gT[:, u, :], gp[0:D // 2, 0, :], ACT.Gelu, bias=gb1[:, 0:1]).then_inc(g_ready, 1)
                    for i in range(HD):
                        act.wait_ge(v_projected, n * HD + (i + 1))
                        if not (early(n, 1) and i < 2):
                            act.wait_ge(hebb_ready, n * HD + (i - 1))
                        act.activation(vG[:, i % 2, :], vp[:, i % 2, 0:L], ACT.Identity, bias=bias_g[:, i:i + 1],
                                       scale=gamma[:, i:i + 1]).then_inc(v_ready, 1)
                    act.wait_ge(a_projected, n + 1)
                    if not early(n, 2):
                        act.wait_ge(mixed_ready, n - 1)
                    act.activation(alpha[:, u, :], gp[:, 1, :], ACT.Sigmoid, bias=gb2[:, 0:1]).then_inc(a_ready, 1)
                over_pairs(act, B, unit)

            @block.vector
            def _(dve):
                dve.wait_ge(loaded, LOADS)
                dve.tensor_copy(wve[:, :, :].rearrange("p i (h j) -> p i h j", h=H),
                                wv[:, :].rearrange("p (h i) -> p i h", h=H).unsqueeze(3)
                                .to_broadcast([P, HD, H, HD])).then_inc(mix_step, 1)
                dve.tensor_copy(gw2e[:, :].rearrange("p (h j) -> p h j", h=H),
                                gw2[:, :].unsqueeze(2).to_broadcast([D // 2, H, HD])).then_inc(mix_step, 1)
                dve.tensor_tensor(bias_g[:, :], bve[:, :], gamma[:, :], ALU.mult).then_inc(mix_step, 1)
                dve.wait_ge(lam_squashed, 1)
                dve.tensor_scalar(retain[:, :], retain[:, :], -1.0, 1.0, ALU.mult, ALU.add).then_inc(mix_step, 1)
                dve.tensor_scalar(bk[:, :], bk[:, :], HD ** -0.5, None, ALU.mult).then_inc(mix_step, 1)
                dve.wait_ge(mix_step, 5)

                def unit(n, u, j):
                    for i in range(HD):
                        dve.wait_ge(hebb_ready, n * HD + (i + 1))
                        if not (early(n, 1) and i < 2):
                            dve.wait_ge(read_ready, n * HD + (i - 1))
                        dve.tensor_tensor_scan(state[:, i % 2, :], retain[:, i:i + 1].to_broadcast([P, L]),
                                               hebb[:, i % 2, :], 0.0, ALU.mult, ALU.add).then_inc(state_ready, 1)
                        dve.wait_ge(state_ready, n * HD + (i + 1))
                        if i == 0:
                            dve.wait_ge(q_ready, n + 1)
                        if not (early(n, 1) and i < 2):
                            dve.wait_ge(summed, n * HD + (i - 1))
                        dve.scalar_tensor_tensor(read[:, i % 2, :], state[:, i % 2, :], static[:, i:i + 1],
                                                 qT[:, u, :], ALU.add, ALU.mult).then_inc(read_ready, 1)
                    dve.wait_ge(a_ready, n + 1)
                    dve.tensor_scalar(beta[:, u, :], alpha[:, u, :], -1.0, 1.0, ALU.mult, ALU.add
                                      ).then_inc(mix_step, 1)
                    dve.wait_ge(y_turned, n + 1)
                    dve.tensor_tensor(soft[:, u, :], tp[:, :, :].rearrange("p s t -> p (s t)"), alpha[:, u, :],
                                      ALU.mult).then_inc(mix_step, 1)
                    dve.wait_ge(mix_step, n * 3 + 7)
                    dve.wait_ge(summed, (n + 1) * HD)
                    dve.tensor_tensor(stp[:, u, :], yp[:, u, 0:L], beta[:, u, :], ALU.mult).then_inc(mix_step, 1)
                    dve.wait_ge(mix_step, n * 3 + 8)
                    if not early(n, 2):
                        dve.wait_ge(out_projected, n - 1)
                    dve.tensor_tensor(mixed[:, u, :], soft[:, u, :], stp[:, u, :], ALU.add).then_inc(mixed_ready, 1)
                    dve.wait_ge(out_projected, n + 1)
                    if not early(n, 2):
                        dve.wait_ge(added, n - 1)
                    dve.tensor_tensor(new[:, u, :, :], op[:, :, :], bo[:, :].unsqueeze(1).to_broadcast([P, 2, P]),
                                      ALU.add).then_inc(biased, 1)
                    dve.wait_ge(biased, n + 1)
                    xs = X[:, bass.ds(n * 2, 2), :]
                    dve.tensor_tensor(xs, xs, new[:, u, :, :], ALU.add).then_inc(added, 1)
                over_pairs(dve, B, unit)


def router_scores(pe, XT, gw, logits, E):
    for n in range(TILES):
        ins = pe.matmul(logits[:, n, :], XT[:, n * P:(n + 1) * P], gw[:, :], start=True, stop=True)
    return ins


def router_stage(nc, name, XT, ident, gate_w, E, GS, gate_bias=None):
    GROUPS, TOP, SCALING = 4, 8, 2.5
    EG = E // GROUPS
    CAPACITY = -(-NT * 2 * 5 // (4 * E))
    BIG = 1.0e30
    T = [P, TILES, E]
    grouped = gate_bias is not None
    with Stage(nc, name) as st:
        gnat = st.sb("gnat", [E, P])
        gw = st.sb("gw", [P, E])
        score = st.sb("score", T)
        choice = st.sb("choice", T)
        eq = st.sb("eq", T)
        other = st.sb("other", T)
        chosen = st.sb("chosen", T)
        weight = st.sb("weight", T)
        tsum = st.sb("tsum", [P, TILES])
        tsum2 = st.sb("tsum2", [P, TILES])
        GT = st.sb("GT", [E, NT])
        grest = st.sb("grest", [E, NT])
        gmid = st.sb("gmid", [E, NT])
        if grouped:
            bias = st.sb("bias", [P, E])
            best = st.sb("best", [P, TILES, GROUPS])
            second = st.sb("second", [P, TILES, GROUPS])
            count = st.sb("count", [P, TILES, GROUPS])
            gsum = st.sb("gsum", [P, TILES, GROUPS])
            more = st.sb("more", [P, TILES, GROUPS, GROUPS])
            tie = st.sb("tie", [P, TILES, GROUPS, GROUPS])
            before = st.sb("before", [P, GROUPS, GROUPS])
            rank = st.sb("rank", [P, TILES, GROUPS])
            top8 = st.sb("top8", [P, TILES, 8])
            running = st.sb("running", T)
            resume = st.sb("resume", T)
            need = st.sb("need", [P, TILES])
        else:
            more = st.sb("more", [P, TILES, E, E])
            tie = st.sb("tie", [P, TILES, E, E])
            before = st.sb("before", [P, E, E])
            rank = st.sb("rank", T)
            member = st.sb("member", [E, NT])
            running = st.sb("running", [E, NT])
            keep = st.sb("keep", [E, NT])
        logits = st.ps("logits", T)
        tp = st.ps("tp", [P, 4, 512])

        loaded = st.sem("loaded")
        built = st.sem("built")
        turned = st.sem("turned")
        gw_ready = st.sem("gw_ready")
        scored = st.sem("scored")
        squashed = st.sem("squashed")
        step = st.sem("step")
        w_ready = st.sem("w_ready")
        w_turned = st.sem("w_turned")
        w_copied = st.sem("w_copied")
        m_turned = st.sem("m_turned")
        m_copied = st.sem("m_copied")

        with st.block() as block:
            @block.sync
            def _(sp):
                sp.dma_start(gnat[:, :], gate_w).then_inc(loaded, 16)
                if grouped:
                    sp.dma_start(bias[:, :], gate_bias.partition_broadcast(P)).then_inc(loaded, 16)

            @block.gpsimd
            def _(pool):
                N = GROUPS if grouped else E
                pool.memset(before[:, :, :], 1.0).then_inc(built, 1)
                pool.wait_ge(built, 1)
                pool.affine_select(out=before[:, :, :], in_=before[:, :, :], compare_op=ALU.is_gt, fill=0.0,
                                   base=0, pattern=[[1, N], [-1, N]], channel_multiplier=0).then_inc(built, 1)
                pool.memset(GS[:, :], 0.0).then_inc(built, 1)
                if grouped:
                    pool.memset(resume[:, :, :], 1.0).then_inc(built, 1)
                    pool.wait_ge(built, 4)
                    pool.memset(resume[:, :, 0:1], 0.0).then_inc(built, 1)
                else:
                    pool.memset(grest[:, :], 1.0).then_inc(built, 1)

            @block.tensor
            def _(pe):
                pe.wait_ge(loaded, 32 if grouped else 16)
                pe.transpose(tp[:, 0, 0:E], gnat[:, :], ident[0:E, 0:E]).then_inc(turned, 1)
                pe.wait_ge(gw_ready, 1)
                router_scores(pe, XT, gw, logits, E).then_inc(scored, 1)
                pe.wait_ge(w_ready, 1)
                for n in range(TILES):
                    q = n // 4
                    if n % 4 == 0 and q >= 4:
                        pe.wait_ge(w_copied, q - 3)
                    ins = pe.transpose(tp[0:E, q % 4, (n % 4) * P:(n % 4 + 1) * P], weight[:, n, :], ident[:, :])
                    if n % 4 == 3:
                        ins.then_inc(w_turned, 1)
                if not grouped:
                    for n in range(TILES):
                        q = n // 4
                        if n % 4 == 0:
                            pe.wait_ge(w_copied, min(8, q + 5))
                            if q >= 4:
                                pe.wait_ge(m_copied, q - 3)
                        ins = pe.transpose(tp[0:E, q % 4, (n % 4) * P:(n % 4 + 1) * P], chosen[:, n, :], ident[:, :])
                        if n % 4 == 3:
                            ins.then_inc(m_turned, 1)

            @block.scalar
            def _(act):
                act.wait_ge(turned, 1)
                act.activation(gw[:, :], tp[:, 0, 0:E], ACT.Copy).then_inc(gw_ready, 1)
                if grouped:
                    act.wait_ge(scored, 1)
                    act.activation(score[:, :, :], logits[:, :, :], ACT.Sigmoid).then_inc(squashed, 1)
                else:
                    act.wait_ge(step, 2)
                    act.activation(other[:, :, :], choice[:, :, :], ACT.Exp).then_inc(squashed, 1)
                for q in range(TILES // 4):
                    act.wait_ge(w_turned, q + 1)
                    act.activation(GT[:, q * 512:(q + 1) * 512], tp[0:E, q % 4, :], ACT.Copy).then_inc(w_copied, 1)
                if not grouped:
                    for q in range(TILES // 4):
                        act.wait_ge(m_turned, q + 1)
                        act.activation(member[:, q * 512:(q + 1) * 512], tp[0:E, q % 4, :], ACT.Copy
                                       ).then_inc(m_copied, 1)

            @block.vector
            def _(dve):
                link = Chain(dve, step)

                def spread(ap, n):
                    return ap.unsqueeze(len(ap.shape)).to_broadcast(list(ap.shape) + [n])

                dve.wait_ge(built, 5 if grouped else 4)
                dve.wait_ge(loaded, 32 if grouped else 16)
                if grouped:
                    dve.wait_ge(squashed, 1)
                    link(dve.tensor_tensor(choice[:, :, :], score[:, :, :],
                                           bias[:, :].unsqueeze(1).to_broadcast(T), ALU.add))
                    cg = choice[:, :, :].rearrange("p t (g e) -> p (t g) e", g=GROUPS)
                    eg = eq[:, :, :].rearrange("p t (g e) -> p (t g) e", g=GROUPS)
                    og = other[:, :, :].rearrange("p t (g e) -> p (t g) e", g=GROUPS)
                    flat = lambda a: a[:, :, :].rearrange("p t g -> p (t g)")
                    link(dve.tensor_reduce(flat(best), cg, AX.X, ALU.max))
                    link(dve.tensor_tensor(eg, cg, spread(flat(best), EG), ALU.is_equal))
                    link(dve.tensor_reduce(flat(count), eg, AX.X, ALU.add))
                    link(dve.scalar_tensor_tensor(og, eg, -BIG, cg, ALU.mult, ALU.add))
                    link(dve.tensor_reduce(flat(second), og, AX.X, ALU.max))
                    link(dve.tensor_scalar(flat(count), flat(count), 1.5, None, ALU.is_gt))
                    link(dve.tensor_tensor(flat(gsum), flat(best), flat(count), ALU.mult))
                    link(dve.tensor_scalar(flat(count), flat(count), BIG, -BIG, ALU.mult, ALU.add))
                    link(dve.tensor_tensor(flat(gsum), flat(gsum), flat(count), ALU.add))
                    link(dve.tensor_tensor(flat(second), flat(second), flat(gsum), ALU.max))
                    link(dve.tensor_tensor(flat(gsum), flat(best), flat(second), ALU.add))
                    rank_of(dve, link, gsum, rank, more, tie, before, GROUPS)
                    link(dve.tensor_scalar(flat(rank), flat(rank), 1.5, None, ALU.is_lt))
                    link(dve.tensor_tensor(cg, cg, spread(flat(rank), EG), ALU.mult))
                    for n in range(TILES):
                        ins = dve.max(top8[:, n, :], choice[:, n, :])
                    link(ins)
                    eighth = top8[:, :, TOP - 1]
                    link(dve.tensor_tensor(eq[:, :, :], choice[:, :, :], spread(eighth, E), ALU.is_equal))
                    link(dve.tensor_tensor(chosen[:, :, :], choice[:, :, :], spread(eighth, E), ALU.is_gt))
                    link(dve.tensor_reduce(tsum[:, :], chosen[:, :, :], AX.X, ALU.add))
                    link(dve.tensor_scalar(need[:, :], tsum[:, :], -1.0, TOP + 0.5, ALU.mult, ALU.add))
                    link(dve.tensor_tensor_scan(running[:, :, :].rearrange("p t e -> p (t e)"),
                                                resume[:, :, :].rearrange("p t e -> p (t e)"),
                                                eq[:, :, :].rearrange("p t e -> p (t e)"), 0.0, ALU.mult, ALU.add))
                    link(dve.tensor_tensor(running[:, :, :], running[:, :, :], spread(need[:, :], E), ALU.is_lt))
                    link(dve.tensor_tensor(eq[:, :, :], eq[:, :, :], running[:, :, :], ALU.mult))
                    link(dve.tensor_tensor(chosen[:, :, :], chosen[:, :, :], eq[:, :, :], ALU.add))
                else:
                    dve.wait_ge(scored, 1)
                    link(dve.tensor_reduce(tsum[:, :], logits[:, :, :], AX.X, ALU.max))
                    link(dve.tensor_tensor(choice[:, :, :], logits[:, :, :], spread(tsum[:, :], E), ALU.subtract))
                    dve.wait_ge(squashed, 1)
                    link(dve.tensor_reduce(tsum[:, :], other[:, :, :], AX.X, ALU.add))
                    link(dve.reciprocal(tsum2[:, :], tsum[:, :]))
                    link(dve.tensor_tensor(score[:, :, :], other[:, :, :], spread(tsum2[:, :], E), ALU.mult))
                    rank_of(dve, link, score, rank, more, tie, before, E)
                    link(dve.tensor_scalar(chosen[:, :, :], rank[:, :, :], 1.5, None, ALU.is_lt))
                link(dve.tensor_tensor(weight[:, :, :], score[:, :, :], chosen[:, :, :], ALU.mult))
                link(dve.tensor_reduce(tsum[:, :], weight[:, :, :], AX.X, ALU.add))
                link(dve.tensor_scalar(tsum[:, :], tsum[:, :], 1e-20, None, ALU.add))
                link(dve.reciprocal(tsum2[:, :], tsum[:, :]))
                if grouped:
                    link(dve.tensor_scalar(tsum2[:, :], tsum2[:, :], SCALING, None, ALU.mult))
                dve.tensor_tensor(weight[:, :, :], weight[:, :, :], spread(tsum2[:, :], E), ALU.mult
                                  ).then_inc(w_ready, 1)
                dve.wait_ge(w_ready, 1)
                dve.wait_ge(w_copied, TILES // 4)
                if not grouped:
                    dve.wait_ge(m_copied, TILES // 4)
                    link(dve.tensor_tensor_scan(running[:, :], grest[:, :], member[:, :], 0.0, ALU.mult, ALU.add))
                    link(dve.tensor_scalar(keep[:, :], running[:, :], CAPACITY + 0.5, None, ALU.is_lt))
                    link(dve.tensor_tensor(GT[:, :], GT[:, :], keep[:, :], ALU.mult))
                link(dve.tensor_copy(GS[0:E, :], GT[:, :]))
                link(dve.tensor_tensor(grest[:, :], GT[:, :], GS[0:E, :], ALU.subtract))
                link(dve.tensor_copy(GS[32:32 + E, :], grest[:, :]))
                link(dve.tensor_copy(gmid[:, :], GS[32:32 + E, :]))
                link(dve.tensor_tensor(gmid[:, :], grest[:, :], gmid[:, :], ALU.subtract))
                link(dve.tensor_copy(GS[64:64 + E, :], gmid[:, :]))


def rank_of(dve, link, value, rank, more, tie, before, N):
    mine = value[:, :, :].unsqueeze(3).to_broadcast([P, TILES, N, N])
    theirs = value[:, :, :].unsqueeze(2).to_broadcast([P, TILES, N, N])
    link(dve.tensor_tensor(more[:, :, :, :], theirs, mine, ALU.is_gt))
    link(dve.tensor_tensor(tie[:, :, :, :], theirs, mine, ALU.is_equal))
    link(dve.tensor_tensor(tie[:, :, :, :], tie[:, :, :, :],
                           before[:, :, :].unsqueeze(1).to_broadcast([P, TILES, N, N]), ALU.mult))
    link(dve.tensor_tensor(more[:, :, :, :], more[:, :, :, :], tie[:, :, :, :], ALU.add))
    link(dve.tensor_reduce(rank[:, :, :], more[:, :, :, :], AX.X, ALU.add))


def experts_stage(nc, name, X, XT, ident, GS, gates, ups, downs, routed, per, direct=False):
    S = len(gates)
    C = 512
    CHUNKS = NT // C
    with Stage(nc, name) as st:
        wT = st.sb("wT", [P, 3, S, P])
        nat = wT if direct else st.sb("nat", [P, 3, S, P])
        if routed:
            pick = st.sb("pick", [96, routed, P], BF16)
        sg = st.sb("sg", [P, 2, C])
        hu = st.sb("hu", [P, 2, C])
        hid = st.sb("hid", [P, 2, C])
        oT = st.sb("oT", [P, C])
        gp = st.ps("gp", [P, 2, C])
        up = st.ps("up", [P, 2, C])
        wp = st.ps("wp", [P, 2, C])
        op = st.ps("op", [P, C])
        tp = st.ps("tp", [P, C])
        loaded = st.sem("loaded")
        built = st.sem("built")
        w_turned = st.sem("w_turned")
        w_copied = st.sem("w_copied")
        g_ready = st.sem("g_ready")
        u_ready = st.sem("u_ready")
        r_ready = st.sem("r_ready")
        sg_ready = st.sem("sg_ready")
        hu_ready = st.sem("hu_ready")
        hid_ready = st.sem("hid_ready")
        downed = st.sem("downed")
        oT_ready = st.sem("oT_ready")
        o_turned = st.sem("o_turned")
        added = st.sem("added")
        NW = 3 * S

        with st.block() as block:
            @block.sync
            def _(sp):
                for m, mats in enumerate((gates, ups, downs)):
                    for s in range(S):
                        src = mats[s]
                        dst = nat[:, m, s, :]
                        if len(src.shape) == 3:
                            dst = dst.rearrange("h (e i) -> h e i", e=src.shape[1])
                        sp.dma_start(dst, src).then_inc(loaded, 16)

            @block.gpsimd
            def _(pool):
                if routed:
                    pool.memset(pick[:, :, :], 0.0).then_inc(built, 1)
                for b in range(3 if routed else 0):
                    pool.wait_ge(built, b + 1)
                    pv = pick[:, :, :].rearrange("p s (a i) -> p s a i", a=per)
                    pool.affine_select(out=pv, in_=pv, compare_op=ALU.not_equal, fill=1.0, base=-32 * b,
                                       pattern=[[-per, routed], [-1, per], [0, P // per]],
                                       channel_multiplier=1).then_inc(built, 1)

            @block.tensor
            def _(pe):
                pe.wait_ge(loaded, 16 * NW)
                for i in range(0 if direct else NW):
                    q = i // 4
                    if i % 4 == 0 and q >= 2:
                        pe.wait_ge(w_copied, q - 1)
                    m, s = divmod(i, S)
                    ins = pe.transpose(gp[:, q % 2, (i % 4) * P:(i % 4 + 1) * P], nat[:, m, s, :], ident[:, :])
                    if i % 4 == 3 or i == NW - 1:
                        ins.then_inc(w_turned, 1)
                if not direct:
                    pe.wait_ge(w_copied, -(-NW // 4))
                if routed:
                    pe.wait_ge(built, 4)

                def down(n, s):
                    pe.wait_ge(hid_ready, n * S + (s + 1))
                    ins = pe.matmul(op[:, :], wT[:, 2, s, :], hid[:, s % 2, :], start=(s == 0), stop=(s == S - 1))
                    ins.then_inc(downed, 1)

                def turn_out(n):
                    pe.wait_ge(oT_ready, n + 1)
                    if not early(n, 1):
                        pe.wait_ge(added, n)
                    for k in range(4):
                        ins = pe.transpose(tp[:, k * P:(k + 1) * P], oT[:, k * P:(k + 1) * P], ident[:, :])
                    ins.then_inc(o_turned, 1)

                def chunk(n):
                    x = XT[:, bass.ds(n * C, C)]
                    for s in range(S):
                        if not (early(n, 1) and s < 2):
                            pe.wait_ge(sg_ready, n * S + s - 1)
                            pe.wait_ge(hu_ready, n * S + s - 1)
                            pe.wait_ge(hid_ready, n * S + s - 1)
                        pe.matmul(gp[:, s % 2, :], wT[:, 0, s, :], x, start=True, stop=True).then_inc(g_ready, 1)
                        pe.matmul(up[:, s % 2, :], wT[:, 1, s, :], x, start=True, stop=True).then_inc(u_ready, 1)
                        if s < routed:
                            pe.matmul(wp[:, s % 2, :], pick[:, s, :], GS[:, bass.ds(n * C, C)], start=True, stop=True
                                      ).then_inc(r_ready, 1)
                        if s == 2 and not early(n, 1):
                            turn_out(n - 1)
                        if s == 1 and not early(n, 1):
                            pe.wait_ge(oT_ready, n)
                        if s >= 1:
                            down(n, s - 1)
                    down(n, S - 1)
                over(pe, CHUNKS, chunk)
                turn_out(CHUNKS - 1)

            @block.scalar
            def _(act):
                for q in range(0 if direct else -(-NW // 4)):
                    m = min(4, NW - 4 * q)
                    act.wait_ge(w_turned, q + 1)
                    act.activation(wT[:, :, :, :].rearrange("p m s f -> p (m s f)")[:, q * 512:q * 512 + m * P],
                                   gp[:, q % 2, 0:m * P], ACT.Copy).then_inc(w_copied, 1)

                def chunk(n):
                    for s in range(S):
                        act.wait_ge(g_ready, n * S + (s + 1))
                        if not (early(n, 1) and s < 2):
                            act.wait_ge(hu_ready, n * S + s - 1)
                        act.activation(sg[:, s % 2, :], gp[:, s % 2, :], ACT.Silu).then_inc(sg_ready, 1)
                    act.wait_ge(downed, (n + 1) * S)
                    if not early(n, 1):
                        act.wait_ge(o_turned, n)
                    act.activation(oT[:, :], op[:, :], ACT.Copy).then_inc(oT_ready, 1)
                over(act, CHUNKS, chunk)

            @block.vector
            def _(dve):
                def add_out(n):
                    dve.wait_ge(o_turned, n + 1)
                    xs = X[:, bass.ds(n * 4, 4), :]
                    dve.tensor_tensor(xs, xs, tp[:, :].rearrange("p (k d) -> p k d", k=4), ALU.add).then_inc(added, 1)

                def chunk(n):
                    for s in range(S):
                        dve.wait_ge(sg_ready, n * S + (s + 1))
                        dve.wait_ge(u_ready, n * S + (s + 1))
                        if not (early(n, 1) and s < 2):
                            dve.wait_ge(hid_ready, n * S + s - 1)
                        dve.tensor_tensor(hu[:, s % 2, :], sg[:, s % 2, :], up[:, s % 2, :], ALU.mult
                                          ).then_inc(hu_ready, 1)
                        dve.wait_ge(hu_ready, n * S + (s + 1))
                        if not (early(n, 1) and s < 2):
                            dve.wait_ge(downed, n * S + s - 1)
                        if s < routed:
                            dve.wait_ge(r_ready, n * routed + (s + 1))
                            ins = dve.tensor_tensor(hid[:, s % 2, :], hu[:, s % 2, :], wp[:, s % 2, :], ALU.mult)
                        else:
                            ins = dve.tensor_copy(hid[:, s % 2, :], hu[:, s % 2, :])
                        ins.then_inc(hid_ready, 1)
                        if s == 3 and not early(n, 1):
                            add_out(n - 1)
                over(dve, CHUNKS, chunk)
                add_out(CHUNKS - 1)


def moe0(nc, X, ident, t):
    E, I = 32, 64
    with ExitStack() as ctx:
        XT = ctx.enter_context(nc.sbuf_tensor("f0_XT", [P, NT], F32))
        GS = ctx.enter_context(nc.sbuf_tensor("f0_GS", [96, NT], BF16))
        norm_stage(nc, "f0n", X, XT, ident)
        router_stage(nc, "f0r", XT, ident, t["L0_ffn_gate_w"], E, GS, gate_bias=t["L0_ffn_gate_bias"])
        pairs = [(2 * k, 2 * k + 2) for k in range(E // 2)]
        gates = [t["L0_ffn_expert_gate"][a:b].rearrange("e i h -> (e i) h") for a, b in pairs]
        ups = [t["L0_ffn_expert_up"][a:b].rearrange("e i h -> (e i) h") for a, b in pairs]
        downs = [t["L0_ffn_expert_down"][a:b].rearrange("e h i -> h e i") for a, b in pairs]
        experts_stage(nc, "f0e", X, XT, ident, GS, gates + [t["L0_ffn_shared_gate"]], ups + [t["L0_ffn_shared_up"]],
                      downs + [t["L0_ffn_shared_down"]], len(pairs), 2)


def moe1(nc, X, ident, t):
    E, SHARED = 8, 2
    with ExitStack() as ctx:
        XT = ctx.enter_context(nc.sbuf_tensor("f1_XT", [P, NT], F32))
        GS = ctx.enter_context(nc.sbuf_tensor("f1_GS", [96, NT], BF16))
        norm_stage(nc, "f1n", X, XT, ident)
        router_stage(nc, "f1r", XT, ident, t["L1_ffn_gate_w"], E, GS)
        cut = [slice(s * P, (s + 1) * P) for s in range(SHARED)]
        gates = [t["L1_ffn_we_gate"][e] for e in range(E)] + [t["L1_ffn_ws_gate"][c, :] for c in cut]
        ups = [t["L1_ffn_we_up"][e] for e in range(E)] + [t["L1_ffn_ws_up"][c, :] for c in cut]
        downs = [t["L1_ffn_we_down"][e] for e in range(E)] + [t["L1_ffn_ws_down"][:, c] for c in cut]
        experts_stage(nc, "f1e", X, XT, ident, GS, gates, ups, downs, E, 1)


S_HEADS, DK, DV = 8, 64, 128
PAIRS_H = S_HEADS // 2
R_AU, F_FF, CK = 64, 512, 4


def conv_stage(nc, name, HT, t):
    with Stage(nc, name) as st:
        cw = st.sb("cw", [P, CK])
        cb = st.sb("cb", [P, 1])
        acc = st.sb("acc", [P, B, L])
        loaded = st.sem("loaded")
        step = st.sem("step")
        summed = st.sem("summed")
        hv = HT[:, :].rearrange("p (b t) -> p b t", b=B)
        HALF = B // 2

        with st.block() as block:
            @block.sync
            def _(sp):
                sp.dma_start(cw[:, :], t["L1_attn_conv_w"]).then_inc(loaded, 16)
                sp.dma_start(cb[:, :], column(t["L1_attn_conv_b"])).then_inc(loaded, 16)

            @block.vector
            def _(dve):
                dve.wait_ge(loaded, 32)
                link = Chain(dve, step)
                for g in range(2):
                    bs = slice(g * HALF, (g + 1) * HALF)
                    link(dve.tensor_scalar(acc[:, bs, :], hv[:, bs, :], cw[:, CK - 1:CK], None, ALU.mult))
                    for s in range(1, CK):
                        ins = dve.scalar_tensor_tensor(acc[:, bs, s:L], hv[:, bs, 0:L - s], cw[:, CK - 1 - s:CK - s],
                                                       acc[:, bs, s:L], ALU.mult, ALU.add)
                        if s < CK - 1:
                            link(ins)
                        else:
                            ins.then_inc(summed, 1)

            @block.scalar
            def _(act):
                act.wait_ge(loaded, 32)
                for g in range(2):
                    bs = slice(g * HALF, (g + 1) * HALF)
                    act.wait_ge(summed, g + 1)
                    act.activation(hv[:, bs, :], acc[:, bs, :], ACT.Silu, bias=cb[:, 0:1])


def spike_stage(nc, name, HT, SD, AUT, t):
    C = 512
    CHUNKS = NT // C
    DECAY = 0.9
    STEP = 8
    with Stage(nc, name) as st:
        w = st.sb("w", [P, S_HEADS * DK])
        wau = st.sb("wau", [P, R_AU])
        bau = st.sb("bau", [R_AU, 1])
        N = st.sb("N", [P, 2, PAIRS_H, B])
        sdp = st.ps("sdp", [P, 4, C])
        aup = st.ps("aup", [R_AU, 2, C])
        loaded = st.sem("loaded")
        projected = st.sem("projected")
        doubled = st.sem("doubled")
        au_projected = st.sem("au_projected")
        au_ready = st.sem("au_ready")
        charged = st.sem("charged")
        reset = st.sem("reset")
        zeroed = st.sem("zeroed")
        sd_flat = SD[:, :, :, :].rearrange("p x b t -> p x (b t)")

        with st.block() as block:
            @block.sync
            def _(sp):
                sp.dma_start(w[:, :], t["L1_attn_w_spike"]).then_inc(loaded, 16)
                sp.dma_start(wau[:, :], t["L1_attn_w_au"]).then_inc(loaded, 16)
                sp.dma_start(bau[:, :], column(t["L1_attn_b_au"], 0, R_AU)).then_inc(loaded, 16)

            @block.tensor
            def _(pe):
                pe.wait_ge(loaded, 48)
                for c in range(CHUNKS):
                    x = HT[:, c * C:(c + 1) * C]
                    for h in range(PAIRS_H):
                        if c >= 1:
                            pe.wait_ge(doubled, (c - 1) * PAIRS_H + h + 1)
                        pe.matmul(sdp[:, h, :], w[:, h * P:(h + 1) * P], x, start=True, stop=True
                                  ).then_inc(projected, 1)
                    if c >= 2:
                        pe.wait_ge(au_ready, c - 1)
                    pe.matmul(aup[:, c % 2, :], wau[:, :], x, start=True, stop=True).then_inc(au_projected, 1)

            @block.scalar
            def _(act):
                act.wait_ge(loaded, 48)
                for c in range(CHUNKS):
                    for h in range(PAIRS_H):
                        act.wait_ge(projected, c * PAIRS_H + h + 1)
                        act.activation(sd_flat[:, h, c * C:(c + 1) * C], sdp[:, h, :], ACT.Copy, scale=2.0
                                       ).then_inc(doubled, 1)
                    act.wait_ge(au_projected, c + 1)
                    act.activation(AUT[:, c * C:(c + 1) * C], aup[:, c % 2, :], ACT.Silu, bias=bau[:, 0:1]
                                   ).then_inc(au_ready, 1)

            @block.vector
            def _(dve):
                dve.memset(N[:, :, :, :], 0.0).then_inc(zeroed, 1)
                dve.wait_ge(zeroed, 1)
                dve.wait_ge(doubled, CHUNKS * PAIRS_H)

                def token(i, k):
                    m = SD[:, :, :, bass.ds(i, 1)].rearrange("p x b a -> p x (b a)")
                    if not early(i, 1):
                        dve.wait_ge(reset, i)
                    dve.scalar_tensor_tensor(m, N[:, k % 2, :, :], -DECAY, m, ALU.mult, ALU.add).then_inc(charged, 1)
                    dve.wait_ge(charged, i + 1)
                    dve.scalar_tensor_tensor(N[:, 1 - k % 2, :, :], m, 1.0, m, ALU.is_gt, ALU.subtract
                                             ).then_inc(reset, 1)
                for k in range(STEP):
                    token(k, k)
                with dve.Fori(1, L // STEP) as g:
                    for k in range(STEP):
                        token(g * STEP + k, k)
                dve.wait_ge(reset, L)
                for h in range(PAIRS_H):
                    dve.tensor_scalar(sd_flat[:, h, :], sd_flat[:, h, :], 1.0, None, ALU.is_gt)


def prepare_stage(nc, name, HT, SD, AUT, t, unit_in, unit_v):
    EPS = 1e-6
    U = B * PAIRS_H
    with Stage(nc, name) as st:
        wq = st.sb("wq", [P, S_HEADS * DK])
        wk = st.sb("wk", [P, S_HEADS * DK])
        wv = st.sb("wv", [P, S_HEADS * DV])
        wad = st.sb("wad", [R_AU, S_HEADS * DK])
        bad = st.sb("bad", [P, PAIRS_H])
        asp = st.sb("asp", [P, PAIRS_H])
        bsp = st.sb("bsp", [P, PAIRS_H])
        wb = st.sb("wb", [P, S_HEADS])
        wbe = st.sb("wbe", [P, S_HEADS, DK])
        bbe = st.sb("bbe", [P, PAIRS_H])
        same = st.sb("same", [P, P])
        bmat = st.sb("bmat", [P, PAIRS_H, P])
        hs = st.sb("hs", [P, 2, P])
        sq = st.sb("sq", [P, 2, 2, L])
        nrm = st.sb("nrm", [P, 2, 2, L])
        rcp = st.sb("rcp", [P, 2, 2, L])
        za = st.sb("za", [P, 2, L])
        a0 = st.sb("a0", [P, 2, L])
        b0 = st.sb("b0", [P, 2, L])
        a1 = st.sb("a1", [P, 2, L])
        b1 = st.sb("b1", [P, 2, L])
        res = st.sb("res", [P, 2, 4, L])
        vs = st.sb("vs", [P, 2, 2, 2 * DV])
        qk = st.ps("qk", [P, 2, 2, L])
        ab = st.ps("ab", [P, 2, 2, L])
        ssq = st.ps("ssq", [P, 2, L])
        cnt = st.ps("cnt", [P, 2, 2 * L])
        vp = st.ps("vp", [P, 2, 2 * DV])

        loaded = st.sem("loaded")
        built = st.sem("built")
        spread_ready = st.sem("spread_ready")
        hs_ready = st.sem("hs_ready")
        qk_projected = st.sem("qk_projected")
        ab_projected = st.sem("ab_projected")
        counted = st.sem("counted")
        v_projected = st.sem("v_projected")
        v_copied = st.sem("v_copied")
        squared = st.sem("squared")
        ssq_ready = st.sem("ssq_ready")
        rooted = st.sem("rooted")
        eps_added = st.sem("eps_added")
        inverted = st.sem("inverted")
        normed = st.sem("normed")
        za_ready = st.sem("za_ready")
        a0_ready = st.sem("a0_ready")
        b0_ready = st.sem("b0_ready")
        a1_ready = st.sem("a1_ready")
        alpha_ready = st.sem("alpha_ready")
        b1_ready = st.sem("b1_ready")
        kb_ready = st.sem("kb_ready")
        in_stored = [st.sem("in_stored0"), st.sem("in_stored1")]
        v_stored = [st.sem("v_stored0"), st.sem("v_stored1")]
        hard = SD[:, :, :, :].rearrange("p x b t -> p x (b t)")
        LOADS = 16 * (8 + S_HEADS)

        def units(eng, body):
            def batch(b):
                for h in range(PAIRS_H):
                    body(b * PAIRS_H + h, h, b)
            over(eng, B, batch)

        with st.block() as block:
            @block.sync
            def _(sp):
                rows = lambda a: a.rearrange("(x p) -> p x", p=P)
                with nc.allow_non_contiguous_dma(reason="one column of parameters for each head pair"):
                    for dst, src in [(wq[:, :], t["L1_attn_wq"]), (wk[:, :], t["L1_attn_wk"]),
                                     (wv[:, :], t["L1_attn_wv"]), (wad[:, :], t["L1_attn_w_ad"]),
                                     (bad[:, :], rows(t["L1_attn_b_ad"])),
                                     (asp[:, :], rows(t["L1_attn_alpha_spike"].rearrange("a h k -> (a h k)"))),
                                     (bsp[:, :], rows(t["L1_attn_beta_spike"].rearrange("a h k -> (a h k)"))),
                                     (wb[:, :], t["L1_attn_w_beta"])]:
                        sp.dma_start(dst, src).then_inc(loaded, 16)
                    for h in range(S_HEADS):
                        sp.dma_start(bbe[(h % 2) * DK:(h % 2 + 1) * DK, h // 2:h // 2 + 1],
                                     t["L1_attn_b_beta"][h:h + 1].partition_broadcast(DK)).then_inc(loaded, 16)

                def unit(n, h, b):
                    u = h % 2
                    sp.wait_ge(alpha_ready, n + 1)
                    sp.wait_ge(kb_ready, n + 1)
                    sp.dma_start(unit_in[bass.ds(n, 1)].rearrange("a p c t -> (a p) c t"), res[:, u, :, :]
                                 ).then_inc(in_stored[u], 16)
                    sp.wait_ge(v_copied, n + 1)
                    sp.dma_start(unit_v[bass.ds(n, 1)].rearrange("a p c t -> (a p) c t"), vs[:, u, :, :]
                                 ).then_inc(v_stored[u], 16)
                units(sp, unit)
                for u in range(2):
                    sp.wait_ge(in_stored[u], 16 * U // 2)
                    sp.wait_ge(v_stored[u], 16 * U // 2)

            @block.gpsimd
            def _(pool):
                pool.memset(same[:, :], 1.0).then_inc(built, 1)
                pool.wait_ge(built, 1)
                sv = same[:, :].rearrange("p (h c) -> p h c", h=2)
                pool.affine_select(out=sv, in_=sv, compare_op=ALU.is_ge, fill=0.0, base=0,
                                   pattern=[[-DK, 2], [0, DK]], channel_multiplier=1).then_inc(built, 1)
                pool.wait_ge(built, 2)
                pool.affine_select(out=sv, in_=sv, compare_op=ALU.is_ge, fill=0.0, base=DK - 1,
                                   pattern=[[DK, 2], [0, DK]], channel_multiplier=-1).then_inc(built, 1)

            @block.tensor
            def _(pe):
                pe.wait_ge(loaded, LOADS)
                pe.wait_ge(built, 3)
                pe.wait_ge(spread_ready, 2)

                def square_sum(n, u):
                    pe.wait_ge(squared, n + 1)
                    if not early(n, 1):
                        pe.wait_ge(rooted, n)
                    pe.matmul(ssq[:, :, :].rearrange("p c t -> p (c t)"), same[:, :],
                              sq[:, u, :, :].rearrange("p c t -> p (c t)"), start=True, stop=True
                              ).then_inc(ssq_ready, 1)

                def unit(n, h, b):
                    u = h % 2
                    first = isinstance(b, int) and h < 2
                    x = HT[:, bass.ds(b * L, L)]
                    rows = slice(h * P, (h + 1) * P)
                    if not first:
                        pe.wait_ge(normed, n - 1)
                        pe.wait_ge(za_ready, n - 1)
                        pe.wait_ge(b0_ready, n - 1)
                        pe.wait_ge(b1_ready, n - 1)
                        pe.wait_ge(alpha_ready, n - 1)
                    pe.matmul(qk[:, u, 0, :], wk[:, rows], x, start=True, stop=True)
                    pe.matmul(qk[:, u, 1, :], wq[:, rows], x, start=True, stop=True).then_inc(qk_projected, 1)
                    pe.matmul(ab[:, u, 0, :], wad[:, rows], AUT[:, bass.ds(b * L, L)], start=True, stop=True)
                    pe.matmul(ab[:, u, 1, :], wbe[:, 2 * h:2 * h + 2, :].rearrange("p a d -> p (a d)"), x,
                              start=True, stop=False)
                    fired = hard[:, h, bass.ds(b * L, L)]
                    pe.matmul(ab[:, u, 1, :], bmat[:, h, :], fired, start=False, stop=True
                              ).then_inc(ab_projected, 1)
                    pe.matmul(cnt[:, u, 0:L], same[:, :], fired, start=True, stop=True).then_inc(counted, 1)
                    square_sum(n, u)
                    if h == 0:
                        pe.wait_ge(hs_ready, b + 1)
                    if not early(n, 1) and not (isinstance(b, int) and h == 0):
                        pe.wait_ge(v_copied, n)
                    for s in range(2):
                        ins = pe.matmul(vp[:, s, :], hs[:, s, :], wv[:, 2 * h * DV:2 * (h + 1) * DV],
                                        start=True, stop=True)
                    ins.then_inc(v_projected, 1)
                units(pe, unit)

            @block.scalar
            def _(act):
                def unit(n, h, b):
                    u = h % 2
                    first = isinstance(b, int) and h < 2
                    if h == 0:
                        if not early(b, 1):
                            act.wait_ge(v_projected, n)
                        act.activation(hs[:, :, :].rearrange("p s t -> p (s t)"), HT[:, bass.ds(b * L, L)], ACT.Copy
                                       ).then_inc(hs_ready, 1)
                    act.wait_ge(qk_projected, n + 1)
                    if not first:
                        act.wait_ge(ssq_ready, n - 1)
                    act.activation(sq[:, u, :, :], qk[:, u, :, :], ACT.Square).then_inc(squared, 1)
                    act.wait_ge(ssq_ready, n + 1)
                    if not first:
                        act.wait_ge(eps_added, n - 1)
                    act.activation(nrm[:, u, :, :], ssq[:, :, :], ACT.Sqrt).then_inc(rooted, 1)
                    act.wait_ge(za_ready, n + 1)
                    if not first:
                        act.wait_ge(a1_ready, n - 1)
                        act.wait_ge(b1_ready, n - 1)
                    act.activation(a0[:, u, :], za[:, u, :], ACT.Sigmoid, bias=bad[:, h:h + 1]).then_inc(a0_ready, 1)
                    act.wait_ge(ab_projected, n + 1)
                    act.activation(b0[:, u, :], ab[:, u, 1, :], ACT.Sigmoid, bias=bbe[:, h:h + 1]
                                   ).then_inc(b0_ready, 1)
                    act.wait_ge(v_projected, n + 1)
                    if not first:
                        act.wait_ge(v_stored[u], b * 32 + (h // 2) * 16)
                    act.activation(vs[:, u, :, :], vp[:, :, :], ACT.Copy).then_inc(v_copied, 1)
                act.wait_ge(loaded, LOADS)
                units(act, unit)

            @block.vector
            def _(dve):
                dve.wait_ge(loaded, LOADS)
                dve.tensor_copy(wbe[:, :, :], wb[:, :].unsqueeze(2).to_broadcast([P, S_HEADS, DK])
                                ).then_inc(spread_ready, 1)
                dve.wait_ge(built, 3)
                dve.tensor_tensor(bmat[:, :, :], same[:, :].unsqueeze(1).to_broadcast([P, PAIRS_H, P]),
                                  bsp[:, :].unsqueeze(2).to_broadcast([P, PAIRS_H, P]), ALU.mult
                                  ).then_inc(spread_ready, 1)

                def unit(n, h, b):
                    u = h % 2
                    first = isinstance(b, int) and h < 2
                    dve.wait_ge(ab_projected, n + 1)
                    if not first:
                        dve.wait_ge(a0_ready, n - 1)
                    dve.scalar_tensor_tensor(za[:, u, :], hard[:, h, bass.ds(b * L, L)], asp[:, h:h + 1],
                                             ab[:, u, 0, :], ALU.mult, ALU.add).then_inc(za_ready, 1)
                    dve.wait_ge(rooted, n + 1)
                    if not first:
                        dve.wait_ge(normed, n - 1)
                    dve.tensor_scalar(nrm[:, u, :, :], nrm[:, u, :, :], EPS, None, ALU.add).then_inc(eps_added, 1)
                    dve.wait_ge(eps_added, n + 1)
                    dve.reciprocal(rcp[:, u, :, :], nrm[:, u, :, :]).then_inc(inverted, 1)
                    dve.wait_ge(inverted, n + 1)
                    if not first:
                        dve.wait_ge(in_stored[u], b * 32 + (h // 2) * 16)
                    dve.tensor_tensor(res[:, u, 0:2, :], qk[:, u, :, :], rcp[:, u, :, :], ALU.mult
                                      ).then_inc(normed, 1)
                    dve.wait_ge(a0_ready, n + 1)
                    dve.wait_ge(counted, n + 1)
                    if not first:
                        dve.wait_ge(alpha_ready, n - 1)
                        dve.wait_ge(kb_ready, n - 1)
                    dve.scalar_tensor_tensor(a1[:, u, :], cnt[:, u, 0:L], 0.5, a0[:, u, :], ALU.is_gt, ALU.mult
                                             ).then_inc(a1_ready, 1)
                    dve.wait_ge(b0_ready, n + 1)
                    dve.scalar_tensor_tensor(b1[:, u, :], cnt[:, u, 0:L], 0.5, b0[:, u, :], ALU.is_gt, ALU.mult
                                             ).then_inc(b1_ready, 1)
                    dve.wait_ge(a1_ready, n + 1)
                    dve.scalar_tensor_tensor(res[:, u, 2, :], cnt[:, u, 0:L], 0.5, a1[:, u, :], ALU.is_lt, ALU.add
                                             ).then_inc(alpha_ready, 1)
                    dve.wait_ge(b1_ready, n + 1)
                    dve.wait_ge(normed, n + 1)
                    dve.tensor_tensor(res[:, u, 3, :], res[:, u, 0, :], b1[:, u, :], ALU.mult).then_inc(kb_ready, 1)
                units(dve, unit)


def delta_stage(nc, name, ident, unit_in, unit_v, unit_o):
    LEVELS = 7
    DUOS = B * PAIRS_H // 2
    TAU = 4
    with Stage(nc, name) as st:
        src = st.sb("src", [P, 2, 2, 4, L])
        val = st.sb("val", [P, 2, 2, 2, 2 * DV])
        total = st.sb("total", [P, 2, 2, L])
        mask = st.sb("mask", [P, LEVELS, P])
        LT = st.sb("LT", [P, 2, TAU, P])
        BT = st.sb("BT", [P, 2, TAU, P])
        part = st.sb("part", [P, 2, TAU, P])
        T = st.sb("T", [P, 2, TAU, P])
        X = st.sb("X", [P, 2, TAU, P])
        R = st.sb("R", [P, 2, TAU, P])
        cross_ = st.sb("cross", [P, 2, 2, 2, P])
        W = st.sb("W", [P, 2, 2, 2, DV])
        V1 = st.sb("V1", [P, 2, 2, DV])
        osb = st.sb("osb", [P, 2, 2, 2, DV])
        lb = st.ps("lb", [P, 2, TAU, 2, P])
        wp = st.ps("wp", [P, 2, TAU, P])
        ep = st.ps("ep", [P, 2, 2, 2, DV])

        s_ = lambda x: st.sem(x)
        masks_ready = s_("masks_ready")
        src_loaded = [s_("src_loaded0"), s_("src_loaded1")]
        val_loaded = [s_("val_loaded0"), s_("val_loaded1")]
        diag_scored = s_("diag_scored")
        diag_ready = s_("diag_ready")
        decayed = s_("decayed")
        started = s_("started")
        scored = s_("scored")
        lt_ready = s_("lt_ready")
        part_ready = s_("part_ready")
        bt_ready = s_("bt_ready")
        kq_ready = s_("kq_ready")
        kg_ready = s_("kg_ready")
        total_ready = s_("total_ready")
        r_scored = s_("r_scored")
        r_ready = s_("r_ready")
        dt_scored = s_("dt_scored")
        t_ready = s_("t_ready")
        t_turned = s_("t_turned")
        x_ready = s_("x_ready")
        cross_scored = s_("cross_scored")
        cross_ready = s_("cross_ready")
        w0_scored = s_("w0_scored")
        w0_ready = s_("w0_ready")
        u_scored = s_("u_scored")
        v1_ready = s_("v1_ready")
        w1_scored = s_("w1_scored")
        w1_ready = s_("w1_ready")
        o_scored = s_("o_scored")
        o_ready = s_("o_ready")
        o_stored = s_("o_stored")

        def after(n, u):
            return n * 2 + (u + 1)

        def at(n, v, u):
            return (n * LEVELS + v) * 2 + (u + 1)

        with st.block() as block:
            @block.sync
            def _(sp):
                def duo(n, w, j):
                    if not early(n, 2):
                        sp.wait_ge(cross_scored, (n - 1) * 2)
                        sp.wait_ge(w0_scored, (n - 1) * 2)
                        sp.wait_ge(v1_ready, (n - 1) * 2)
                    for u in range(2):
                        sp.dma_start(src[:, w, u, :, :], unit_in[bass.ds(n * 2 + u, 1)]
                                     .rearrange("a p c t -> (a p) c t")).then_inc(src_loaded[w], 16)
                        sp.dma_start(val[:, w, u, :, :], unit_v[bass.ds(n * 2 + u, 1)]
                                     .rearrange("a p c t -> (a p) c t")).then_inc(val_loaded[w], 16)
                    if not early(n, 1):
                        store(n - 1)

                def store(n):
                    for u in range(2):
                        sp.wait_ge(o_ready, after(n, u))
                        sp.dma_start(unit_o[bass.ds(n * 2 + u, 1)].rearrange("a p c t -> (a p) c t"),
                                     osb[:, u, :, :, :].rearrange("p s h v -> p s (h v)")).then_inc(o_stored, 16)
                over_pairs(sp, DUOS, duo)
                store(DUOS - 1)
                sp.wait_ge(o_stored, 32 * DUOS)

            @block.gpsimd
            def _(pool):
                pool.memset(mask[:, :, :], 1.0).then_inc(masks_ready, 1)
                for v in range(LEVELS):
                    c = 1 << v
                    nb = P // (2 * c)
                    m = mask[:, v, :].rearrange("p (b h i) -> p b h i", b=nb, h=2)
                    pool.wait_ge(masks_ready, 3 * v + 1)
                    pool.memset(m[:, :, 0, :], 0.0).then_inc(masks_ready, 1)
                    second = m[:, :, 1, :]
                    pool.wait_ge(masks_ready, 3 * v + 2)
                    pool.affine_select(out=second, in_=second, compare_op=ALU.is_ge, fill=0.0, base=0,
                                       pattern=[[-2 * c, nb], [0, c]], channel_multiplier=1).then_inc(masks_ready, 1)
                    pool.wait_ge(masks_ready, 3 * v + 3)
                    pool.affine_select(out=second, in_=second, compare_op=ALU.is_ge, fill=0.0, base=c - 1,
                                       pattern=[[2 * c, nb], [0, c]], channel_multiplier=-1).then_inc(masks_ready, 1)

                def duo(n, w, j):
                    for u in range(2):
                        pool.wait_ge(diag_scored, after(n, u))
                        a = src[:, w, u, 2, :]
                        pool.tensor_tensor(src[:, w, u, 0:2, :], src[:, w, u, 0:2, :],
                                           a.unsqueeze(1).to_broadcast([P, 2, L]), ALU.mult).then_inc(decayed, 1)
                    for v in range(LEVELS):
                        c = 1 << v
                        nb = L // (2 * c)
                        for u in range(2):
                            tot = (src[:, w, u, 2, :] if v == 0 else total[:, u, (v - 1) % 2, 0:2 * nb]
                                   ).rearrange("p (b h) -> p b h", h=2)
                            if v == 0:
                                pool.wait_ge(decayed, after(n, u))
                            else:
                                pool.wait_ge(total_ready, at(n, v - 1, u))
                            pool.wait_ge(scored, at(n, v, u))
                            kq = src[:, w, u, 0:2, :].rearrange("p a (b h i) -> p a b h i", b=nb, h=2)[:, :, :, 1, :]
                            for x in range(2):
                                ins = pool.tensor_tensor(kq[:, x], kq[:, x],
                                                         tot[:, :, 0].unsqueeze(2).to_broadcast([P, nb, c]), ALU.mult)
                            ins.then_inc(kq_ready, 1)
                            kg = src[:, w, u, 3, :].rearrange("p (b h i) -> p b h i", b=nb, h=2)[:, :, 0, :]
                            pool.tensor_tensor(kg, kg, tot[:, :, 1].unsqueeze(2).to_broadcast([P, nb, c]), ALU.mult
                                               ).then_inc(kg_ready, 1)
                            pool.tensor_tensor(total[:, u, v % 2, 0:nb], tot[:, :, 0], tot[:, :, 1], ALU.mult
                                               ).then_inc(total_ready, 1)
                            pool.wait_ge(part_ready, at(n, v, u))
                            if v == 0:
                                pool.wait_ge(diag_ready, after(n, u))
                            else:
                                pool.wait_ge(bt_ready, at(n, v - 1, u))
                            pool.tensor_tensor(BT[:, u, :, :], BT[:, u, :, :], part[:, u, :, :], ALU.add
                                               ).then_inc(bt_ready, 1)
                over_pairs(pool, DUOS, duo)

            @block.tensor
            def _(pe):
                pe.wait_ge(masks_ready, 3 * LEVELS + 1)

                def duo(n, w, j):
                    pe.wait_ge(src_loaded[w], (j + 1) * 32)
                    for u in range(2):
                        if not early(n, 1):
                            pe.wait_ge(cross_ready, after(n - 1, u))
                        for k in range(TAU):
                            h, s = divmod(k, 2)
                            rows, cols = slice(h * DK, (h + 1) * DK), slice(s * P, (s + 1) * P)
                            ins = pe.matmul(lb[:, u, k, 1, :], src[rows, w, u, 3, cols], src[rows, w, u, 1, cols],
                                            start=True, stop=True)
                        ins.then_inc(diag_scored, 1)
                    for v in range(LEVELS):
                        for u in range(2):
                            if v == 0:
                                pe.wait_ge(decayed, after(n, u))
                                pe.wait_ge(diag_ready, after(n, u))
                            else:
                                pe.wait_ge(kq_ready, at(n, v - 1, u))
                                pe.wait_ge(kg_ready, at(n, v - 1, u))
                                pe.wait_ge(lt_ready, at(n, v - 1, u))
                                pe.wait_ge(part_ready, at(n, v - 1, u))
                            for k in range(TAU):
                                h, s = divmod(k, 2)
                                rows, cols = slice(h * DK, (h + 1) * DK), slice(s * P, (s + 1) * P)
                                ins = pe.matmul(lb[:, u, k, :, :], src[rows, w, u, 3, cols],
                                                src[rows, w, u, 0:2, cols], start=True, stop=True)
                            ins.then_inc(scored, 1)
                        for u in range(2):
                            pe.wait_ge(lt_ready, at(n, v, u))
                            if v == 0:
                                pe.wait_ge(started, after(n, u))
                                if not early(n, 1):
                                    pe.wait_ge(w1_ready, after(n - 1, u))
                            else:
                                pe.wait_ge(x_ready, at(n, v - 1, u))
                            for k in range(TAU):
                                ins = pe.matmul(wp[:, u, k, :], LT[:, u, k, :], T[:, u, k, :], start=True, stop=True)
                            ins.then_inc(r_scored, 1)
                        for u in range(2):
                            pe.wait_ge(r_ready, at(n, v, u))
                            for k in range(TAU):
                                ins = pe.matmul(wp[:, u, k, :], X[:, u, k, :], R[:, u, k, :], start=True, stop=True)
                            ins.then_inc(dt_scored, 1)
                        for u in range(2):
                            pe.wait_ge(t_ready, at(n, v, u))
                            for k in range(TAU):
                                ins = pe.transpose(wp[:, u, k, :], T[:, u, k, :], ident[:, :])
                            ins.then_inc(t_turned, 1)
                    pe.wait_ge(val_loaded[w], (j + 1) * 32)
                    for u in range(2):
                        pe.wait_ge(kq_ready, at(n, LEVELS - 1, u))
                        pe.wait_ge(kg_ready, at(n, LEVELS - 1, u))
                        pe.wait_ge(part_ready, at(n, LEVELS - 1, u))
                        for h in range(2):
                            rows = slice(h * DK, (h + 1) * DK)
                            ins = pe.matmul(lb[:, u, 2 * h, :, :], src[rows, w, u, 3, 0:P], src[rows, w, u, 0:2, P:L],
                                            start=True, stop=True)
                        ins.then_inc(cross_scored, 1)
                        pe.wait_ge(x_ready, at(n, LEVELS - 1, u))
                        for h in range(2):
                            ins = pe.matmul(wp[:, u, h, :], X[:, u, 2 * h, :], val[:, w, u, 0, h * DV:(h + 1) * DV],
                                            start=True, stop=True)
                        ins.then_inc(w0_scored, 1)
                    for u in range(2):
                        pe.wait_ge(cross_ready, after(n, u))
                        pe.wait_ge(w0_ready, after(n, u))
                        for h in range(2):
                            ins = pe.matmul(wp[:, u, 2 + h, :], cross_[:, u, h, 0, :], W[:, u, 0, h, :],
                                            start=True, stop=True)
                        ins.then_inc(u_scored, 1)
                    for u in range(2):
                        pe.wait_ge(v1_ready, after(n, u))
                        for h in range(2):
                            ins = pe.matmul(wp[:, u, h, :], X[:, u, 2 * h + 1, :], V1[:, u, h, :],
                                            start=True, stop=True)
                        ins.then_inc(w1_scored, 1)
                    for u in range(2):
                        pe.wait_ge(w1_ready, after(n, u))
                        pe.wait_ge(bt_ready, at(n, LEVELS - 1, u))
                        if not early(n, 1):
                            pe.wait_ge(o_ready, after(n - 1, u))
                        for h in range(2):
                            pe.matmul(ep[:, u, 0, h, :], BT[:, u, 2 * h, :], W[:, u, 0, h, :], start=True, stop=True)
                            pe.matmul(ep[:, u, 1, h, :], BT[:, u, 2 * h + 1, :], W[:, u, 1, h, :],
                                      start=True, stop=False)
                            ins = pe.matmul(ep[:, u, 1, h, :], cross_[:, u, h, 1, :], W[:, u, 0, h, :],
                                            start=False, stop=True)
                        ins.then_inc(o_scored, 1)
                over_pairs(pe, DUOS, duo)

            @block.vector
            def _(dve):
                dve.wait_ge(masks_ready, 3 * LEVELS + 1)
                eye = ident[:, :].unsqueeze(1).to_broadcast([P, TAU, P])

                def duo(n, w, j):
                    for u in range(2):
                        dve.wait_ge(diag_scored, after(n, u))
                        if not early(n, 1):
                            dve.wait_ge(o_scored, after(n - 1, u))
                        dve.tensor_tensor(BT[:, u, :, :], lb[:, u, :, 1, :], eye, ALU.mult).then_inc(diag_ready, 1)
                        dve.tensor_copy(T[:, u, :, :], eye)
                        dve.tensor_copy(X[:, u, :, :], eye).then_inc(started, 1)
                    for v in range(LEVELS):
                        m = mask[:, v, :].unsqueeze(1).to_broadcast([P, TAU, P])
                        for u in range(2):
                            dve.wait_ge(scored, at(n, v, u))
                            if v > 0:
                                dve.wait_ge(r_scored, at(n, v - 1, u))
                            dve.tensor_tensor(LT[:, u, :, :], lb[:, u, :, 0, :], m, ALU.mult).then_inc(lt_ready, 1)
                            if v > 0:
                                dve.wait_ge(bt_ready, at(n, v - 1, u))
                            dve.tensor_tensor(part[:, u, :, :], lb[:, u, :, 1, :], m, ALU.mult
                                              ).then_inc(part_ready, 1)
                        for u in range(2):
                            dve.wait_ge(dt_scored, at(n, v, u))
                            dve.tensor_tensor(T[:, u, :, :], T[:, u, :, :], wp[:, u, :, :], ALU.subtract
                                              ).then_inc(t_ready, 1)
                    for u in range(2):
                        dve.wait_ge(cross_scored, after(n, u))
                        dve.tensor_copy(cross_[:, u, :, :, :], lb[:, u, 0:TAU:2, :, :]).then_inc(cross_ready, 1)
                    for u in range(2):
                        dve.wait_ge(u_scored, after(n, u))
                        dve.wait_ge(val_loaded[w], (j + 1) * 32)
                        dve.tensor_tensor(V1[:, u, :, :], val[:, w, u, 1, :].rearrange("p (h v) -> p h v", h=2),
                                          wp[:, u, 2:4, :], ALU.subtract).then_inc(v1_ready, 1)
                over_pairs(dve, DUOS, duo)

            @block.scalar
            def _(act):
                def duo(n, w, j):
                    for v in range(LEVELS):
                        for u in range(2):
                            act.wait_ge(r_scored, at(n, v, u))
                            act.activation(R[:, u, :, :], wp[:, u, :, :], ACT.Copy).then_inc(r_ready, 1)
                        for u in range(2):
                            act.wait_ge(t_turned, at(n, v, u))
                            act.activation(X[:, u, :, :], wp[:, u, :, :], ACT.Copy).then_inc(x_ready, 1)
                    for u in range(2):
                        act.wait_ge(w0_scored, after(n, u))
                        act.activation(W[:, u, 0, :, :], wp[:, u, 0:2, :], ACT.Copy).then_inc(w0_ready, 1)
                    for u in range(2):
                        act.wait_ge(w1_scored, after(n, u))
                        act.activation(W[:, u, 1, :, :], wp[:, u, 0:2, :], ACT.Copy).then_inc(w1_ready, 1)
                    for u in range(2):
                        act.wait_ge(o_scored, after(n, u))
                        if not early(n, 1):
                            act.wait_ge(o_stored, n * 32)
                        act.activation(osb[:, u, :, :, :], ep[:, u, :, :, :], ACT.Copy).then_inc(o_ready, 1)
                over_pairs(act, DUOS, duo)


def gate_stage(nc, name, X, XN, XNT, Y, ident, t, unit_o):
    EPS = 1e-6
    S = S_HEADS
    with Stage(nc, name) as st:
        wo = st.sb("wo", [P, S, D])
        whn = st.sb("whn", [P, S, DV])
        wu1 = st.sb("wu1", [P, R_AU])
        bu1 = st.sb("bu1", [R_AU, 1])
        wu2 = st.sb("wu2", [R_AU, D])
        bu2 = st.sb("bu2", [P, D])
        U1 = st.sb("U1", [R_AU, NT])
        o = st.sb("o", [P, 2, S, DV])
        sq = st.sb("sq", [P, 2, S, DV])
        ms = st.sb("ms", [P, 2, S])
        var = st.sb("var", [P, 2, S])
        rt = st.sb("rt", [P, TILES, S])
        rs = st.sb("rs", [P, 2, S])
        on = st.sb("on", [P, 2, S, DV])
        on2 = st.sb("on2", [P, 2, S, DV])
        oT = st.sb("oT", [P, 2, S, P])
        u1 = st.sb("u1", [R_AU, 2, P])
        gz = st.sb("gz", [P, TILES, D])
        gate = st.sb("gate", [P, TILES, D])
        gated = st.sb("gated", [P, 2, D])
        up_ = st.ps("up", [R_AU, 2, 512])
        tp = st.ps("tp", [P, S, P])
        gp = st.ps("gp", [P, 2, 512])
        op = st.ps("op", [P, 2, 512])
        loaded = st.sem("loaded")
        u_projected = st.sem("u_projected")
        u_ready = st.sem("u_ready")
        g_projected = st.sem("g_projected")
        gz_ready = st.sem("gz_ready")
        g_ready = st.sem("g_ready")
        o_loaded = [st.sem("o_loaded0"), st.sem("o_loaded1")]
        squared = st.sem("squared")
        ms_ready = st.sem("ms_ready")
        var_ready = st.sem("var_ready")
        rt_ready = st.sem("rt_ready")
        rs_ready = st.sem("rs_ready")
        on_ready = st.sem("on_ready")
        on2_ready = st.sem("on2_ready")
        turned = st.sem("turned")
        oT_ready = st.sem("oT_ready")
        projected = st.sem("projected")
        gated_ready = st.sem("gated_ready")
        y_ready = st.sem("y_ready")
        added = st.sem("added")
        C = 512

        with st.block() as block:
            @block.sync
            def _(sp):
                for dst, src in [(wo[:, :, :], t["L1_attn_w_out"].rearrange("(h v) d -> v h d", v=DV)),
                                 (whn[:, :, :].rearrange("p h v -> p (h v)"),
                                  t["L1_attn_w_hn"].rearrange("h v -> (h v)").partition_broadcast(P)),
                                 (wu1[:, :], t["L1_attn_w_u1"]), (bu1[:, :], column(t["L1_attn_b_u1"], 0, R_AU)),
                                 (wu2[:, :], t["L1_attn_w_u2"]), (bu2[:, :], t["L1_attn_b_u2"].partition_broadcast(P))]:
                    sp.dma_start(dst, src).then_inc(loaded, 16)
                ov = unit_o.rearrange("(b x) p s f -> b p s x f", x=PAIRS_H)

                def unit(n, u, j):
                    if not early(n, 2):
                        sp.wait_ge(on_ready, n - 1)
                    sp.dma_start(o[:, u, :, :].rearrange("p (x h) v -> p x (h v)", x=PAIRS_H),
                                 ov[bass.ds(j, 1), :, u, :, :].rearrange("b p x f -> (b p) x f")
                                 ).then_inc(o_loaded[u], 16)
                over_pairs(sp, TILES, unit)

            @block.gpsimd
            def _(pool):
                def unit(n, u, j):
                    pool.wait_ge(on_ready, n + 1)
                    if not early(n, 2):
                        pool.wait_ge(turned, n - 1)
                    pool.tensor_tensor(on2[:, u, :, :], on[:, u, :, :], whn[:, :, :], ALU.mult).then_inc(on2_ready, 1)
                pool.wait_ge(loaded, 96)
                over_pairs(pool, TILES, unit)

            @block.tensor
            def _(pe):
                pe.wait_ge(loaded, 96)
                for c in range(NT // C):
                    if c >= 2:
                        pe.wait_ge(u_ready, c - 1)
                    pe.matmul(up_[:, c % 2, :], wu1[:, :], XNT[:, c * C:(c + 1) * C], start=True, stop=True
                              ).then_inc(u_projected, 1)
                for n in range(TILES):
                    pe.wait_ge(u_ready, n // 4 + 1)
                    if n >= 2:
                        pe.wait_ge(gz_ready, n - 1)
                    pe.matmul(gp[:, n % 2, 0:D], U1[:, n * P:(n + 1) * P], wu2[:, :], start=True, stop=True
                              ).then_inc(g_projected, 1)

                def unit(n, u, j):
                    pe.wait_ge(on2_ready, n + 1)
                    if not early(n, 1):
                        pe.wait_ge(oT_ready, n)
                    for h in range(S):
                        ins = pe.transpose(tp[:, h, :], on2[:, u, h, :], ident[:, :])
                    ins.then_inc(turned, 1)
                    pe.wait_ge(oT_ready, n + 1)
                    if not early(n, 2):
                        pe.wait_ge(gated_ready, n - 1)
                    for h in range(S):
                        ins = pe.matmul(op[:, u, 0:D], oT[:, u, h, :], wo[:, h, :], start=(h == 0), stop=(h == S - 1))
                    ins.then_inc(projected, 1)
                over_pairs(pe, TILES, unit)

            @block.scalar
            def _(act):
                act.wait_ge(loaded, 96)
                for c in range(NT // C):
                    act.wait_ge(u_projected, c + 1)
                    act.activation(U1[:, c * C:(c + 1) * C], up_[:, c % 2, :], ACT.Silu, bias=bu1[:, 0:1]
                                   ).then_inc(u_ready, 1)
                act.wait_ge(gz_ready, TILES)
                act.activation(gate[:, :, :], gz[:, :, :], ACT.Sigmoid).then_inc(g_ready, 1)

                def unit(n, u, j):
                    act.wait_ge(o_loaded[u], (j + 1) * 16)
                    if not early(n, 2):
                        act.wait_ge(ms_ready, n - 1)
                    act.activation(sq[:, u, :, :], o[:, u, :, :], ACT.Square).then_inc(squared, 1)
                    act.wait_ge(var_ready, n + 1)
                    act.activation(rt[:, u, :], var[:, u, :], ACT.Sqrt).then_inc(rt_ready, 1)
                    act.wait_ge(turned, n + 1)
                    if not early(n, 2):
                        act.wait_ge(projected, n - 1)
                    act.activation(oT[:, u, :, :], tp[:, :, :], ACT.Copy).then_inc(oT_ready, 1)
                over_pairs(act, TILES, unit)

            @block.vector
            def _(dve):
                dve.wait_ge(loaded, 96)
                for n in range(TILES):
                    dve.wait_ge(g_projected, n + 1)
                    dve.tensor_tensor(gz[:, n, :], gp[:, n % 2, 0:D], bu2[:, :], ALU.add).then_inc(gz_ready, 1)
                dve.wait_ge(g_ready, 1)

                def unit(n, u, j):
                    dve.wait_ge(squared, n + 1)
                    if not early(n, 2):
                        dve.wait_ge(var_ready, n - 1)
                        dve.wait_ge(rt_ready, n - 1)
                    dve.tensor_reduce(ms[:, u, :], sq[:, u, :, :], AX.X, ALU.add).then_inc(ms_ready, 1)
                    dve.wait_ge(ms_ready, n + 1)
                    dve.tensor_scalar(var[:, u, :], ms[:, u, :], 1.0 / DV, EPS, ALU.mult, ALU.add).then_inc(var_ready, 1)
                    dve.wait_ge(rt_ready, n + 1)
                    dve.reciprocal(rs[:, u, :], rt[:, u, :]).then_inc(rs_ready, 1)
                    dve.wait_ge(rs_ready, n + 1)
                    if not early(n, 2):
                        dve.wait_ge(on2_ready, n - 1)
                    dve.tensor_tensor(on[:, u, :, :], o[:, u, :, :], rs[:, u, :].unsqueeze(2).to_broadcast([P, S, DV]),
                                      ALU.mult).then_inc(on_ready, 1)
                    dve.wait_ge(projected, n + 1)
                    one = lambda a: a[:, bass.ds(n, 1), :].rearrange("p a d -> p (a d)")
                    dve.tensor_tensor(gated[:, u, :], op[:, u, 0:D], one(gate), ALU.mult).then_inc(gated_ready, 1)
                    dve.wait_ge(gated_ready, n + 1)
                    dve.tensor_tensor(one(Y), gated[:, u, :], one(XN), ALU.add).then_inc(y_ready, 1)
                    dve.wait_ge(y_ready, n + 1)
                    dve.tensor_tensor(one(X), one(X), one(Y), ALU.add).then_inc(added, 1)
                over_pairs(dve, TILES, unit)


def delta(nc, X, ident, t):
    unit_in = nc.dram_tensor("unit_in", [B * PAIRS_H, P, 4, L], F32, kind="Internal").ap()
    unit_v = nc.dram_tensor("unit_v", [B * PAIRS_H, P, 2, 2 * DV], F32, kind="Internal").ap()
    unit_o = nc.dram_tensor("unit_o", [B * PAIRS_H, P, 2, 2 * DV], F32, kind="Internal").ap()
    with ExitStack() as ctx:
        XN = ctx.enter_context(nc.sbuf_tensor("d_XN", [P, TILES, D], F32))
        XNT = ctx.enter_context(nc.sbuf_tensor("d_XNT", [P, NT], F32))
        norm_stage(nc, "dn", X, XNT, ident, XN=XN)
        with ExitStack() as early_part:
            HT = early_part.enter_context(nc.sbuf_tensor("d_HT", [P, NT], F32))
            norm_stage(nc, "dh", XN, HT, ident, eps=1e-6, centre=False, weight=t["L1_attn_w_norm_in"])
            conv_stage(nc, "dc", HT, t)
            SD = early_part.enter_context(nc.sbuf_tensor("d_SD", [P, PAIRS_H, B, L], F32))
            AUT = early_part.enter_context(nc.sbuf_tensor("d_AUT", [R_AU, NT], F32))
            spike_stage(nc, "ds", HT, SD, AUT, t)
            prepare_stage(nc, "dp", HT, SD, AUT, t, unit_in, unit_v)
        delta_stage(nc, "dd", ident, unit_in, unit_v, unit_o)
        Y = ctx.enter_context(nc.sbuf_tensor("d_Y", [P, TILES, D], F32))
        gate_stage(nc, "dg", X, XN, XNT, Y, ident, t, unit_o)
        norm_stage(nc, "df", Y, XNT, ident, eps=1e-6, centre=False, weight=t["L1_attn_w_ffn"])
        cut = [slice(s * P, (s + 1) * P) for s in range(F_FF // P)]
        experts_stage(nc, "de", X, XNT, ident, None, [t["L1_attn_w_ff1"][:, c] for c in cut],
                      [t["L1_attn_w_ff3"][:, c] for c in cut], [t["L1_attn_w_ff2"][c, :] for c in cut], 0, 1,
                      direct=True)


NAMES = ["x", "ctx_768", "L0_attn_Wqkv_w", "L0_attn_Wqkv_b", "L0_attn_out_w", "L0_attn_out_b", "L0_attn_W_static",
         "L0_attn_Lambda_raw", "L0_attn_Gamma", "L0_attn_gate_w1", "L0_attn_gate_b1", "L0_attn_gate_w2",
         "L0_attn_gate_b2", "L0_xattn_Wq", "L0_xattn_bq", "L0_xattn_Wk", "L0_xattn_bk", "L0_xattn_Wv", "L0_xattn_bv",
         "L0_xattn_Wo", "L0_xattn_bo", "L0_ffn_gate_w", "L0_ffn_gate_bias", "L0_ffn_expert_gate",
         "L0_ffn_expert_up", "L0_ffn_expert_down", "L0_ffn_shared_gate", "L0_ffn_shared_up",
         "L0_ffn_shared_down", "L1_attn_w_norm_in", "L1_attn_conv_w", "L1_attn_conv_b", "L1_attn_wq",
         "L1_attn_wk", "L1_attn_wv", "L1_attn_w_out", "L1_attn_w_spike", "L1_attn_w_au", "L1_attn_b_au",
         "L1_attn_w_ad", "L1_attn_b_ad", "L1_attn_alpha_spike", "L1_attn_w_beta", "L1_attn_b_beta",
         "L1_attn_beta_spike", "L1_attn_w_hn", "L1_attn_w_u1", "L1_attn_b_u1", "L1_attn_w_u2", "L1_attn_b_u2",
         "L1_attn_w_ffn", "L1_attn_w_ff1", "L1_attn_w_ff3", "L1_attn_w_ff2", "L1_xattn_Wq", "L1_xattn_bq",
         "L1_xattn_Wk", "L1_xattn_bk", "L1_xattn_Wv", "L1_xattn_bv", "L1_xattn_Wo", "L1_xattn_bo",
         "L1_xattn_scale", "L1_ffn_gate_w", "L1_ffn_we_gate", "L1_ffn_we_up", "L1_ffn_we_down",
         "L1_ffn_ws_gate", "L1_ffn_ws_up", "L1_ffn_ws_down"]


def decoder(nc, t, out):
    def dram(name, shape, dt=F32):
        return nc.dram_tensor(name, shape, dt, kind="Internal").ap()

    with ExitStack() as ctx:
        X = ctx.enter_context(nc.sbuf_tensor("X", [P, TILES, D], F32))
        ident = ctx.enter_context(nc.sbuf_tensor("ident", [P, P], F32))
        setup_stage(nc, X, ident, t["x"])
        q_parts = dram("q_parts", [B, P, 3, L], BF16)
        k_self = dram("k_self", [B, P, 3, L], BF16)
        k_ctx = dram("k_ctx", [B, P, 3, LC], BF16)
        v_self = dram("v_self", [B, H // HG, L, HG * HD])
        v_ctx = dram("v_ctx", [B, H // HG, LC, HG * HD])
        y_units = dram("y_units", [UNITS, L, HG * HD])

        with nc.sbuf_tensor("XT", [P, NT], F32) as XT:
            norm_stage(nc, "n0", X, XT, ident)
            w, bias = t["L0_attn_Wqkv_w"], t["L0_attn_Wqkv_b"]
            project_stage(nc, "q0", XT, w, bias, HD ** -0.5, q_parts, 0)
            project_stage(nc, "k0", XT, w, bias, 1.0, k_self, P)
            value_stage(nc, "v0", XT, w, bias, v_self)
            attention_stage(nc, "s0", q_parts, k_self, v_self, y_units, ident, L, causal=True)
            mix_stage(nc, "m0", X, XT, ident, t, y_units)
        cross(nc, "c0", X, ident, t, "L0_xattn", q_parts, k_ctx, v_ctx, y_units, clip=True)
        moe0(nc, X, ident, t)
        delta(nc, X, ident, t)
        cross(nc, "c1", X, ident, t, "L1_xattn", q_parts, k_ctx, v_ctx, y_units, clip=False)
        moe1(nc, X, ident, t)
        with Stage(nc, "store") as st:
            stored = st.sem("stored")
            with st.block() as block:
                @block.sync
                def _(sp):
                    sp.dma_start(out.rearrange("b (s p) d -> p (b s) d", p=P), X[:, :, :]).then_inc(stored, 16)
                    sp.wait_ge(stored, 16)


def kernel(**inputs):
    import numpy as _np
    import concourse.bacc as _bacc
    from concourse import mybir as _mybir
    from concourse.bass_utils import run_bass_kernel_spmd as _run

    nc = _bacc.Bacc("TRN2", target_bir_lowering=False, num_devices=1)
    arrays, t = {}, {}
    for name in NAMES:
        a = _np.ascontiguousarray(inputs[name])
        arrays[f"in_{name}_dram"] = a
        t[name] = nc.dram_tensor(f"in_{name}_dram", a.shape, _mybir.dt.from_np(a.dtype), kind="ExternalInput").ap()
    out = nc.dram_tensor("out_0_dram", (B, L, D), F32, kind="ExternalOutput").ap()
    decoder(nc, t, out)
    r = _run(nc, [arrays], core_ids=[0])
    return r.results[0]["out_0_dram"]
```

```python
from contextlib import ExitStack

import concourse.bass as bass
from concourse import mybir

ALU = mybir.AluOpType
ACT = mybir.ActivationFunctionType
AX = mybir.AxisListType
F32 = mybir.dt.float32
BF16 = mybir.dt.bfloat16
I32 = mybir.dt.int32

P = 128
B, L, D = 16, 256, 128
NT = B * L
TILES = NT // P
LC, DC = 1601, 96
H, HD = 16, 8
HG = 4
UNITS = B * H // HG
NEG = -10000.0
CLAMP = 10000.0


class Stage:

    def __init__(self, nc, name):
        self.nc, self.name, self.ctx, self.sems = nc, name, ExitStack(), []

    def __enter__(self):
        return self

    def sb(self, name, shape, dt=F32):
        return self.ctx.enter_context(self.nc.sbuf_tensor(f"{self.name}_{name}", shape, dt))

    def ps(self, name, shape, dt=F32):
        return self.ctx.enter_context(self.nc.psum_tensor(f"{self.name}_{name}", shape, dt))

    def sem(self, name):
        s = self.nc.alloc_semaphore(f"{self.name}_{name}")
        self.sems.append(s)
        return s

    def block(self):
        return self.nc.Block(f"{self.name}_block")

    def __exit__(self, *e):
        if e[0] is None:
            for s in self.sems:
                self.nc.gpsimd.sem_clear(s)
                self.nc.release_semaphore(s)
            self.nc.all_engine_barrier()
        self.ctx.close()
        return False


def over_pairs(eng, total, body):
    body(0, 0, 0)
    body(1, 1, 0)
    with eng.Fori(1, total // 2 - 1) as j:
        body(j * 2, 0, j)
        body(j * 2 + 1, 1, j)
    body(total - 2, 0, total // 2 - 1)
    body(total - 1, 1, total // 2 - 1)


def over_fours(eng, total, body):
    for v in range(4):
        body(v, v, 0)
    with eng.Fori(1, total // 4 - 1) as j:
        for v in range(4):
            body(j * 4 + v, v, j)
    for v in range(4):
        body(total - 4 + v, v, total // 4 - 1)


def early(n, k):
    return isinstance(n, int) and n < k


def over(eng, total, body):
    body(0)
    with eng.Fori(1, total) as n:
        body(n)


class Chain:

    def __init__(self, eng, sem):
        self.eng, self.sem, self.count = eng, sem, 0

    def __call__(self, instruction):
        self.count += 1
        instruction.then_inc(self.sem, 1)
        self.eng.wait_ge(self.sem, self.count)


def setup_stage(nc, X, ident, x_in):
    with Stage(nc, "setup") as st:
        x_loaded = st.sem("x_loaded")
        ident_zeroed = st.sem("ident_zeroed")
        with st.block() as block:
            @block.sync
            def _(sp):
                sp.dma_start(X[:, :, :], x_in.rearrange("b (s p) d -> p (b s) d", p=P)).then_inc(x_loaded, 16)
                sp.wait_ge(x_loaded, 16)

            @block.gpsimd
            def _(pool):
                pool.memset(ident[:, :], 0.0).then_inc(ident_zeroed, 1)
                pool.wait_ge(ident_zeroed, 1)
                pool.affine_select(out=ident[:, :], in_=ident[:, :], compare_op=ALU.not_equal, fill=1.0,
                                   base=0, pattern=[[-1, P]], channel_multiplier=1)


def norm_stage(nc, name, X, XT, ident, eps=1e-5, centre=True, XN=None, weight=None):
    GROUPS = 4
    GT = TILES // GROUPS
    with Stage(nc, name) as st:
        xn = XN if XN is not None else st.sb("xn", [P, TILES, D])
        sq = st.sb("sq", [P, TILES, D])
        total = st.sb("total", [P, TILES])
        mean = st.sb("mean", [P, TILES])
        power = st.sb("power", [P, TILES])
        var = st.sb("var", [P, TILES])
        std = st.sb("std", [P, TILES])
        rstd = st.sb("rstd", [P, TILES])
        wcol = st.sb("wcol", [P, 1])
        tp = st.ps("tp", [P, 2, 4, P])
        summed = st.sem("summed")
        meaned = st.sem("meaned")
        centred = st.sem("centred")
        squared = st.sem("squared")
        powered = st.sem("powered")
        var_ready = st.sem("var_ready")
        std_ready = st.sem("std_ready")
        rstd_ready = st.sem("rstd_ready")
        xn_ready = st.sem("xn_ready")
        turned = st.sem("turned")
        copied = st.sem("copied")
        w_loaded = st.sem("w_loaded")
        src = xn if centre else X

        with st.block() as block:
            @block.sync
            def _(sp):
                if weight is not None:
                    sp.dma_start(wcol[:, :], weight.rearrange("(p a) -> p a", a=1)).then_inc(w_loaded, 16)
                    sp.wait_ge(w_loaded, 16)

            @block.vector
            def _(dve):
                for g in range(GROUPS):
                    s = slice(g * GT, (g + 1) * GT)
                    if centre:
                        dve.tensor_reduce(total[:, s], X[:, s, :], AX.X, ALU.add).then_inc(summed, 1)
                        dve.wait_ge(summed, g + 1)
                        dve.tensor_scalar(mean[:, s], total[:, s], 1.0 / D, None, ALU.mult).then_inc(meaned, 1)
                        dve.wait_ge(meaned, g + 1)
                        dve.tensor_tensor(xn[:, s, :], X[:, s, :],
                                          mean[:, s].unsqueeze(2).to_broadcast([P, GT, D]),
                                          ALU.subtract).then_inc(centred, 1)
                for g in range(GROUPS):
                    s = slice(g * GT, (g + 1) * GT)
                    dve.wait_ge(squared, g + 1)
                    dve.tensor_reduce(power[:, s], sq[:, s, :], AX.X, ALU.add).then_inc(powered, 1)
                    dve.wait_ge(powered, g + 1)
                    dve.tensor_scalar(var[:, s], power[:, s], 1.0 / D, eps, ALU.mult, ALU.add).then_inc(var_ready, 1)
                for g in range(GROUPS):
                    s = slice(g * GT, (g + 1) * GT)
                    dve.wait_ge(std_ready, g + 1)
                    dve.reciprocal(rstd[:, s], std[:, s]).then_inc(rstd_ready, 1)
                    dve.wait_ge(rstd_ready, g + 1)
                    dve.tensor_tensor(xn[:, s, :], src[:, s, :], rstd[:, s].unsqueeze(2).to_broadcast([P, GT, D]),
                                      ALU.mult).then_inc(xn_ready, 1)

            @block.gpsimd
            def _(pool):
                for g in range(GROUPS):
                    s = slice(g * GT, (g + 1) * GT)
                    if centre:
                        pool.wait_ge(centred, g + 1)
                    pool.tensor_tensor(sq[:, s, :], src[:, s, :], src[:, s, :], ALU.mult).then_inc(squared, 1)

            @block.tensor
            def _(pe):
                for n in range(TILES):
                    pe.wait_ge(xn_ready, n // GT + 1)
                    if n % 4 == 0 and n >= 8:
                        pe.wait_ge(copied, n // 4 - 1)
                    ins = pe.transpose(tp[:, (n // 4) % 2, n % 4, :], xn[:, n, :], ident[:, :])
                    if n % 4 == 3:
                        ins.then_inc(turned, 1)

            @block.scalar
            def _(act):
                for g in range(GROUPS):
                    s = slice(g * GT, (g + 1) * GT)
                    act.wait_ge(var_ready, g + 1)
                    act.activation(std[:, s], var[:, s], ACT.Sqrt).then_inc(std_ready, 1)
                if weight is not None:
                    act.wait_ge(w_loaded, 16)
                for q in range(TILES // 4):
                    act.wait_ge(turned, q + 1)
                    act.activation(XT[:, q * 4 * P:(q + 1) * 4 * P], tp[:, q % 2, :, :].rearrange("p a b -> p (a b)"),
                                   ACT.Copy if weight is None else ACT.Identity,
                                   scale=1.0 if weight is None else wcol[:, 0:1]).then_inc(copied, 1)


def column(vec, base=0, n=P):
    return vec[base:base + n].rearrange("(p a) -> p a", a=1)


def by_dimension(vec, base=0):
    return vec[base:base + P].rearrange("(h d) -> d h", d=HD)


def project_stage(nc, name, XT, w, bias, factor, dst, wcols=0, factor_dram=None):
    with Stage(nc, name) as st:
        w_in = st.sb("w_in", [P, P])
        w_sb = st.sb("w", [P, P])
        b_sb = st.sb("b", [P, 1])
        f_sb = st.sb("f", [P, 1])
        full = st.sb("full", [P, 2, L])
        rest = st.sb("rest", [P, 2, L])
        rest2 = st.sb("rest2", [P, 2, L])
        parts = st.sb("parts", [P, 2, 3, L], BF16)
        proj = st.ps("proj", [P, 2, 512])
        loaded = st.sem("loaded")
        w_sorted = st.sem("w_sorted")
        projected = st.sem("projected")
        biased = st.sem("biased")
        evacuated = st.sem("evacuated")
        hi_ready = st.sem("hi_ready")
        rest_ready = st.sem("rest_ready")
        mid_ready = st.sem("mid_ready")
        rest2_ready = st.sem("rest2_ready")
        lo_ready = st.sem("lo_ready")
        stored = [st.sem("stored0"), st.sem("stored1")]

        with st.block() as block:
            @block.sync
            def _(sp):
                sp.dma_start(w_in[:, :], w[:, wcols:wcols + P]).then_inc(loaded, 16)
                with nc.allow_non_contiguous_dma(reason="one bias for each partition"):
                    sp.dma_start(b_sb[:, :], by_dimension(bias, wcols)).then_inc(loaded, 16)
                if factor_dram is not None:
                    sp.dma_start(f_sb[:, :], factor_dram.partition_broadcast(P)).then_inc(loaded, 16)

                def unit(n, u, j):
                    sp.wait_ge(lo_ready, n + 1)
                    sp.dma_start(dst[bass.ds(n, 1), :, :, :].rearrange("a c p t -> (a p) c t"),
                                 parts[:, u, :, :]).then_inc(stored[u], 16)
                over_pairs(sp, B, unit)
                sp.wait_ge(stored[0], 16 * B // 2)
                sp.wait_ge(stored[1], 16 * B // 2)

            @block.tensor
            def _(pe):
                pe.wait_ge(w_sorted, 1)

                def unit(n, u, j):
                    if not early(n, 2):
                        pe.wait_ge(evacuated, n - 1)
                    pe.matmul(proj[:, u, 0:L], w_sb[:, :], XT[:, bass.ds(n * L, L)],
                              start=True, stop=True).then_inc(projected, 1)
                over_pairs(pe, B, unit)

            @block.vector
            def _(dve):
                dve.wait_ge(loaded, 48 if factor_dram is not None else 32)
                dve.tensor_copy(w_sb[:, :].rearrange("p (d h) -> p d h", d=HD),
                                w_in[:, :].rearrange("p (h d) -> p d h", d=HD)).then_inc(w_sorted, 1)

                def unit(n, u, j):
                    dve.wait_ge(projected, n + 1)
                    if not early(n, 2):
                        dve.wait_ge(rest_ready, n - 1)
                    dve.tensor_scalar(full[:, u, :], proj[:, u, 0:L], b_sb[:, 0:1],
                                      f_sb[:, 0:1] if factor_dram is not None else float(factor),
                                      ALU.add, ALU.mult).then_inc(evacuated, 1)
                    dve.wait_ge(evacuated, n + 1)
                    if not early(n, 2):
                        dve.wait_ge(stored[u], j * 16)
                    dve.tensor_copy(parts[:, u, 0, :], full[:, u, :]).then_inc(hi_ready, 1)
                    dve.wait_ge(hi_ready, n + 1)
                    dve.tensor_tensor(rest[:, u, :], full[:, u, :], parts[:, u, 0, :],
                                      ALU.subtract).then_inc(rest_ready, 1)
                    dve.wait_ge(rest_ready, n + 1)
                    dve.tensor_copy(parts[:, u, 1, :], rest[:, u, :]).then_inc(mid_ready, 1)
                    dve.wait_ge(mid_ready, n + 1)
                    dve.tensor_tensor(rest2[:, u, :], rest[:, u, :], parts[:, u, 1, :],
                                      ALU.subtract).then_inc(rest2_ready, 1)
                    dve.wait_ge(rest2_ready, n + 1)
                    dve.tensor_copy(parts[:, u, 2, :], rest2[:, u, :]).then_inc(lo_ready, 1)
                over_pairs(dve, B, unit)


def value_stage(nc, name, XT, w, bias, dst):
    wcols = 2 * P
    with Stage(nc, name) as st:
        w_sb = st.sb("w", [P, P])
        b_sb = st.sb("b", [P, P])
        xs = st.sb("xs", [P, 2, 2, P])
        vt = st.sb("vt", [P, 2, 2, P])
        vp = st.ps("vp", [P, 2, 512])
        loaded = st.sem("loaded")
        x_copied = st.sem("x_copied")
        projected = st.sem("projected")
        biased = st.sem("biased")
        stored = [st.sem("stored0"), st.sem("stored1")]

        with st.block() as block:
            @block.sync
            def _(sp):
                sp.dma_start(w_sb[:, :], w[:, wcols:wcols + P]).then_inc(loaded, 16)
                sp.dma_start(b_sb[:, :], bias[wcols:wcols + P].partition_broadcast(P)).then_inc(loaded, 16)

                def unit(n, u, j):
                    sp.wait_ge(biased, n + 1)
                    for s in range(2):
                        sp.dma_start(dst[bass.ds(n, 1), :, s * P:(s + 1) * P, :].rearrange("a g p c -> (a p) g c"),
                                     vt[:, u, s, :].rearrange("p (g c) -> p g c", g=H // HG)).then_inc(stored[u], 16)
                over_pairs(sp, B, unit)
                sp.wait_ge(stored[0], 16 * B)
                sp.wait_ge(stored[1], 16 * B)

            @block.scalar
            def _(act):
                def unit(n, u, j):
                    if not early(n, 2):
                        act.wait_ge(projected, n - 1)
                    act.activation(xs[:, u, :, :].rearrange("p s t -> p (s t)"), XT[:, bass.ds(n * L, L)],
                                   ACT.Copy).then_inc(x_copied, 1)
                over_pairs(act, B, unit)

            @block.tensor
            def _(pe):
                pe.wait_ge(loaded, 32)

                def unit(n, u, j):
                    pe.wait_ge(x_copied, n + 1)
                    if not early(n, 2):
                        pe.wait_ge(biased, n - 1)
                    for s in range(2):
                        ins = pe.matmul(vp[:, u, s * P:(s + 1) * P], xs[:, u, s, :], w_sb[:, :], start=True, stop=True)
                    ins.then_inc(projected, 1)
                over_pairs(pe, B, unit)

            @block.vector
            def _(dve):
                dve.wait_ge(loaded, 32)

                def unit(n, u, j):
                    dve.wait_ge(projected, n + 1)
                    if not early(n, 2):
                        dve.wait_ge(stored[u], j * 32)
                    dve.tensor_tensor(vt[:, u, :, :], vp[:, u, 0:2 * P].rearrange("p (s t) -> p s t", s=2),
                                      b_sb[:, :].unsqueeze(1).to_broadcast([P, 2, P]),
                                      ALU.add).then_inc(biased, 1)
                over_pairs(dve, B, unit)


def context_stage(nc, name, ctx_in, ident, wk, bk, wv, bv, k_dst, v_dst):
    KT = -(-LC // P)
    TAIL = LC - (KT - 1) * P
    QUADS = [(q * 4, min(4, KT - q * 4)) for q in range(-(-KT // 4))]
    NQ = len(QUADS)
    with Stage(nc, name) as st:
        wk_in = st.sb("wk_in", [DC, P])
        wk_sb = st.sb("wk", [DC, P])
        bk_sb = st.sb("bk", [P, 1])
        wv_sb = st.sb("wv", [DC, P])
        bv_sb = st.sb("bv", [P, P])
        cin = st.sb("cin", [P, 2, KT, DC])
        cT = st.sb("cT", [DC, 2, KT * P])
        full = st.sb("full", [P, 2, LC])
        rest = st.sb("rest", [P, 2, LC])
        parts = st.sb("parts", [P, 2, 3, LC], BF16)
        vt = st.sb("vt", [P, 2, KT, P])
        tp = st.ps("tp", [P, 2, 512])
        kp = st.ps("kp", [P, 2, 512])
        vp = st.ps("vp", [P, 2, 512])
        loaded = st.sem("loaded")
        w_sorted = st.sem("w_sorted")
        cin_loaded = [st.sem("cin_loaded0"), st.sem("cin_loaded1")]
        turned = st.sem("turned")
        cT_ready = st.sem("cT_ready")
        k_projected = st.sem("k_projected")
        k_biased = st.sem("k_biased")
        v_projected = st.sem("v_projected")
        v_biased = st.sem("v_biased")
        hi_ready = st.sem("hi_ready")
        rest_ready = st.sem("rest_ready")
        mid_ready = st.sem("mid_ready")
        rest2_ready = st.sem("rest2_ready")
        lo_ready = st.sem("lo_ready")
        k_stored = [st.sem("k_stored0"), st.sem("k_stored1")]
        v_stored = [st.sem("v_stored0"), st.sem("v_stored1")]

        def keys_of(q):
            t0, n = QUADS[q]
            return t0 * P, min(LC, (t0 + n) * P)

        with st.block() as block:
            @block.sync
            def _(sp):
                sp.dma_start(wk_in[:, :], wk).then_inc(loaded, 16)
                with nc.allow_non_contiguous_dma(reason="one bias for each partition"):
                    sp.dma_start(bk_sb[:, :], by_dimension(bk)).then_inc(loaded, 16)
                sp.dma_start(wv_sb[:, :], wv).then_inc(loaded, 16)
                sp.dma_start(bv_sb[:, :], bv.partition_broadcast(P)).then_inc(loaded, 16)

                def store(n, u):
                    sp.wait_ge(lo_ready, n + 1)
                    sp.dma_start(k_dst[bass.ds(n, 1), :, :, :].rearrange("a c p t -> (a p) c t"),
                                 parts[:, u, :, :]).then_inc(k_stored[u], 16)
                    sp.wait_ge(v_biased, (n + 1) * NQ)
                    for t in range(KT):
                        rows = P if t < KT - 1 else TAIL
                        sp.dma_start(v_dst[bass.ds(n, 1), :, t * P:t * P + rows, :].rearrange("a g p c -> (a p) g c"),
                                     vt[0:rows, u, t, :].rearrange("p (g c) -> p g c", g=H // HG)
                                     ).then_inc(v_stored[u], 16)

                def unit(n, u, j):
                    if not early(n, 2):
                        sp.wait_ge(turned, (n - 1) * NQ)
                    whole = (KT - 1) * P
                    sp.dma_start(cin[:, u, 0:KT - 1, :],
                                 ctx_in[bass.ds(n, 1), 0:whole, :].rearrange("a (k p) d -> p (a k) d", p=P)
                                 ).then_inc(cin_loaded[u], 16)
                    sp.dma_start(cin[0:TAIL, u, KT - 1, :],
                                 ctx_in[bass.ds(n, 1), whole:LC, :].rearrange("a p d -> (a p) d")
                                 ).then_inc(cin_loaded[u], 16)
                    if not early(n, 2):
                        store(n - 2, u)
                over_pairs(sp, B, unit)
                store(B - 2, 0)
                store(B - 1, 1)
                for u in range(2):
                    sp.wait_ge(k_stored[u], 16 * B // 2)
                    sp.wait_ge(v_stored[u], 16 * KT * B // 2)

            @block.gpsimd
            def _(pool):
                def unit(n, u, j):
                    pool.wait_ge(hi_ready, n + 1)
                    if not early(n, 2):
                        pool.wait_ge(rest2_ready, n - 1)
                        pool.wait_ge(lo_ready, n - 1)
                    pool.tensor_tensor(rest[:, u, :], full[:, u, :], parts[:, u, 0, :],
                                       ALU.subtract).then_inc(rest_ready, 1)
                    pool.wait_ge(mid_ready, n + 1)
                    pool.tensor_tensor(full[:, u, :], rest[:, u, :], parts[:, u, 1, :],
                                       ALU.subtract).then_inc(rest2_ready, 1)
                over_pairs(pool, B, unit)

            @block.tensor
            def _(pe):
                pe.wait_ge(loaded, 64)
                pe.wait_ge(w_sorted, 1)

                def unit(n, u, j):
                    pe.wait_ge(cin_loaded[u], (j + 1) * 32)
                    for q, (t0, count) in enumerate(QUADS):
                        if not (early(n, 1) and q < 2):
                            pe.wait_ge(cT_ready, n * NQ + q - 1)
                        for t in range(t0, t0 + count):
                            rows = P if t < KT - 1 else TAIL
                            ins = pe.transpose(tp[0:DC, q % 2, (t - t0) * P:(t - t0) * P + rows],
                                               cin[0:rows, u, t, :], ident[0:rows, 0:rows])
                        ins.then_inc(turned, 1)
                    for q, (t0, count) in enumerate(QUADS):
                        a, b = keys_of(q)
                        pe.wait_ge(cT_ready, n * NQ + q + 1)
                        if not (early(n, 1) and q < 2):
                            pe.wait_ge(k_biased, n * NQ + q - 1)
                        pe.matmul(kp[:, q % 2, 0:b - a], wk_sb[:, :], cT[:, u, a:b],
                                  start=True, stop=True).then_inc(k_projected, 1)
                        if not (early(n, 1) and q < 2):
                            pe.wait_ge(v_biased, n * NQ + q - 1)
                        for t in range(t0, t0 + count):
                            rows = P if t < KT - 1 else TAIL
                            ins = pe.matmul(vp[0:rows, q % 2, (t - t0) * P:(t - t0 + 1) * P],
                                            cT[:, u, t * P:t * P + rows], wv_sb[:, :], start=True, stop=True)
                        ins.then_inc(v_projected, 1)
                over_pairs(pe, B, unit)

            @block.scalar
            def _(act):
                def turn(n, u, q):
                    if q == 0 and not early(n, 2):
                        act.wait_ge(v_projected, (n - 1) * NQ)
                    a, b = keys_of(q)
                    act.wait_ge(turned, n * NQ + q + 1)
                    act.activation(cT[:, u, a:b], tp[0:DC, q % 2, 0:b - a], ACT.Copy).then_inc(cT_ready, 1)

                def split(n, u, j, part):
                    if part == 0:
                        act.wait_ge(k_biased, (n + 1) * NQ)
                        if not early(n, 2):
                            act.wait_ge(k_stored[u], j * 16)
                        act.activation(parts[:, u, 0, :], full[:, u, :], ACT.Copy).then_inc(hi_ready, 1)
                    elif part == 1:
                        act.wait_ge(rest_ready, n + 1)
                        act.activation(parts[:, u, 1, :], rest[:, u, :], ACT.Copy).then_inc(mid_ready, 1)
                    else:
                        act.wait_ge(rest2_ready, n + 1)
                        act.activation(parts[:, u, 2, :], full[:, u, :], ACT.Copy).then_inc(lo_ready, 1)

                def unit(n, u, j):
                    for q in range(max(NQ, 3)):
                        if q < NQ and not (isinstance(n, int) and n == B - 1):
                            turn(n + 1, 1 - u, q)
                        if q < 3:
                            split(n, u, j, q)
                for q in range(NQ):
                    turn(0, 0, q)
                over_pairs(act, B, unit)

            @block.vector
            def _(dve):
                dve.wait_ge(loaded, 64)
                dve.tensor_copy(wk_sb[:, :].rearrange("p (d h) -> p d h", d=HD),
                                wk_in[:, :].rearrange("p (h d) -> p d h", d=HD)).then_inc(w_sorted, 1)

                def unit(n, u, j):
                    if not early(n, 2):
                        dve.wait_ge(lo_ready, n - 1)
                        dve.wait_ge(v_stored[u], j * 16 * KT)
                    for q, (t0, count) in enumerate(QUADS):
                        a, b = keys_of(q)
                        dve.wait_ge(k_projected, n * NQ + q + 1)
                        dve.tensor_scalar(full[:, u, a:b], kp[:, q % 2, 0:b - a], bk_sb[:, 0:1], None,
                                          ALU.add).then_inc(k_biased, 1)
                        dve.wait_ge(v_projected, n * NQ + q + 1)
                        rows = TAIL if t0 == KT - 1 else P
                        dve.tensor_tensor(vt[0:rows, u, t0:t0 + count, :],
                                          vp[0:rows, q % 2, 0:count * P].rearrange("p (s t) -> p s t", s=count),
                                          bv_sb[0:rows, :].unsqueeze(1).to_broadcast([rows, count, P]),
                                          ALU.add).then_inc(v_biased, 1)
                over_pairs(dve, B, unit)


def attention_stage(nc, name, q_parts, k_parts, v_units, y_units, ident, keys, groups, causal=False, clip=False):
    K_LOADS = [(0, 3), (0, 2), (0, 1)]
    Q_LOADS = [(0, 3), (1, 2), (2, 1)]
    PAIRS = [(0, 0), (1, 0), (2, 0), (0, 1), (1, 1), (0, 2)]
    MROW = 96
    KR = MROW + 3
    KT = -(-keys // P)
    PIECES = -(-keys // 512)
    QW = -(-keys // PIECES)
    NHD = HG * groups
    NM = NHD * 2
    BOTH = keys * 2 <= 512
    NC = groups * KT
    NA = NHD * PIECES * (1 if BOTH else 2)
    NV = 32
    LOADS = 4
    M_SLOT = NC - (4 if clip or causal else 5)
    N_UNITS = UNITS // groups
    RING = 2
    assert N_UNITS * groups == UNITS
    BIG_A, BIG_B = -80.0, 125.0
    assert BIG_A * BIG_B == NEG

    with Stage(nc, name) as st:
        K = st.sb("K", [KR, LOADS, NHD, keys], BF16)
        Q = st.sb("Q", [KR, LOADS, NHD, L], BF16)
        V = st.sb("V", [P, LOADS, groups, KT, HG * HD])
        VG = st.sb("VG", [P, 2, groups, KT, HG, NV])
        prob = st.sb("prob", [P, RING, HG, L])
        pmax = st.sb("pmax", [P, 2, NM, PIECES])
        negm = st.sb("negm", [P, 2, NM])
        mfull = st.sb("mfull", [NM, 2, P])
        mrest = st.sb("mrest", [NM, 2, P])
        mrest2 = st.sb("mrest2", [NM, 2, P])
        mparts = st.sb("mparts", [NM, 2, 3, P], BF16)
        osb = st.sb("osb", [P, 2, L])
        rsum = st.sb("rsum", [P, 2, 2, HG])
        yout = st.sb("yout", [P, 2, 2, HG, HD])
        if causal:
            maskA = st.sb("maskA", [P, 2, L], BF16)
            maskB = st.sb("maskB", [P, 2, L], BF16)
            scaled = st.sb("scaled", [P, P], BF16)
        if clip:
            raised = st.sb("raised", [P, 2, HG, L])
            floor = st.sb("floor", [P, 1])

            pick = st.sb("pick", [KR, P], BF16)
            low = st.sb("low", [P, 2, HG, L])
        sa = st.ps("sa", [P, 2, 512])
        sb_ = st.ps("sb", [P, 2, HG, L])
        pv = st.ps("pv", [P, L])
        misc = st.ps("misc", [P, 512])

        K_loaded = [st.sem(f"K_loaded{v}") for v in range(LOADS)]
        m_loaded = [st.sem("m_loaded0"), st.sem("m_loaded1")]
        V_loaded = [st.sem(f"V_loaded{v}") for v in range(LOADS)]
        zeroed = st.sem("zeroed")
        ones_set = st.sem("ones_set")
        masks_ready = st.sem("masks_ready")
        VG_ready = st.sem("VG_ready")
        a_scored = st.sem("a_scored")
        a_reduced = st.sem("a_reduced")
        negm_ready = st.sem("negm_ready")
        m_turned = st.sem("m_turned")
        m_copied = st.sem("m_copied")
        m_step = st.sem("m_step")
        mparts_ready = st.sem("mparts_ready")
        b_scored = st.sem("b_scored")
        b_clipped = st.sem("b_clipped")
        b_exp = st.sem("b_exp")
        b_used = st.sem("b_used")
        low_spread = st.sem("low_spread")
        low_ready = st.sem("low_ready")
        o_copied = st.sem("o_copied")
        o_turned = st.sem("o_turned")
        r_ready = st.sem("r_ready")
        y_ready = st.sem("y_ready")
        y_stored = [st.sem("y_stored0"), st.sem("y_stored1")]

        K_DMAS = 2 * len(K_LOADS)
        V_DMAS = groups * (2 if keys % P else 1)

        def c0(u, c):
            return (u * NC + c) % 2

        def c3(u, c):
            return (u * NC + c) % RING

        def chunk_of(c):
            g, t = divmod(c, KT)
            return g, t, min(P, keys - t * P)

        def piece_of(i):
            hq, k = divmod(i, PIECES)
            h, tiles = (hq, (0, 1)) if BOTH else (hq // 2, (hq % 2,))
            return h, tiles, k * QW, min(keys, (k + 1) * QW), k

        def slots(c):
            return range(NA * c // M_SLOT, NA * (c + 1) // M_SLOT) if c < M_SLOT else range(0)

        def par(u, g):
            return g % 2 if groups > 1 else u

        def group_no(n, g):
            return n * groups + g

        def pairs(j, v):
            return j * 2 + v // 2

        def stored_before(j, u, g):
            return (2 * j + u) * (groups // 2) + g // 2 if groups > 1 else j

        with st.block() as block:
            @block.sync
            def _(sp):
                sp.wait_ge(zeroed, 3)
                vd = v_units.rearrange("b (y x) t c -> (b y) x t c", x=groups)

                def load(n, v, b, x):
                    kd = k_parts[bass.ds(b, 1)].rearrange("b c (d x g) t -> b c d x g t", d=HD, g=NHD)[:, :, :, x]
                    qd = q_parts[bass.ds(b, 1)].rearrange("b c (d x g) t -> b c d x g t", d=HD, g=NHD)[:, :, :, x]
                    if not early(n, LOADS):
                        sp.wait_ge(b_used, (n - LOADS + 1) * NC)
                        sp.wait_ge(VG_ready, n - LOADS + 1)
                    r = 0
                    for (first, count), (cq, _count) in zip(K_LOADS, Q_LOADS):
                        sp.dma_start(K[r * HD:(r + count) * HD, v, :, :],
                                     kd[:, first:first + count].rearrange("b c d g t -> (b c d) g t")
                                     ).then_inc(K_loaded[v], 16)
                        sp.dma_start(Q[r * HD:(r + count) * HD, v, :, :],
                                     qd[:, cq:cq + 1].rearrange("b c d g t -> (b c) d g t")
                                     .to_broadcast([count, HD, NHD, L])).then_inc(K_loaded[v], 16)
                        r += count
                    whole = keys // P
                    for g in range(groups):
                        sp.dma_start(V[:, v, g, 0:whole, :],
                                     vd[bass.ds(n, 1), g, 0:whole * P, :].rearrange("a (k p) c -> p (a k) c", p=P)
                                     ).then_inc(V_loaded[v], 16)
                        if keys % P:
                            sp.dma_start(V[0:keys % P, v, g, whole, :],
                                         vd[bass.ds(n, 1), g, whole * P:keys, :].rearrange("a p c -> (a p) c")
                                         ).then_inc(V_loaded[v], 16)
                def load_ahead(n, v, j):
                    if groups > 1:
                        load(n, v % LOADS, n, 0)
                    else:
                        load(n, v % LOADS, j + v // LOADS, v % LOADS)

                def put_maxima(n, v):
                    for c in range(3):
                        if c < 2:
                            sp.wait_ge(m_step, n * 4 + (2 * c + 1))
                        else:
                            sp.wait_ge(mparts_ready, n + 1)
                        sp.dma_start(Q[MROW + c:MROW + c + 1, v, :, :].rearrange("r g (s t) -> r (g s) t", s=2),
                                     mparts[:, v % 2, c, :]).then_inc(m_loaded[v % 2], 16)

                def put_y(gn, p):
                    sp.wait_ge(y_ready, gn + 1)
                    for s in range(2):
                        sp.dma_start(y_units[bass.ds(gn, 1), s * P:(s + 1) * P, :].rearrange("a p c -> (a p) c"),
                                     yout[:, p, s, :, :].rearrange("p g d -> p (g d)")).then_inc(y_stored[p], 16)

                for v in range(LOADS - 1):
                    load_ahead(v, v, 0)
                put_maxima(0, 0)

                def unit(n, v, j):
                    u = v % 2
                    if not (isinstance(n, int) and n + LOADS - 1 >= N_UNITS):
                        load_ahead(n + LOADS - 1, v + LOADS - 1, j)
                    for c in range(NC):
                        g = c // KT
                        if c % KT == 1 and not early(group_no(n, g), 1):
                            put_y(group_no(n, g) - 1, (g - 1) % 2 if groups > 1 else 1 - u)
                        if c == M_SLOT and not (isinstance(n, int) and n == N_UNITS - 1):
                            put_maxima(n + 1, (v + 1) % LOADS)
                over_fours(sp, N_UNITS, unit)
                put_y(UNITS - 1, 1)
                sp.wait_ge(y_stored[0], UNITS // 2 * 32)
                sp.wait_ge(y_stored[1], UNITS // 2 * 32)

            @block.gpsimd
            def _(pool):
                pool.memset(K[:, :, :, :], 1.0).then_inc(zeroed, 1)
                pool.memset(Q[:, :, :, :], 0.0).then_inc(zeroed, 1)
                pool.memset(V[:, :, :, :, :], 0.0).then_inc(zeroed, 1)
                pool.memset(VG[:, :, :, :, :, :], 0.0).then_inc(ones_set, 1)
                pool.wait_ge(ones_set, 1)
                pool.memset(VG[:, :, :, :, :, HD:HD + 1], 1.0).then_inc(ones_set, 1)
                if causal:
                    pool.memset(maskA[:, :, :], 0.0).then_inc(masks_ready, 1)
                    pool.memset(maskB[:, :, :], 0.0).then_inc(masks_ready, 1)
                    pool.memset(scaled[:, :], 0.0).then_inc(masks_ready, 1)
                    pool.wait_ge(masks_ready, 3)
                    pool.affine_select(out=scaled[:, :], in_=scaled[:, :], compare_op=ALU.not_equal, fill=BIG_A,
                                       base=0, pattern=[[-1, P]], channel_multiplier=1).then_inc(masks_ready, 1)
                    for s in range(2):
                        pool.affine_select(out=maskA[:, s, :], in_=maskA[:, s, :], compare_op=ALU.is_ge, fill=BIG_B,
                                           base=s * P, pattern=[[-1, L]], channel_multiplier=1).then_inc(masks_ready, 1)
                        pool.affine_select(out=maskB[:, s, :], in_=maskB[:, s, :], compare_op=ALU.is_ge, fill=BIG_B,
                                           base=-s * P, pattern=[[1, L]], channel_multiplier=-1).then_inc(masks_ready, 1)
                if clip:
                    pool.memset(pick[:, :], 1.0).then_inc(masks_ready, 1)
                    pool.wait_ge(masks_ready, 1)
                    pool.affine_select(out=pick[:, :], in_=pick[:, :], compare_op=ALU.is_ge, fill=0.0,
                                       base=-MROW, pattern=[[0, P]], channel_multiplier=1).then_inc(masks_ready, 1)
                    pool.memset(floor[:, :], -CLAMP).then_inc(masks_ready, 1)

            @block.tensor
            def _(pe):
                def a_piece(n, v, i, loads):
                    h, tiles, a, b, k = piece_of(i)
                    w = b - a
                    if i == 0:
                        pe.wait_ge(K_loaded[v], loads * 16 * K_DMAS)
                    if clip and i == 0 and not early(n, 1):
                        pe.wait_ge(low_ready, n)
                    elif not (early(n, 1) and i < 2):
                        pe.wait_ge(a_reduced, n * NA + (i - 1))
                    if causal:
                        pe.matmul(sa[:, i % 2, :], scaled[:, :], maskA[:, :, :].rearrange("p s t -> p (s t)"),
                                  start=True, stop=False, skip_group_check=True)
                    for x, s in enumerate(tiles):
                        ins = pe.matmul(sa[:, i % 2, x * w:(x + 1) * w], Q[0:MROW, v, h, s * P:(s + 1) * P],
                                        K[0:MROW, v, h, a:b], start=not causal, stop=True, skip_group_check=True)
                    ins.then_inc(a_scored, 1)

                def m_turn(n, u):
                    pe.wait_ge(negm_ready, n + 1)
                    if not early(n, 1):
                        pe.wait_ge(m_copied, n)
                        if groups > 1 or not early(n, 2):
                            pe.wait_ge(y_ready, group_no(n - 1, (M_SLOT - 1) // KT))
                    pe.transpose(misc[0:NM, 256:256 + P], negm[:, u, :], ident[:, :]).then_inc(m_turned, 1)

                def b_scores(n, v, c):
                    u = v % 2
                    g, t, r = chunk_of(c)
                    if not (early(n, 1) and c < 2):
                        pe.wait_ge(b_exp, n * NC + (c - 1))
                    if causal:
                        for x in range(2):
                            pe.matmul(sb_[:, c0(u, c), 2 * x:2 * x + 2, :], scaled[:, :],
                                      maskB[:, t, :].unsqueeze(1).to_broadcast([P, 2, L]),
                                      start=True, stop=False, skip_group_check=True)
                    for x in range(HG):
                        ins = pe.matmul(sb_[0:r, c0(u, c), x, :], K[:, v, g * HG + x, t * P:t * P + r],
                                        Q[:, v, g * HG + x, :], start=not causal, stop=True, skip_group_check=True)
                    ins.then_inc(b_scored, 1)

                def b_values(n, u, c):
                    g, t, r = chunk_of(c)
                    if c == 0:
                        pe.wait_ge(VG_ready, n + 1)
                    if t == 0 and not early(group_no(n, g), 1):
                        pe.wait_ge(o_copied, group_no(n, g))
                    pe.wait_ge(b_clipped if clip else b_exp, n * NC + (c + 1))
                    for x in range(HG):
                        ins = pe.matmul(pv[x * NV:(x + 1) * NV, :], VG[0:r, u, g, t, x, :],
                                        prob[0:r, c3(u, c), x, :], start=(t == 0), stop=(t == KT - 1),
                                        tile_position=(0, x * NV), skip_group_check=True)
                    ins.then_inc(b_used, 1)

                def o_turn(gn, p, maxima):
                    pe.wait_ge(o_copied, gn + 1)
                    pe.wait_ge(m_copied, maxima)
                    if not early(gn, 1):
                        pe.wait_ge(y_ready, gn)
                    for s in range(2):
                        ins = pe.transpose(misc[:, s * P:(s + 1) * P], osb[:, p, s * P:(s + 1) * P], ident[:, :])
                    ins.then_inc(o_turned, 1)

                def spread_maxima(n, v):
                    pe.wait_ge(a_reduced, (n + 1) * NA)
                    for x in range(2):
                        pe.matmul(sa[:, x, :], pick[:, :], Q[:, v, 2 * x:2 * x + 2, :].rearrange("r g t -> r (g t)"),
                                  start=True, stop=True).then_inc(low_spread, 1)

                pe.wait_ge(zeroed, 3)
                if causal or clip:
                    pe.wait_ge(masks_ready, 8 if causal else 3)
                for i in range(NA):
                    a_piece(0, 0, i, 1)
                m_turn(0, 0)
                pe.wait_ge(m_loaded[0], 48)
                if clip:
                    spread_maxima(0, 0)
                b_scores(0, 0, 0)
                b_scores(0, 0, 1)

                def unit(n, v, j):
                    u, after = v % 2, (v + 1) % LOADS
                    last = isinstance(n, int) and n == N_UNITS - 1
                    for c in range(NC):
                        if c % KT == 1 and not early(group_no(n, c // KT), 1):
                            g = c // KT
                            o_turn(group_no(n, g) - 1, par(u, g - 1) if groups > 1 else 1 - u,
                                   n + 2 if c > M_SLOT and not last else n + 1)
                        pieces = [] if last else list(slots(c))
                        for i in pieces[:2]:
                            a_piece(n + 1, after, i, j + 1 + (v + 1) // LOADS)
                        b_values(n, u, c)
                        for i in pieces[2:3]:
                            a_piece(n + 1, after, i, j + 1 + (v + 1) // LOADS)
                        if c == M_SLOT and not last:
                            m_turn(n + 1, 1 - u)
                        if c + 2 < NC:
                            b_scores(n, v, c + 2)
                        elif not last:
                            if c + 2 == NC:
                                pe.wait_ge(m_loaded[1 - u], pairs(j, v + 1) * 48 + 48)
                            b_scores(n + 1, after, c + 2 - NC)
                            if clip and c + 2 == NC:
                                spread_maxima(n + 1, after)
                        for i in pieces[3:]:
                            a_piece(n + 1, after, i, j + 1 + (v + 1) // LOADS)
                over_fours(pe, N_UNITS, unit)
                o_turn(UNITS - 1, 1, N_UNITS)

            @block.vector
            def _(dve):
                def a_reduce(n, u, i):
                    h, tiles, a, b, k = piece_of(i)
                    m = len(tiles)
                    dve.wait_ge(a_scored, n * NA + (i + 1))
                    dve.tensor_reduce(pmax[:, u, 2 * h + tiles[0]:2 * h + tiles[0] + m, k:k + 1]
                                      .rearrange("p m a -> p (m a)"),
                                      sa[:, i % 2, 0:m * (b - a)].rearrange("p (m w) -> p m w", m=m),
                                      AX.X, ALU.max).then_inc(a_reduced, 1)

                def m_find(n, u):
                    dve.wait_ge(a_reduced, (n + 1) * NA)
                    if not early(n, 2):
                        dve.wait_ge(m_turned, n - 1)
                    dve.tensor_reduce(negm[:, u, :], pmax[:, u, :, :], AX.X, ALU.max, negate=True
                                      ).then_inc(negm_ready, 1)

                def m_split(n, u, stored):
                    dve.wait_ge(m_turned, n + 1)
                    if clip:
                        dve.tensor_scalar(mfull[:, u, :], misc[0:NM, 256:256 + P], CLAMP, -CLAMP, ALU.min, ALU.max
                                          ).then_inc(m_copied, 1)
                    else:
                        dve.tensor_copy(mfull[:, u, :], misc[0:NM, 256:256 + P]).then_inc(m_copied, 1)
                    dve.wait_ge(m_copied, n + 1)
                    if stored is not None:
                        dve.wait_ge(m_loaded[u], stored)
                    dve.tensor_copy(mparts[:, u, 0, :], mfull[:, u, :]).then_inc(m_step, 1)
                    dve.wait_ge(m_step, n * 4 + 1)
                    dve.tensor_tensor(mrest[:, u, :], mfull[:, u, :], mparts[:, u, 0, :], ALU.subtract).then_inc(m_step, 1)
                    dve.wait_ge(m_step, n * 4 + 2)
                    dve.tensor_copy(mparts[:, u, 1, :], mrest[:, u, :]).then_inc(m_step, 1)
                    dve.wait_ge(m_step, n * 4 + 3)
                    dve.tensor_tensor(mrest2[:, u, :], mrest[:, u, :], mparts[:, u, 1, :], ALU.subtract).then_inc(m_step, 1)
                    dve.wait_ge(m_step, n * 4 + 4)
                    dve.tensor_copy(mparts[:, u, 2, :], mrest2[:, u, :]).then_inc(mparts_ready, 1)

                def b_clip(n, u, c):
                    g, t, r = chunk_of(c)
                    dve.wait_ge(b_exp, n * NC + (c + 1))
                    if c == 0:
                        dve.wait_ge(low_ready, n + 1)
                    if not (early(n, 1) and c < RING):
                        dve.wait_ge(b_used, n * NC + (c - RING + 1))
                    dve.scalar_tensor_tensor(prob[0:r, c3(u, c), :, :], raised[0:r, c0(u, c), :, :], 1.0,
                                             low[0:r, u, :, :], ALU.min, ALU.max).then_inc(b_clipped, 1)

                def o_copy(n, u, g):
                    gn = group_no(n, g)
                    dve.wait_ge(b_used, n * NC + (g + 1) * KT)
                    if not early(gn, 2):
                        dve.wait_ge(o_turned, gn - 1)
                    p = par(u, g)
                    dve.tensor_copy(osb[:, p, :], pv[:, :]).then_inc(o_copied, 1)

                def o_norm(gn, p, stored):
                    dve.wait_ge(o_turned, gn + 1)
                    o = misc[:, 0:2 * P].rearrange("p (s g c) -> p s g c", s=2, g=HG)
                    dve.reciprocal(rsum[:, p, :, :], o[:, :, :, HD]).then_inc(r_ready, 1)
                    dve.wait_ge(r_ready, gn + 1)
                    if stored is not None:
                        dve.wait_ge(y_stored[p], stored)
                    dve.tensor_tensor(yout[:, p, :, :, :], o[:, :, :, 0:HD],
                                      rsum[:, p, :, :].unsqueeze(3).to_broadcast([P, 2, HG, HD]),
                                      ALU.mult).then_inc(y_ready, 1)

                def norm_before(n, u, j, g):
                    gn = group_no(n, g)
                    if early(gn, 1):
                        return
                    if groups > 1:
                        p = (g - 1) % 2
                        if g == 0:
                            count = stored_before(j, u, 0) - 1
                        else:
                            count = stored_before(j, u, g - 1)
                    else:
                        p = 1 - u
                        count = j - 1 + u
                    o_norm(gn - 1, p, None if early(gn, 3) else count * 32)

                for i in range(NA):
                    a_reduce(0, 0, i)
                m_find(0, 0)
                m_split(0, 0, None)
                if clip:
                    b_clip(0, 0, 0)
                def unit(n, u, j):
                    last = isinstance(n, int) and n == N_UNITS - 1
                    for c in range(NC):
                        if c % KT == 0 and c > 0:
                            o_copy(n, u, c // KT - 1)
                        if c % KT == 1:
                            norm_before(n, u, j, c // KT)
                        if not last:
                            for i in list(slots(c))[:2]:
                                a_reduce(n + 1, 1 - u, i)
                        if clip and c + 1 < NC:
                            b_clip(n, u, c + 1)
                        elif clip and not last:
                            b_clip(n + 1, 1 - u, 0)
                        if not last:
                            for i in list(slots(c))[2:]:
                                a_reduce(n + 1, 1 - u, i)
                            if c == M_SLOT:
                                m_find(n + 1, 1 - u)
                                m_split(n + 1, 1 - u, None if early(n, 1) else (j + u) * 48)
                    o_copy(n, u, groups - 1)
                over_pairs(dve, N_UNITS, unit)
                o_norm(UNITS - 1, 1, (UNITS // 2 - 1) * 32)

            @block.scalar
            def _(act):
                def spread_values(n, v, loads):
                    act.wait_ge(V_loaded[v], loads * 16 * V_DMAS)
                    if not early(n, 2):
                        act.wait_ge(b_used, (n - 1) * NC)
                    act.activation(VG[:, v % 2, :, :, :, 0:HD].rearrange("p y k g d -> p (y k) g d"),
                                   V[:, v, :, :, :].rearrange("p y k (g d) -> p (y k) g d", g=HG), ACT.Copy
                                   ).then_inc(VG_ready, 1)

                def put_low(n, u):
                    act.wait_ge(low_spread, (n + 1) * 2)
                    if not early(n, 2):
                        act.wait_ge(b_clipped, (n - 1) * NC)
                    for x in range(2):
                        ins = act.activation(low[:, u, 2 * x:2 * x + 2, :].rearrange("p g t -> p (g t)"),
                                             sa[:, x, :], ACT.Exp, bias=floor[:, 0:1])
                    ins.then_inc(low_ready, 1)

                act.wait_ge(ones_set, 2)
                spread_values(0, 0, 1)
                if clip:
                    act.wait_ge(masks_ready, 3)
                    put_low(0, 0)

                def unit(n, v, j):
                    u = v % 2
                    last = isinstance(n, int) and n == N_UNITS - 1
                    for c in range(NC):
                        g, t, r = chunk_of(c)
                        act.wait_ge(b_scored, n * NC + (c + 1))
                        dst = raised if clip else prob
                        if not (early(n, 1) and c < 2):
                            act.wait_ge(b_clipped if clip else b_used, n * NC + (c - 1))
                        act.activation(dst[0:r, c0(u, c), :, :], sb_[0:r, c0(u, c), :, :], ACT.Exp).then_inc(b_exp, 1)
                        if c == 2 and not last:
                            spread_values(n + 1, (v + 1) % LOADS, j + 1 + (v + 1) // LOADS)
                    if clip and not last:
                        put_low(n + 1, 1 - u)
                over_fours(act, N_UNITS, unit)


def out_stage(nc, name, X, ident, y_units, wo, bo):
    with Stage(nc, name) as st:
        w_sb = st.sb("w", [P, P])
        b_sb = st.sb("b", [P, P])
        y = st.sb("y", [P, 2, P])
        yT = st.sb("yT", [P, 2, P])
        new = st.sb("new", [P, 2, P])
        tp = st.ps("tp", [P, 2, 512])
        op = st.ps("op", [P, 2, 512])
        loaded = st.sem("loaded")
        y_loaded = [st.sem("y_loaded0"), st.sem("y_loaded1")]
        turned = st.sem("turned")
        yT_ready = st.sem("yT_ready")
        projected = st.sem("projected")
        biased = st.sem("biased")
        added = st.sem("added")

        with st.block() as block:
            @block.sync
            def _(sp):
                sp.dma_start(w_sb[:, :], wo).then_inc(loaded, 16)
                sp.dma_start(b_sb[:, :], bo.partition_broadcast(P)).then_inc(loaded, 16)

                def unit(n, u, j):
                    if not early(n, 2):
                        sp.wait_ge(turned, n - 1)
                    yb = y_units.rearrange("(b x) t c -> b x t c", x=H // HG)
                    sp.dma_start(y[:, u, :].rearrange("p (x c) -> p x c", x=H // HG),
                                 yb[bass.ds(j, 1), :, u * P:(u + 1) * P, :].rearrange("b x p c -> (b p) x c")
                                 ).then_inc(y_loaded[u], 16)
                over_pairs(sp, TILES, unit)

            @block.tensor
            def _(pe):
                pe.wait_ge(loaded, 32)

                def unit(n, u, j):
                    pe.wait_ge(y_loaded[u], (j + 1) * 16)
                    if not early(n, 2):
                        pe.wait_ge(yT_ready, n - 1)
                    pe.transpose(tp[:, u, 0:P], y[:, u, :], ident[:, :]).then_inc(turned, 1)
                    pe.wait_ge(yT_ready, n + 1)
                    if not early(n, 2):
                        pe.wait_ge(biased, n - 1)
                    pe.matmul(op[:, u, 0:P], yT[:, u, :], w_sb[:, :], start=True, stop=True).then_inc(projected, 1)
                over_pairs(pe, TILES, unit)

            @block.scalar
            def _(act):
                def unit(n, u, j):
                    act.wait_ge(turned, n + 1)
                    if not early(n, 2):
                        act.wait_ge(projected, n - 1)
                    act.activation(yT[:, u, :], tp[:, u, 0:P], ACT.Copy).then_inc(yT_ready, 1)
                over_pairs(act, TILES, unit)

            @block.vector
            def _(dve):
                dve.wait_ge(loaded, 32)

                def unit(n, u, j):
                    dve.wait_ge(projected, n + 1)
                    if not early(n, 2):
                        dve.wait_ge(added, n - 1)
                    dve.tensor_tensor(new[:, u, :], op[:, u, 0:P], b_sb[:, :], ALU.add).then_inc(biased, 1)
                    dve.wait_ge(biased, n + 1)
                    xs = X[:, bass.ds(n, 1), :].rearrange("p a d -> p (a d)")
                    dve.tensor_tensor(xs, xs, new[:, u, :], ALU.add).then_inc(added, 1)
                over_pairs(dve, TILES, unit)


def cross(nc, name, X, ident, t, key, q_parts, k_ctx, v_ctx, y_units, clip):
    with nc.sbuf_tensor(f"{name}_XT", [P, NT], F32) as XT:
        norm_stage(nc, name + "n", X, XT, ident)
        scale = None if clip else t[f"{key}_scale"]
        project_stage(nc, name + "q", XT, t[f"{key}_Wq"], t[f"{key}_bq"], HD ** -0.5, q_parts, factor_dram=scale)
    context_stage(nc, name + "k", t["ctx_768"], ident, t[f"{key}_Wk"], t[f"{key}_bk"], t[f"{key}_Wv"],
                  t[f"{key}_bv"], k_ctx, v_ctx)
    attention_stage(nc, name + "a", q_parts, k_ctx, v_ctx, y_units, ident, LC, 1, clip=clip)
    out_stage(nc, name + "o", X, ident, y_units, t[f"{key}_Wo"], t[f"{key}_bo"])


def mix_stage(nc, name, X, XT, ident, t, y_units):
    RING = 4
    with Stage(nc, name) as st:
        wq = st.sb("wq", [P, P])
        wk = st.sb("wk", [P, P])
        wv = st.sb("wv", [P, P])
        wve = st.sb("wve", [P, HD, P])
        bq = st.sb("bq", [P, 1])
        bk = st.sb("bk", [P, 1])
        bve = st.sb("bve", [P, HD])
        gamma = st.sb("gamma", [P, HD])
        lam = st.sb("lam", [P, HD])
        retain = st.sb("retain", [P, HD])
        static = st.sb("static", [P, HD])
        bias_g = st.sb("bias_g", [P, HD])
        select = st.sb("select", [P, HD, P])
        same = st.sb("same", [P, P])
        gw1 = st.sb("gw1", [P, D // 2])
        gb1 = st.sb("gb1", [D // 2, 1])
        gw2 = st.sb("gw2", [D // 2, H])
        gw2e = st.sb("gw2e", [D // 2, P])
        gb2 = st.sb("gb2", [P, 1])
        wo = st.sb("wo", [P, P])
        bo = st.sb("bo", [P, P])
        qT = st.sb("qT", [P, 2, L])
        kT = st.sb("kT", [P, 2, L])
        gT = st.sb("gT", [D // 2, 2, L])
        alpha = st.sb("alpha", [P, 2, L])
        beta = st.sb("beta", [P, 2, L])
        vG = st.sb("vG", [P, RING, L])
        hebb = st.sb("hebb", [P, RING, L])
        state = st.sb("state", [P, RING, L])
        read = st.sb("read", [P, RING, L])
        y = st.sb("y", [P, 2, 2, P])
        soft = st.sb("soft", [P, 2, L])
        stp = st.sb("stp", [P, 2, L])
        mixed = st.sb("mixed", [P, 2, L])
        new = st.sb("new", [P, 2, 2, P])
        qk = st.ps("qk", [P, 2, L])
        gp = st.ps("gp", [P, 2, L])
        vp = st.ps("vp", [P, 2, 512])
        yp = st.ps("yp", [P, 2, 512])
        tp = st.ps("tp", [P, 2, P])
        op = st.ps("op", [P, 2, P])

        loaded = st.sem("loaded")
        built = st.sem("built")
        lam_squashed = st.sem("lam_squashed")
        y_loaded = [st.sem("y_loaded0"), st.sem("y_loaded1")]
        qk_projected = st.sem("qk_projected")
        q_ready = st.sem("q_ready")
        k_ready = st.sem("k_ready")
        g_projected = st.sem("g_projected")
        g_ready = st.sem("g_ready")
        a_projected = st.sem("a_projected")
        a_ready = st.sem("a_ready")
        v_projected = st.sem("v_projected")
        v_ready = st.sem("v_ready")
        hebb_ready = st.sem("hebb_ready")
        state_ready = st.sem("state_ready")
        read_ready = st.sem("read_ready")
        summed = st.sem("summed")
        y_turned = st.sem("y_turned")
        mix_step = st.sem("mix_step")
        mixed_ready = st.sem("mixed_ready")
        out_projected = st.sem("out_projected")
        biased = st.sem("biased")
        added = st.sem("added")

        with st.block() as block:
            @block.sync
            def _(sp):
                w = t["L0_attn_Wqkv_w"]
                b = t["L0_attn_Wqkv_b"]
                for dst, src in [
                        (wq[:, :], w[:, 0:P]), (wk[:, :], w[:, P:2 * P]), (wv[:, :], w[:, 2 * P:3 * P]),
                        (bq[:, :], column(b, 0)), (bk[:, :], column(b, P)),
                        (gw1[:, :], t["L0_attn_gate_w1"]), (gb1[:, :], column(t["L0_attn_gate_b1"], 0, D // 2)),
                        (gw2[:, :], t["L0_attn_gate_w2"]),
                        (wo[:, :], t["L0_attn_out_w"]), (bo[:, :], t["L0_attn_out_b"].partition_broadcast(P))]:
                    sp.dma_start(dst, src).then_inc(loaded, 16)
                for h in range(H):
                    rows = slice(h * HD, (h + 1) * HD)
                    for dst, src in ((gamma, t["L0_attn_Gamma"]), (lam, t["L0_attn_Lambda_raw"]),
                                     (static, t["L0_attn_W_static"])):
                        with nc.allow_non_contiguous_dma(reason="8 x 8 matrices, transposed"):
                            sp.dma_start(dst[rows, :], src[h].rearrange("i j -> j i")).then_inc(loaded, 16)
                    sp.dma_start(bve[rows, :], b[2 * P + h * HD:2 * P + (h + 1) * HD].partition_broadcast(HD)
                                 ).then_inc(loaded, 16)
                    sp.dma_start(gb2[rows, :], t["L0_attn_gate_b2"][h:h + 1].partition_broadcast(HD)
                                 ).then_inc(loaded, 16)

                def unit(n, u, j):
                    if not early(n, 2):
                        sp.wait_ge(y_turned, n - 1)
                    yb = y_units.rearrange("(b x) t c -> b x t c", x=H // HG)
                    for s in range(2):
                        sp.dma_start(y[:, u, s, :].rearrange("p (x c) -> p x c", x=H // HG),
                                     yb[bass.ds(n, 1), :, s * P:(s + 1) * P, :].rearrange("b x p c -> (b p) x c")
                                     ).then_inc(y_loaded[u], 16)
                over_pairs(sp, B, unit)

            LOADS = 16 * (10 + 5 * H)

            @block.gpsimd
            def _(pool):
                pool.memset(same[:, :], 1.0).then_inc(built, 1)
                pool.memset(select[:, :, :], 0.0).then_inc(built, 1)
                pool.wait_ge(built, 2)
                sv = same[:, :].rearrange("p (h c) -> p h c", h=H)
                pool.affine_select(out=sv, in_=sv, compare_op=ALU.is_ge, fill=0.0, base=0,
                                   pattern=[[-HD, H], [0, HD]], channel_multiplier=1).then_inc(built, 1)
                pool.wait_ge(built, 3)
                pool.affine_select(out=sv, in_=sv, compare_op=ALU.is_ge, fill=0.0, base=HD - 1,
                                   pattern=[[HD, H], [0, HD]], channel_multiplier=-1).then_inc(built, 1)
                pool.wait_ge(built, 4)
                for i in range(HD):
                    pool.tensor_copy(select[:, i, i:P:HD], same[:, i:P:HD]).then_inc(built, 1)

                def unit(n, u, j):
                    for i in range(HD):
                        pool.wait_ge(v_ready, n * HD + (i + 1))
                        if i == 0:
                            pool.wait_ge(k_ready, n + 1)
                        if not (early(n, 1) and i < RING):
                            pool.wait_ge(state_ready, n * HD + (i - RING + 1))
                        pool.tensor_tensor(hebb[:, i % RING, :], vG[:, i % RING, :], kT[:, u, :], ALU.mult
                                           ).then_inc(hebb_ready, 1)
                over_pairs(pool, B, unit)

            @block.tensor
            def _(pe):
                pe.wait_ge(loaded, LOADS)
                pe.wait_ge(built, 4 + HD)
                pe.wait_ge(mix_step, 5)

                def unit(n, u, j):
                    x = XT[:, bass.ds(n * L, L)]
                    if not early(n, 1):
                        pe.wait_ge(q_ready, n)
                        pe.wait_ge(k_ready, n)
                        pe.wait_ge(a_ready, n)
                    pe.matmul(qk[:, 0, :], wq[:, :], x, start=True, stop=True)
                    pe.matmul(qk[:, 1, :], wk[:, :], x, start=True, stop=True).then_inc(qk_projected, 1)
                    pe.matmul(gp[0:D // 2, 0, :], gw1[:, :], x, start=True, stop=True).then_inc(g_projected, 1)
                    for i in range(HD):
                        if not (early(n, 1) and i < 2):
                            pe.wait_ge(v_ready, n * HD + (i - 1))
                        pe.matmul(vp[:, i % 2, 0:L], wve[:, i, :], x, start=True, stop=True).then_inc(v_projected, 1)
                        if i == 1:
                            pe.wait_ge(g_ready, n + 1)
                            pe.matmul(gp[:, 1, :], gw2e[:, :], gT[:, u, :], start=True, stop=True
                                      ).then_inc(a_projected, 1)
                        if i >= RING - 1:
                            plasticity_sum(n, u, i - RING + 1)
                    for i in range(HD - RING + 1, HD):
                        plasticity_sum(n, u, i)
                    pe.wait_ge(y_loaded[u], (j + 1) * 32)
                    if not early(n, 1):
                        pe.wait_ge(mixed_ready, n)
                    for s in range(2):
                        ins = pe.transpose(tp[:, s, :], y[:, u, s, :], ident[:, :])
                    ins.then_inc(y_turned, 1)
                    pe.wait_ge(mixed_ready, n + 1)
                    if not early(n, 1):
                        pe.wait_ge(biased, n)
                    for s in range(2):
                        ins = pe.matmul(op[:, s, :], mixed[:, u, s * P:(s + 1) * P], wo[:, :], start=True, stop=True)
                    ins.then_inc(out_projected, 1)

                def plasticity_sum(n, u, i):
                    pe.wait_ge(read_ready, n * HD + (i + 1))
                    if i == 0 and not early(n, 2):
                        pe.wait_ge(mixed_ready, n - 1)
                    pe.matmul(yp[:, u, 0:L], select[:, i, :], read[:, i % RING, :], start=(i == 0), stop=(i == HD - 1)
                              ).then_inc(summed, 1)
                over_pairs(pe, B, unit)

            @block.scalar
            def _(act):
                act.wait_ge(loaded, LOADS)
                act.activation(retain[:, :], lam[:, :], ACT.Sigmoid).then_inc(lam_squashed, 1)
                act.wait_ge(mix_step, 5)

                def unit(n, u, j):
                    act.wait_ge(qk_projected, n + 1)
                    if not early(n, 2):
                        act.wait_ge(read_ready, (n - 1) * HD)
                        act.wait_ge(hebb_ready, (n - 1) * HD)
                    act.activation(qT[:, u, :], qk[:, 0, :], ACT.Identity, bias=bq[:, 0:1]).then_inc(q_ready, 1)
                    act.activation(kT[:, u, :], qk[:, 1, :], ACT.Identity, bias=bk[:, 0:1], scale=HD ** -0.5
                                   ).then_inc(k_ready, 1)
                    act.wait_ge(g_projected, n + 1)
                    if not early(n, 2):
                        act.wait_ge(a_projected, n - 1)
                    act.activation(gT[:, u, :], gp[0:D // 2, 0, :], ACT.Gelu, bias=gb1[:, 0:1]).then_inc(g_ready, 1)
                    for i in range(HD):
                        act.wait_ge(v_projected, n * HD + (i + 1))
                        if not (early(n, 1) and i < RING):
                            act.wait_ge(hebb_ready, n * HD + (i - RING + 1))
                        act.activation(vG[:, i % RING, :], vp[:, i % 2, 0:L], ACT.Identity, bias=bias_g[:, i:i + 1],
                                       scale=gamma[:, i:i + 1]).then_inc(v_ready, 1)
                    act.wait_ge(a_projected, n + 1)
                    if not early(n, 2):
                        act.wait_ge(mixed_ready, n - 1)
                    act.activation(alpha[:, u, :], gp[:, 1, :], ACT.Sigmoid, bias=gb2[:, 0:1]).then_inc(a_ready, 1)
                over_pairs(act, B, unit)

            @block.vector
            def _(dve):
                dve.wait_ge(loaded, LOADS)
                dve.tensor_copy(wve[:, :, :].rearrange("p i (h j) -> p i h j", h=H),
                                wv[:, :].rearrange("p (h i) -> p i h", h=H).unsqueeze(3)
                                .to_broadcast([P, HD, H, HD])).then_inc(mix_step, 1)
                dve.tensor_copy(gw2e[:, :].rearrange("p (h j) -> p h j", h=H),
                                gw2[:, :].unsqueeze(2).to_broadcast([D // 2, H, HD])).then_inc(mix_step, 1)
                dve.tensor_tensor(bias_g[:, :], bve[:, :], gamma[:, :], ALU.mult).then_inc(mix_step, 1)
                dve.wait_ge(lam_squashed, 1)
                dve.tensor_scalar(retain[:, :], retain[:, :], -1.0, 1.0, ALU.mult, ALU.add).then_inc(mix_step, 1)
                dve.tensor_scalar(bk[:, :], bk[:, :], HD ** -0.5, None, ALU.mult).then_inc(mix_step, 1)
                dve.wait_ge(mix_step, 5)

                def unit(n, u, j):
                    for i in range(HD):
                        dve.wait_ge(hebb_ready, n * HD + (i + 1))
                        if not (early(n, 1) and i < RING):
                            dve.wait_ge(read_ready, n * HD + (i - RING + 1))
                        dve.tensor_tensor_scan(state[:, i % RING, :], retain[:, i:i + 1].to_broadcast([P, L]),
                                               hebb[:, i % RING, :], 0.0, ALU.mult, ALU.add).then_inc(state_ready, 1)
                        dve.wait_ge(state_ready, n * HD + (i + 1))
                        if i == 0:
                            dve.wait_ge(q_ready, n + 1)
                        if not (early(n, 1) and i < RING):
                            dve.wait_ge(summed, n * HD + (i - RING + 1))
                        dve.scalar_tensor_tensor(read[:, i % RING, :], state[:, i % RING, :], static[:, i:i + 1],
                                                 qT[:, u, :], ALU.add, ALU.mult).then_inc(read_ready, 1)
                    dve.wait_ge(a_ready, n + 1)
                    dve.tensor_scalar(beta[:, u, :], alpha[:, u, :], -1.0, 1.0, ALU.mult, ALU.add
                                      ).then_inc(mix_step, 1)
                    dve.wait_ge(y_turned, n + 1)
                    dve.tensor_tensor(soft[:, u, :], tp[:, :, :].rearrange("p s t -> p (s t)"), alpha[:, u, :],
                                      ALU.mult).then_inc(mix_step, 1)
                    dve.wait_ge(mix_step, n * 3 + 7)
                    dve.wait_ge(summed, (n + 1) * HD)
                    dve.tensor_tensor(stp[:, u, :], yp[:, u, 0:L], beta[:, u, :], ALU.mult).then_inc(mix_step, 1)
                    dve.wait_ge(mix_step, n * 3 + 8)
                    if not early(n, 2):
                        dve.wait_ge(out_projected, n - 1)
                    dve.tensor_tensor(mixed[:, u, :], soft[:, u, :], stp[:, u, :], ALU.add).then_inc(mixed_ready, 1)
                    dve.wait_ge(out_projected, n + 1)
                    if not early(n, 2):
                        dve.wait_ge(added, n - 1)
                    dve.tensor_tensor(new[:, u, :, :], op[:, :, :], bo[:, :].unsqueeze(1).to_broadcast([P, 2, P]),
                                      ALU.add).then_inc(biased, 1)
                    dve.wait_ge(biased, n + 1)
                    xs = X[:, bass.ds(n * 2, 2), :]
                    dve.tensor_tensor(xs, xs, new[:, u, :, :], ALU.add).then_inc(added, 1)
                over_pairs(dve, B, unit)


def router_scores(pe, XT, gw, logits, E):
    for n in range(TILES):
        ins = pe.matmul(logits[:, n, :], XT[:, n * P:(n + 1) * P], gw[:, :], start=True, stop=True)
    return ins


def router_stage(nc, name, XT, ident, gate_w, E, GS, gate_bias=None):
    GROUPS, TOP, SCALING = 4, 8, 2.5
    EG = E // GROUPS
    CAPACITY = -(-NT * 2 * 5 // (4 * E))
    BIG = 1.0e30
    T = [P, TILES, E]
    grouped = gate_bias is not None
    with Stage(nc, name) as st:
        gnat = st.sb("gnat", [E, P])
        gw = st.sb("gw", [P, E])
        score = st.sb("score", T)
        choice = st.sb("choice", T)
        eq = st.sb("eq", T)
        other = st.sb("other", T)
        chosen = st.sb("chosen", T)
        weight = st.sb("weight", T)
        tsum = st.sb("tsum", [P, TILES])
        tsum2 = st.sb("tsum2", [P, TILES])
        GT = st.sb("GT", [E, NT])
        grest = st.sb("grest", [E, NT])
        gmid = st.sb("gmid", [E, NT])
        if grouped:
            bias = st.sb("bias", [P, E])
            best = st.sb("best", [P, TILES, GROUPS])
            second = st.sb("second", [P, TILES, GROUPS])
            count = st.sb("count", [P, TILES, GROUPS])
            gsum = st.sb("gsum", [P, TILES, GROUPS])
            more = st.sb("more", [P, TILES, GROUPS, GROUPS])
            tie = st.sb("tie", [P, TILES, GROUPS, GROUPS])
            before = st.sb("before", [P, GROUPS, GROUPS])
            rank = st.sb("rank", [P, TILES, GROUPS])
            top8 = st.sb("top8", [P, TILES, 8])
            running = st.sb("running", T)
            resume = st.sb("resume", T)
            need = st.sb("need", [P, TILES])
        else:
            more = st.sb("more", [P, TILES, E, E])
            tie = st.sb("tie", [P, TILES, E, E])
            before = st.sb("before", [P, E, E])
            rank = st.sb("rank", T)
            member = st.sb("member", [E, NT])
            running = st.sb("running", [E, NT])
            keep = st.sb("keep", [E, NT])
        logits = st.ps("logits", T)
        tp = st.ps("tp", [P, 4, 512])

        loaded = st.sem("loaded")
        built = st.sem("built")
        turned = st.sem("turned")
        gw_ready = st.sem("gw_ready")
        scored = st.sem("scored")
        squashed = st.sem("squashed")
        step = st.sem("step")
        w_ready = st.sem("w_ready")
        w_turned = st.sem("w_turned")
        w_copied = st.sem("w_copied")
        m_turned = st.sem("m_turned")
        m_copied = st.sem("m_copied")

        with st.block() as block:
            @block.sync
            def _(sp):
                sp.dma_start(gnat[:, :], gate_w).then_inc(loaded, 16)
                if grouped:
                    sp.dma_start(bias[:, :], gate_bias.partition_broadcast(P)).then_inc(loaded, 16)

            @block.gpsimd
            def _(pool):
                N = GROUPS if grouped else E
                pool.memset(before[:, :, :], 1.0).then_inc(built, 1)
                pool.wait_ge(built, 1)
                pool.affine_select(out=before[:, :, :], in_=before[:, :, :], compare_op=ALU.is_gt, fill=0.0,
                                   base=0, pattern=[[1, N], [-1, N]], channel_multiplier=0).then_inc(built, 1)
                pool.memset(GS[:, :], 0.0).then_inc(built, 1)
                if grouped:
                    pool.memset(resume[:, :, :], 1.0).then_inc(built, 1)
                    pool.wait_ge(built, 4)
                    pool.memset(resume[:, :, 0:1], 0.0).then_inc(built, 1)
                else:
                    pool.memset(grest[:, :], 1.0).then_inc(built, 1)

            @block.tensor
            def _(pe):
                pe.wait_ge(loaded, 32 if grouped else 16)
                pe.transpose(tp[:, 0, 0:E], gnat[:, :], ident[0:E, 0:E]).then_inc(turned, 1)
                pe.wait_ge(gw_ready, 1)
                router_scores(pe, XT, gw, logits, E).then_inc(scored, 1)
                pe.wait_ge(w_ready, 1)
                for n in range(TILES):
                    q = n // 4
                    if n % 4 == 0 and q >= 4:
                        pe.wait_ge(w_copied, q - 3)
                    ins = pe.transpose(tp[0:E, q % 4, (n % 4) * P:(n % 4 + 1) * P], weight[:, n, :], ident[:, :])
                    if n % 4 == 3:
                        ins.then_inc(w_turned, 1)
                if not grouped:
                    for n in range(TILES):
                        q = n // 4
                        if n % 4 == 0:
                            pe.wait_ge(w_copied, min(8, q + 5))
                            if q >= 4:
                                pe.wait_ge(m_copied, q - 3)
                        ins = pe.transpose(tp[0:E, q % 4, (n % 4) * P:(n % 4 + 1) * P], chosen[:, n, :], ident[:, :])
                        if n % 4 == 3:
                            ins.then_inc(m_turned, 1)

            @block.scalar
            def _(act):
                act.wait_ge(turned, 1)
                act.activation(gw[:, :], tp[:, 0, 0:E], ACT.Copy).then_inc(gw_ready, 1)
                if grouped:
                    act.wait_ge(scored, 1)
                    act.activation(score[:, :, :], logits[:, :, :], ACT.Sigmoid).then_inc(squashed, 1)
                else:
                    act.wait_ge(step, 2)
                    act.activation(other[:, :, :], choice[:, :, :], ACT.Exp).then_inc(squashed, 1)
                for q in range(TILES // 4):
                    act.wait_ge(w_turned, q + 1)
                    act.activation(GT[:, q * 512:(q + 1) * 512], tp[0:E, q % 4, :], ACT.Copy).then_inc(w_copied, 1)
                if not grouped:
                    for q in range(TILES // 4):
                        act.wait_ge(m_turned, q + 1)
                        act.activation(member[:, q * 512:(q + 1) * 512], tp[0:E, q % 4, :], ACT.Copy
                                       ).then_inc(m_copied, 1)

            @block.vector
            def _(dve):
                link = Chain(dve, step)

                def spread(ap, n):
                    return ap.unsqueeze(len(ap.shape)).to_broadcast(list(ap.shape) + [n])

                dve.wait_ge(built, 5 if grouped else 4)
                dve.wait_ge(loaded, 32 if grouped else 16)
                if grouped:
                    dve.wait_ge(squashed, 1)
                    link(dve.tensor_tensor(choice[:, :, :], score[:, :, :],
                                           bias[:, :].unsqueeze(1).to_broadcast(T), ALU.add))
                    cg = choice[:, :, :].rearrange("p t (g e) -> p (t g) e", g=GROUPS)
                    eg = eq[:, :, :].rearrange("p t (g e) -> p (t g) e", g=GROUPS)
                    og = other[:, :, :].rearrange("p t (g e) -> p (t g) e", g=GROUPS)
                    flat = lambda a: a[:, :, :].rearrange("p t g -> p (t g)")
                    link(dve.tensor_reduce(flat(best), cg, AX.X, ALU.max))
                    link(dve.tensor_tensor(eg, cg, spread(flat(best), EG), ALU.is_equal))
                    link(dve.tensor_reduce(flat(count), eg, AX.X, ALU.add))
                    link(dve.scalar_tensor_tensor(og, eg, -BIG, cg, ALU.mult, ALU.add))
                    link(dve.tensor_reduce(flat(second), og, AX.X, ALU.max))
                    link(dve.tensor_scalar(flat(count), flat(count), 1.5, None, ALU.is_gt))
                    link(dve.tensor_tensor(flat(gsum), flat(best), flat(count), ALU.mult))
                    link(dve.tensor_scalar(flat(count), flat(count), BIG, -BIG, ALU.mult, ALU.add))
                    link(dve.tensor_tensor(flat(gsum), flat(gsum), flat(count), ALU.add))
                    link(dve.tensor_tensor(flat(second), flat(second), flat(gsum), ALU.max))
                    link(dve.tensor_tensor(flat(gsum), flat(best), flat(second), ALU.add))
                    rank_of(dve, link, gsum, rank, more, tie, before, GROUPS)
                    link(dve.tensor_scalar(flat(rank), flat(rank), 1.5, None, ALU.is_lt))
                    link(dve.tensor_tensor(cg, cg, spread(flat(rank), EG), ALU.mult))
                    for n in range(TILES):
                        ins = dve.max(top8[:, n, :], choice[:, n, :])
                    link(ins)
                    eighth = top8[:, :, TOP - 1]
                    link(dve.tensor_tensor(eq[:, :, :], choice[:, :, :], spread(eighth, E), ALU.is_equal))
                    link(dve.tensor_tensor(chosen[:, :, :], choice[:, :, :], spread(eighth, E), ALU.is_gt))
                    link(dve.tensor_reduce(tsum[:, :], chosen[:, :, :], AX.X, ALU.add))
                    link(dve.tensor_scalar(need[:, :], tsum[:, :], -1.0, TOP + 0.5, ALU.mult, ALU.add))
                    link(dve.tensor_tensor_scan(running[:, :, :].rearrange("p t e -> p (t e)"),
                                                resume[:, :, :].rearrange("p t e -> p (t e)"),
                                                eq[:, :, :].rearrange("p t e -> p (t e)"), 0.0, ALU.mult, ALU.add))
                    link(dve.tensor_tensor(running[:, :, :], running[:, :, :], spread(need[:, :], E), ALU.is_lt))
                    link(dve.tensor_tensor(eq[:, :, :], eq[:, :, :], running[:, :, :], ALU.mult))
                    link(dve.tensor_tensor(chosen[:, :, :], chosen[:, :, :], eq[:, :, :], ALU.add))
                else:
                    dve.wait_ge(scored, 1)
                    link(dve.tensor_reduce(tsum[:, :], logits[:, :, :], AX.X, ALU.max))
                    link(dve.tensor_tensor(choice[:, :, :], logits[:, :, :], spread(tsum[:, :], E), ALU.subtract))
                    dve.wait_ge(squashed, 1)
                    link(dve.tensor_reduce(tsum[:, :], other[:, :, :], AX.X, ALU.add))
                    link(dve.reciprocal(tsum2[:, :], tsum[:, :]))
                    link(dve.tensor_tensor(score[:, :, :], other[:, :, :], spread(tsum2[:, :], E), ALU.mult))
                    rank_of(dve, link, score, rank, more, tie, before, E)
                    link(dve.tensor_scalar(chosen[:, :, :], rank[:, :, :], 1.5, None, ALU.is_lt))
                link(dve.tensor_tensor(weight[:, :, :], score[:, :, :], chosen[:, :, :], ALU.mult))
                link(dve.tensor_reduce(tsum[:, :], weight[:, :, :], AX.X, ALU.add))
                link(dve.tensor_scalar(tsum[:, :], tsum[:, :], 1e-20, None, ALU.add))
                link(dve.reciprocal(tsum2[:, :], tsum[:, :]))
                if grouped:
                    link(dve.tensor_scalar(tsum2[:, :], tsum2[:, :], SCALING, None, ALU.mult))
                dve.tensor_tensor(weight[:, :, :], weight[:, :, :], spread(tsum2[:, :], E), ALU.mult
                                  ).then_inc(w_ready, 1)
                dve.wait_ge(w_ready, 1)
                dve.wait_ge(w_copied, TILES // 4)
                if not grouped:
                    dve.wait_ge(m_copied, TILES // 4)
                    link(dve.tensor_tensor_scan(running[:, :], grest[:, :], member[:, :], 0.0, ALU.mult, ALU.add))
                    link(dve.tensor_scalar(keep[:, :], running[:, :], CAPACITY + 0.5, None, ALU.is_lt))
                    link(dve.tensor_tensor(GT[:, :], GT[:, :], keep[:, :], ALU.mult))
                link(dve.tensor_copy(GS[0:E, :], GT[:, :]))
                link(dve.tensor_tensor(grest[:, :], GT[:, :], GS[0:E, :], ALU.subtract))
                link(dve.tensor_copy(GS[32:32 + E, :], grest[:, :]))
                link(dve.tensor_copy(gmid[:, :], GS[32:32 + E, :]))
                link(dve.tensor_tensor(gmid[:, :], grest[:, :], gmid[:, :], ALU.subtract))
                link(dve.tensor_copy(GS[64:64 + E, :], gmid[:, :]))


def rank_of(dve, link, value, rank, more, tie, before, N):
    mine = value[:, :, :].unsqueeze(3).to_broadcast([P, TILES, N, N])
    theirs = value[:, :, :].unsqueeze(2).to_broadcast([P, TILES, N, N])
    link(dve.tensor_tensor(more[:, :, :, :], theirs, mine, ALU.is_gt))
    link(dve.tensor_tensor(tie[:, :, :, :], theirs, mine, ALU.is_equal))
    link(dve.tensor_tensor(tie[:, :, :, :], tie[:, :, :, :],
                           before[:, :, :].unsqueeze(1).to_broadcast([P, TILES, N, N]), ALU.mult))
    link(dve.tensor_tensor(more[:, :, :, :], more[:, :, :, :], tie[:, :, :, :], ALU.add))
    link(dve.tensor_reduce(rank[:, :, :], more[:, :, :, :], AX.X, ALU.add))


def experts_stage(nc, name, X, XT, ident, GS, gates, ups, downs, routed, per, direct=False):
    S = len(gates)
    C = 512
    CHUNKS = NT // C
    with Stage(nc, name) as st:
        wT = st.sb("wT", [P, 3, S, P])
        nat = wT if direct else st.sb("nat", [P, 3, S, P])
        if routed:
            pick = st.sb("pick", [96, routed, P], BF16)
        sg = st.sb("sg", [P, 2, C])
        hu = st.sb("hu", [P, 2, C])
        hid = st.sb("hid", [P, 2, C])
        oT = st.sb("oT", [P, C])
        gp = st.ps("gp", [P, 2, C])
        up = st.ps("up", [P, 2, C])
        wp = st.ps("wp", [P, 2, C])
        op = st.ps("op", [P, C])
        tp = st.ps("tp", [P, C])
        loaded = st.sem("loaded")
        built = st.sem("built")
        w_turned = st.sem("w_turned")
        w_copied = st.sem("w_copied")
        g_ready = st.sem("g_ready")
        u_ready = st.sem("u_ready")
        r_ready = st.sem("r_ready")
        sg_ready = st.sem("sg_ready")
        hu_ready = st.sem("hu_ready")
        hid_ready = st.sem("hid_ready")
        downed = st.sem("downed")
        oT_ready = st.sem("oT_ready")
        o_turned = st.sem("o_turned")
        added = st.sem("added")
        NW = 3 * S

        with st.block() as block:
            @block.sync
            def _(sp):
                for m, mats in enumerate((gates, ups, downs)):
                    for s in range(S):
                        src = mats[s]
                        dst = nat[:, m, s, :]
                        if len(src.shape) == 3:
                            dst = dst.rearrange("h (e i) -> h e i", e=src.shape[1])
                        sp.dma_start(dst, src).then_inc(loaded, 16)

            @block.gpsimd
            def _(pool):
                if routed:
                    pool.memset(pick[:, :, :], 0.0).then_inc(built, 1)
                for b in range(3 if routed else 0):
                    pool.wait_ge(built, b + 1)
                    pv = pick[:, :, :].rearrange("p s (a i) -> p s a i", a=per)
                    pool.affine_select(out=pv, in_=pv, compare_op=ALU.not_equal, fill=1.0, base=-32 * b,
                                       pattern=[[-per, routed], [-1, per], [0, P // per]],
                                       channel_multiplier=1).then_inc(built, 1)

            @block.tensor
            def _(pe):
                pe.wait_ge(loaded, 16 * NW)
                for i in range(0 if direct else NW):
                    q = i // 4
                    if i % 4 == 0 and q >= 2:
                        pe.wait_ge(w_copied, q - 1)
                    m, s = divmod(i, S)
                    ins = pe.transpose(gp[:, q % 2, (i % 4) * P:(i % 4 + 1) * P], nat[:, m, s, :], ident[:, :])
                    if i % 4 == 3 or i == NW - 1:
                        ins.then_inc(w_turned, 1)
                if not direct:
                    pe.wait_ge(w_copied, -(-NW // 4))
                if routed:
                    pe.wait_ge(built, 4)

                def down(n, s):
                    pe.wait_ge(hid_ready, n * S + (s + 1))
                    ins = pe.matmul(op[:, :], wT[:, 2, s, :], hid[:, s % 2, :], start=(s == 0), stop=(s == S - 1))
                    ins.then_inc(downed, 1)

                def turn_out(n):
                    pe.wait_ge(oT_ready, n + 1)
                    if not early(n, 1):
                        pe.wait_ge(added, n)
                    for k in range(4):
                        ins = pe.transpose(tp[:, k * P:(k + 1) * P], oT[:, k * P:(k + 1) * P], ident[:, :])
                    ins.then_inc(o_turned, 1)

                def chunk(n):
                    x = XT[:, bass.ds(n * C, C)]
                    for s in range(S):
                        if not (early(n, 1) and s < 2):
                            pe.wait_ge(sg_ready, n * S + s - 1)
                            pe.wait_ge(hu_ready, n * S + s - 1)
                            pe.wait_ge(hid_ready, n * S + s - 1)
                        pe.matmul(gp[:, s % 2, :], wT[:, 0, s, :], x, start=True, stop=True).then_inc(g_ready, 1)
                        pe.matmul(up[:, s % 2, :], wT[:, 1, s, :], x, start=True, stop=True).then_inc(u_ready, 1)
                        if s < routed:
                            pe.matmul(wp[:, s % 2, :], pick[:, s, :], GS[:, bass.ds(n * C, C)], start=True, stop=True
                                      ).then_inc(r_ready, 1)
                        if s == 2 and not early(n, 1):
                            turn_out(n - 1)
                        if s == 1 and not early(n, 1):
                            pe.wait_ge(oT_ready, n)
                        if s >= 1:
                            down(n, s - 1)
                    down(n, S - 1)
                over(pe, CHUNKS, chunk)
                turn_out(CHUNKS - 1)

            @block.scalar
            def _(act):
                for q in range(0 if direct else -(-NW // 4)):
                    m = min(4, NW - 4 * q)
                    act.wait_ge(w_turned, q + 1)
                    act.activation(wT[:, :, :, :].rearrange("p m s f -> p (m s f)")[:, q * 512:q * 512 + m * P],
                                   gp[:, q % 2, 0:m * P], ACT.Copy).then_inc(w_copied, 1)

                def chunk(n):
                    for s in range(S):
                        act.wait_ge(g_ready, n * S + (s + 1))
                        if not (early(n, 1) and s < 2):
                            act.wait_ge(hu_ready, n * S + s - 1)
                        act.activation(sg[:, s % 2, :], gp[:, s % 2, :], ACT.Silu).then_inc(sg_ready, 1)
                    act.wait_ge(downed, (n + 1) * S)
                    if not early(n, 1):
                        act.wait_ge(o_turned, n)
                    act.activation(oT[:, :], op[:, :], ACT.Copy).then_inc(oT_ready, 1)
                over(act, CHUNKS, chunk)

            @block.vector
            def _(dve):
                def add_out(n):
                    dve.wait_ge(o_turned, n + 1)
                    xs = X[:, bass.ds(n * 4, 4), :]
                    dve.tensor_tensor(xs, xs, tp[:, :].rearrange("p (k d) -> p k d", k=4), ALU.add).then_inc(added, 1)

                def chunk(n):
                    for s in range(S):
                        dve.wait_ge(sg_ready, n * S + (s + 1))
                        dve.wait_ge(u_ready, n * S + (s + 1))
                        if not (early(n, 1) and s < 2):
                            dve.wait_ge(hid_ready, n * S + s - 1)
                        dve.tensor_tensor(hu[:, s % 2, :], sg[:, s % 2, :], up[:, s % 2, :], ALU.mult
                                          ).then_inc(hu_ready, 1)
                        dve.wait_ge(hu_ready, n * S + (s + 1))
                        if not (early(n, 1) and s < 2):
                            dve.wait_ge(downed, n * S + s - 1)
                        if s < routed:
                            dve.wait_ge(r_ready, n * routed + (s + 1))
                            ins = dve.tensor_tensor(hid[:, s % 2, :], hu[:, s % 2, :], wp[:, s % 2, :], ALU.mult)
                        else:
                            ins = dve.tensor_copy(hid[:, s % 2, :], hu[:, s % 2, :])
                        ins.then_inc(hid_ready, 1)
                        if s == 3 and not early(n, 1):
                            add_out(n - 1)
                over(dve, CHUNKS, chunk)
                add_out(CHUNKS - 1)


def moe0(nc, X, ident, t):
    E, I = 32, 64
    with ExitStack() as ctx:
        XT = ctx.enter_context(nc.sbuf_tensor("f0_XT", [P, NT], F32))
        GS = ctx.enter_context(nc.sbuf_tensor("f0_GS", [96, NT], BF16))
        norm_stage(nc, "f0n", X, XT, ident)
        router_stage(nc, "f0r", XT, ident, t["L0_ffn_gate_w"], E, GS, gate_bias=t["L0_ffn_gate_bias"])
        pairs = [(2 * k, 2 * k + 2) for k in range(E // 2)]
        gates = [t["L0_ffn_expert_gate"][a:b].rearrange("e i h -> (e i) h") for a, b in pairs]
        ups = [t["L0_ffn_expert_up"][a:b].rearrange("e i h -> (e i) h") for a, b in pairs]
        downs = [t["L0_ffn_expert_down"][a:b].rearrange("e h i -> h e i") for a, b in pairs]
        experts_stage(nc, "f0e", X, XT, ident, GS, gates + [t["L0_ffn_shared_gate"]], ups + [t["L0_ffn_shared_up"]],
                      downs + [t["L0_ffn_shared_down"]], len(pairs), 2)


def moe1(nc, X, ident, t):
    E, SHARED = 8, 2
    with ExitStack() as ctx:
        XT = ctx.enter_context(nc.sbuf_tensor("f1_XT", [P, NT], F32))
        GS = ctx.enter_context(nc.sbuf_tensor("f1_GS", [96, NT], BF16))
        norm_stage(nc, "f1n", X, XT, ident)
        router_stage(nc, "f1r", XT, ident, t["L1_ffn_gate_w"], E, GS)
        cut = [slice(s * P, (s + 1) * P) for s in range(SHARED)]
        gates = [t["L1_ffn_we_gate"][e] for e in range(E)] + [t["L1_ffn_ws_gate"][c, :] for c in cut]
        ups = [t["L1_ffn_we_up"][e] for e in range(E)] + [t["L1_ffn_ws_up"][c, :] for c in cut]
        downs = [t["L1_ffn_we_down"][e] for e in range(E)] + [t["L1_ffn_ws_down"][:, c] for c in cut]
        experts_stage(nc, "f1e", X, XT, ident, GS, gates, ups, downs, E, 1)

S_HEADS, DK, DV = 8, 64, 128
PAIRS_H = S_HEADS // 2
R_AU, F_FF, CK = 64, 512, 4


def conv_stage(nc, name, HT, t):
    with Stage(nc, name) as st:
        cw = st.sb("cw", [P, CK])
        cb = st.sb("cb", [P, 1])
        acc = st.sb("acc", [P, B, L])
        loaded = st.sem("loaded")
        step = st.sem("step")
        summed = st.sem("summed")
        hv = HT[:, :].rearrange("p (b t) -> p b t", b=B)
        HALF = B // 2

        with st.block() as block:
            @block.sync
            def _(sp):
                sp.dma_start(cw[:, :], t["L1_attn_conv_w"]).then_inc(loaded, 16)
                sp.dma_start(cb[:, :], column(t["L1_attn_conv_b"])).then_inc(loaded, 16)

            @block.vector
            def _(dve):
                dve.wait_ge(loaded, 32)
                link = Chain(dve, step)
                for g in range(2):
                    bs = slice(g * HALF, (g + 1) * HALF)
                    link(dve.tensor_scalar(acc[:, bs, :], hv[:, bs, :], cw[:, CK - 1:CK], None, ALU.mult))
                    for s in range(1, CK):
                        ins = dve.scalar_tensor_tensor(acc[:, bs, s:L], hv[:, bs, 0:L - s], cw[:, CK - 1 - s:CK - s],
                                                       acc[:, bs, s:L], ALU.mult, ALU.add)
                        if s < CK - 1:
                            link(ins)
                        else:
                            ins.then_inc(summed, 1)

            @block.scalar
            def _(act):
                act.wait_ge(loaded, 32)
                for g in range(2):
                    bs = slice(g * HALF, (g + 1) * HALF)
                    act.wait_ge(summed, g + 1)
                    act.activation(hv[:, bs, :], acc[:, bs, :], ACT.Silu, bias=cb[:, 0:1])


def spike_stage(nc, name, HT, SD, AUT, t):
    C = 512
    CHUNKS = NT // C
    DECAY = 0.9
    STEP = 8
    with Stage(nc, name) as st:
        w = st.sb("w", [P, S_HEADS * DK])
        wau = st.sb("wau", [P, R_AU])
        bau = st.sb("bau", [R_AU, 1])
        N = st.sb("N", [P, 2, PAIRS_H, B])
        sdp = st.ps("sdp", [P, 4, C])
        aup = st.ps("aup", [R_AU, 2, C])
        loaded = st.sem("loaded")
        projected = st.sem("projected")
        doubled = st.sem("doubled")
        au_projected = st.sem("au_projected")
        au_ready = st.sem("au_ready")
        charged = st.sem("charged")
        reset = st.sem("reset")
        zeroed = st.sem("zeroed")
        sd_flat = SD[:, :, :, :].rearrange("p x b t -> p x (b t)")

        with st.block() as block:
            @block.sync
            def _(sp):
                sp.dma_start(w[:, :], t["L1_attn_w_spike"]).then_inc(loaded, 16)
                sp.dma_start(wau[:, :], t["L1_attn_w_au"]).then_inc(loaded, 16)
                sp.dma_start(bau[:, :], column(t["L1_attn_b_au"], 0, R_AU)).then_inc(loaded, 16)

            @block.tensor
            def _(pe):
                pe.wait_ge(loaded, 48)
                for c in range(CHUNKS):
                    x = HT[:, c * C:(c + 1) * C]
                    for h in range(PAIRS_H):
                        if c >= 1:
                            pe.wait_ge(doubled, (c - 1) * PAIRS_H + h + 1)
                        pe.matmul(sdp[:, h, :], w[:, h * P:(h + 1) * P], x, start=True, stop=True
                                  ).then_inc(projected, 1)
                    if c >= 2:
                        pe.wait_ge(au_ready, c - 1)
                    pe.matmul(aup[:, c % 2, :], wau[:, :], x, start=True, stop=True).then_inc(au_projected, 1)

            @block.scalar
            def _(act):
                act.wait_ge(loaded, 48)
                for c in range(CHUNKS):
                    for h in range(PAIRS_H):
                        act.wait_ge(projected, c * PAIRS_H + h + 1)
                        act.activation(sd_flat[:, h, c * C:(c + 1) * C], sdp[:, h, :], ACT.Copy, scale=2.0
                                       ).then_inc(doubled, 1)
                    act.wait_ge(au_projected, c + 1)
                    act.activation(AUT[:, c * C:(c + 1) * C], aup[:, c % 2, :], ACT.Silu, bias=bau[:, 0:1]
                                   ).then_inc(au_ready, 1)

            @block.vector
            def _(dve):
                dve.memset(N[:, :, :, :], 0.0).then_inc(zeroed, 1)
                dve.wait_ge(zeroed, 1)
                dve.wait_ge(doubled, CHUNKS * PAIRS_H)

                def token(i, k):
                    m = SD[:, :, :, bass.ds(i, 1)].rearrange("p x b a -> p x (b a)")
                    if not early(i, 1):
                        dve.wait_ge(reset, i)
                    dve.scalar_tensor_tensor(m, N[:, k % 2, :, :], -DECAY, m, ALU.mult, ALU.add).then_inc(charged, 1)
                    dve.wait_ge(charged, i + 1)
                    dve.scalar_tensor_tensor(N[:, 1 - k % 2, :, :], m, 1.0, m, ALU.is_gt, ALU.subtract
                                             ).then_inc(reset, 1)
                for k in range(STEP):
                    token(k, k)
                with dve.Fori(1, L // STEP) as g:
                    for k in range(STEP):
                        token(g * STEP + k, k)
                dve.wait_ge(reset, L)
                for h in range(PAIRS_H):
                    dve.tensor_scalar(sd_flat[:, h, :], sd_flat[:, h, :], 1.0, None, ALU.is_gt)


def prepare_stage(nc, name, HT, SD, AUT, t, unit_in, unit_v):
    EPS = 1e-6
    U = B * PAIRS_H
    with Stage(nc, name) as st:
        wq = st.sb("wq", [P, S_HEADS * DK])
        wk = st.sb("wk", [P, S_HEADS * DK])
        wv = st.sb("wv", [P, S_HEADS * DV])
        wad = st.sb("wad", [R_AU, S_HEADS * DK])
        bad = st.sb("bad", [P, PAIRS_H])
        asp = st.sb("asp", [P, PAIRS_H])
        bsp = st.sb("bsp", [P, PAIRS_H])
        wb = st.sb("wb", [P, S_HEADS])
        wbe = st.sb("wbe", [P, S_HEADS, DK])
        bbe = st.sb("bbe", [P, PAIRS_H])
        same = st.sb("same", [P, P])
        bmat = st.sb("bmat", [P, PAIRS_H, P])
        hs = st.sb("hs", [P, 2, P])
        sq = st.sb("sq", [P, 2, 2, L])
        nrm = st.sb("nrm", [P, 2, 2, L])
        rcp = st.sb("rcp", [P, 2, 2, L])
        za = st.sb("za", [P, 2, L])
        a0 = st.sb("a0", [P, 2, L])
        b0 = st.sb("b0", [P, 2, L])
        a1 = st.sb("a1", [P, 2, L])
        b1 = st.sb("b1", [P, 2, L])
        res = st.sb("res", [P, 2, 4, L])
        vs = st.sb("vs", [P, 2, 2, 2 * DV])
        qk = st.ps("qk", [P, 2, 2, L])
        ab = st.ps("ab", [P, 2, 2, L])
        ssq = st.ps("ssq", [P, 2, L])
        cnt = st.ps("cnt", [P, 2, 2 * L])
        vp = st.ps("vp", [P, 2, 2 * DV])

        loaded = st.sem("loaded")
        built = st.sem("built")
        spread_ready = st.sem("spread_ready")
        hs_ready = st.sem("hs_ready")
        qk_projected = st.sem("qk_projected")
        ab_projected = st.sem("ab_projected")
        counted = st.sem("counted")
        v_projected = st.sem("v_projected")
        v_copied = st.sem("v_copied")
        squared = st.sem("squared")
        ssq_ready = st.sem("ssq_ready")
        rooted = st.sem("rooted")
        eps_added = st.sem("eps_added")
        inverted = st.sem("inverted")
        normed = st.sem("normed")
        za_ready = st.sem("za_ready")
        a0_ready = st.sem("a0_ready")
        b0_ready = st.sem("b0_ready")
        a1_ready = st.sem("a1_ready")
        alpha_ready = st.sem("alpha_ready")
        b1_ready = st.sem("b1_ready")
        kb_ready = st.sem("kb_ready")
        in_stored = [st.sem("in_stored0"), st.sem("in_stored1")]
        v_stored = [st.sem("v_stored0"), st.sem("v_stored1")]
        hard = SD[:, :, :, :].rearrange("p x b t -> p x (b t)")
        LOADS = 16 * (8 + S_HEADS)

        def units(eng, body):
            def batch(b):
                for h in range(PAIRS_H):
                    body(b * PAIRS_H + h, h, b)
            over(eng, B, batch)

        with st.block() as block:
            @block.sync
            def _(sp):
                rows = lambda a: a.rearrange("(x p) -> p x", p=P)
                with nc.allow_non_contiguous_dma(reason="one column of parameters for each head pair"):
                    for dst, src in [(wq[:, :], t["L1_attn_wq"]), (wk[:, :], t["L1_attn_wk"]),
                                     (wv[:, :], t["L1_attn_wv"]), (wad[:, :], t["L1_attn_w_ad"]),
                                     (bad[:, :], rows(t["L1_attn_b_ad"])),
                                     (asp[:, :], rows(t["L1_attn_alpha_spike"].rearrange("a h k -> (a h k)"))),
                                     (bsp[:, :], rows(t["L1_attn_beta_spike"].rearrange("a h k -> (a h k)"))),
                                     (wb[:, :], t["L1_attn_w_beta"])]:
                        sp.dma_start(dst, src).then_inc(loaded, 16)
                    for h in range(S_HEADS):
                        sp.dma_start(bbe[(h % 2) * DK:(h % 2 + 1) * DK, h // 2:h // 2 + 1],
                                     t["L1_attn_b_beta"][h:h + 1].partition_broadcast(DK)).then_inc(loaded, 16)

                def unit(n, h, b):
                    u = h % 2
                    sp.wait_ge(alpha_ready, n + 1)
                    sp.wait_ge(kb_ready, n + 1)
                    sp.dma_start(unit_in[bass.ds(n, 1)].rearrange("a p c t -> (a p) c t"), res[:, u, :, :]
                                 ).then_inc(in_stored[u], 16)
                    sp.wait_ge(v_copied, n + 1)
                    sp.dma_start(unit_v[bass.ds(n, 1)].rearrange("a p c t -> (a p) c t"), vs[:, u, :, :]
                                 ).then_inc(v_stored[u], 16)
                units(sp, unit)
                for u in range(2):
                    sp.wait_ge(in_stored[u], 16 * U // 2)
                    sp.wait_ge(v_stored[u], 16 * U // 2)

            @block.gpsimd
            def _(pool):
                pool.memset(same[:, :], 1.0).then_inc(built, 1)
                pool.wait_ge(built, 1)
                sv = same[:, :].rearrange("p (h c) -> p h c", h=2)
                pool.affine_select(out=sv, in_=sv, compare_op=ALU.is_ge, fill=0.0, base=0,
                                   pattern=[[-DK, 2], [0, DK]], channel_multiplier=1).then_inc(built, 1)
                pool.wait_ge(built, 2)
                pool.affine_select(out=sv, in_=sv, compare_op=ALU.is_ge, fill=0.0, base=DK - 1,
                                   pattern=[[DK, 2], [0, DK]], channel_multiplier=-1).then_inc(built, 1)

            @block.tensor
            def _(pe):
                pe.wait_ge(loaded, LOADS)
                pe.wait_ge(built, 3)
                pe.wait_ge(spread_ready, 2)

                def square_sum(n, u):
                    pe.wait_ge(squared, n + 1)
                    if not early(n, 1):
                        pe.wait_ge(rooted, n)
                    pe.matmul(ssq[:, :, :].rearrange("p c t -> p (c t)"), same[:, :],
                              sq[:, u, :, :].rearrange("p c t -> p (c t)"), start=True, stop=True
                              ).then_inc(ssq_ready, 1)

                def unit(n, h, b):
                    u = h % 2
                    first = isinstance(b, int) and h < 2
                    x = HT[:, bass.ds(b * L, L)]
                    rows = slice(h * P, (h + 1) * P)
                    if not first:
                        pe.wait_ge(normed, n - 1)
                        pe.wait_ge(za_ready, n - 1)
                        pe.wait_ge(b0_ready, n - 1)
                        pe.wait_ge(b1_ready, n - 1)
                        pe.wait_ge(alpha_ready, n - 1)
                    pe.matmul(qk[:, u, 0, :], wk[:, rows], x, start=True, stop=True)
                    pe.matmul(qk[:, u, 1, :], wq[:, rows], x, start=True, stop=True).then_inc(qk_projected, 1)
                    pe.matmul(ab[:, u, 0, :], wad[:, rows], AUT[:, bass.ds(b * L, L)], start=True, stop=True)
                    pe.matmul(ab[:, u, 1, :], wbe[:, 2 * h:2 * h + 2, :].rearrange("p a d -> p (a d)"), x,
                              start=True, stop=False)
                    fired = hard[:, h, bass.ds(b * L, L)]
                    pe.matmul(ab[:, u, 1, :], bmat[:, h, :], fired, start=False, stop=True
                              ).then_inc(ab_projected, 1)
                    pe.matmul(cnt[:, u, 0:L], same[:, :], fired, start=True, stop=True).then_inc(counted, 1)
                    square_sum(n, u)
                    if h == 0:
                        pe.wait_ge(hs_ready, b + 1)
                    if not early(n, 1) and not (isinstance(b, int) and h == 0):
                        pe.wait_ge(v_copied, n)
                    for s in range(2):
                        ins = pe.matmul(vp[:, s, :], hs[:, s, :], wv[:, 2 * h * DV:2 * (h + 1) * DV],
                                        start=True, stop=True)
                    ins.then_inc(v_projected, 1)
                units(pe, unit)

            @block.scalar
            def _(act):
                def unit(n, h, b):
                    u = h % 2
                    first = isinstance(b, int) and h < 2
                    if h == 0:
                        if not early(b, 1):
                            act.wait_ge(v_projected, n)
                        act.activation(hs[:, :, :].rearrange("p s t -> p (s t)"), HT[:, bass.ds(b * L, L)], ACT.Copy
                                       ).then_inc(hs_ready, 1)
                    act.wait_ge(qk_projected, n + 1)
                    if not first:
                        act.wait_ge(ssq_ready, n - 1)
                    act.activation(sq[:, u, :, :], qk[:, u, :, :], ACT.Square).then_inc(squared, 1)
                    act.wait_ge(ssq_ready, n + 1)
                    if not first:
                        act.wait_ge(eps_added, n - 1)
                    act.activation(nrm[:, u, :, :], ssq[:, :, :], ACT.Sqrt).then_inc(rooted, 1)
                    act.wait_ge(za_ready, n + 1)
                    if not first:
                        act.wait_ge(a1_ready, n - 1)
                        act.wait_ge(b1_ready, n - 1)
                    act.activation(a0[:, u, :], za[:, u, :], ACT.Sigmoid, bias=bad[:, h:h + 1]).then_inc(a0_ready, 1)
                    act.wait_ge(ab_projected, n + 1)
                    act.activation(b0[:, u, :], ab[:, u, 1, :], ACT.Sigmoid, bias=bbe[:, h:h + 1]
                                   ).then_inc(b0_ready, 1)
                    act.wait_ge(v_projected, n + 1)
                    if not first:
                        act.wait_ge(v_stored[u], b * 32 + (h // 2) * 16)
                    act.activation(vs[:, u, :, :], vp[:, :, :], ACT.Copy).then_inc(v_copied, 1)
                act.wait_ge(loaded, LOADS)
                units(act, unit)

            @block.vector
            def _(dve):
                dve.wait_ge(loaded, LOADS)
                dve.tensor_copy(wbe[:, :, :], wb[:, :].unsqueeze(2).to_broadcast([P, S_HEADS, DK])
                                ).then_inc(spread_ready, 1)
                dve.wait_ge(built, 3)
                dve.tensor_tensor(bmat[:, :, :], same[:, :].unsqueeze(1).to_broadcast([P, PAIRS_H, P]),
                                  bsp[:, :].unsqueeze(2).to_broadcast([P, PAIRS_H, P]), ALU.mult
                                  ).then_inc(spread_ready, 1)

                def unit(n, h, b):
                    u = h % 2
                    first = isinstance(b, int) and h < 2
                    dve.wait_ge(ab_projected, n + 1)
                    if not first:
                        dve.wait_ge(a0_ready, n - 1)
                    dve.scalar_tensor_tensor(za[:, u, :], hard[:, h, bass.ds(b * L, L)], asp[:, h:h + 1],
                                             ab[:, u, 0, :], ALU.mult, ALU.add).then_inc(za_ready, 1)
                    dve.wait_ge(rooted, n + 1)
                    if not first:
                        dve.wait_ge(normed, n - 1)
                    dve.tensor_scalar(nrm[:, u, :, :], nrm[:, u, :, :], EPS, None, ALU.add).then_inc(eps_added, 1)
                    dve.wait_ge(eps_added, n + 1)
                    dve.reciprocal(rcp[:, u, :, :], nrm[:, u, :, :]).then_inc(inverted, 1)
                    dve.wait_ge(inverted, n + 1)
                    if not first:
                        dve.wait_ge(in_stored[u], b * 32 + (h // 2) * 16)
                    dve.tensor_tensor(res[:, u, 0:2, :], qk[:, u, :, :], rcp[:, u, :, :], ALU.mult
                                      ).then_inc(normed, 1)
                    dve.wait_ge(a0_ready, n + 1)
                    dve.wait_ge(counted, n + 1)
                    if not first:
                        dve.wait_ge(alpha_ready, n - 1)
                        dve.wait_ge(kb_ready, n - 1)
                    dve.scalar_tensor_tensor(a1[:, u, :], cnt[:, u, 0:L], 0.5, a0[:, u, :], ALU.is_gt, ALU.mult
                                             ).then_inc(a1_ready, 1)
                    dve.wait_ge(b0_ready, n + 1)
                    dve.scalar_tensor_tensor(b1[:, u, :], cnt[:, u, 0:L], 0.5, b0[:, u, :], ALU.is_gt, ALU.mult
                                             ).then_inc(b1_ready, 1)
                    dve.wait_ge(a1_ready, n + 1)
                    dve.scalar_tensor_tensor(res[:, u, 2, :], cnt[:, u, 0:L], 0.5, a1[:, u, :], ALU.is_lt, ALU.add
                                             ).then_inc(alpha_ready, 1)
                    dve.wait_ge(b1_ready, n + 1)
                    dve.wait_ge(normed, n + 1)
                    dve.tensor_tensor(res[:, u, 3, :], res[:, u, 0, :], b1[:, u, :], ALU.mult).then_inc(kb_ready, 1)
                units(dve, unit)


def delta_stage(nc, name, ident, unit_in, unit_v, unit_o):
    LEVELS = 7
    DUOS = B * PAIRS_H // 2
    TAU = 4
    with Stage(nc, name) as st:
        src = st.sb("src", [P, 2, 2, 4, L])
        val = st.sb("val", [P, 2, 2, 2, 2 * DV])
        total = st.sb("total", [P, 2, 2, L])
        mask = st.sb("mask", [P, LEVELS, P // 2])
        LT = st.sb("LT", [P, 2, LEVELS, TAU, P])
        R = st.sb("R", [P, 2, TAU, P])
        BT = st.sb("BT", [P, 2, TAU, P])
        part = st.sb("part", [P, 2, TAU, P // 2])
        T = st.sb("T", [P, 2, TAU, P])
        X = st.sb("X", [P, 2, TAU, P])
        cross_ = st.sb("cross", [P, 2, 2, 2, P])
        W = st.sb("W", [P, 2, 2, 2, DV])
        V1 = st.sb("V1", [P, 2, 2, DV])
        osb = st.sb("osb", [P, 2, 2, 2, DV])
        lb = st.ps("lb", [P, 2, TAU, 2 * P])
        wp = st.ps("wp", [P, 2, TAU, P])
        dp = st.ps("dp", [P, 2, TAU, P])
        diag = lambda u: lb[:, u, :, 0:P]
        halves = lambda u: lb[:, u, :, 0:P].rearrange("p k (a t) -> p k a t", a=2)
        across = lambda u: lb[:, u, 0:TAU:2, :].rearrange("p h (a t) -> p h a t", a=2)
        outputs = lambda u: dp[:, u, :, :].rearrange("p (s h) t -> p s h t", s=2)

        s_ = lambda x: st.sem(x)
        masks_ready = s_("masks_ready")
        src_loaded = [s_("src_loaded0"), s_("src_loaded1")]
        val_loaded = [s_("val_loaded0"), s_("val_loaded1")]
        diag_scored = s_("diag_scored")
        diag_ready = s_("diag_ready")
        decayed = s_("decayed")
        scored = s_("scored")
        lt_ready = s_("lt_ready")
        part_ready = s_("part_ready")
        bt_ready = s_("bt_ready")
        kq_ready = s_("kq_ready")
        kg_ready = s_("kg_ready")
        total_ready = s_("total_ready")
        r_scored = s_("r_scored")
        r_ready = s_("r_ready")
        d_scored = s_("d_scored")
        t_ready = s_("t_ready")
        cross_scored = s_("cross_scored")
        cross_ready = s_("cross_ready")
        w0_scored = s_("w0_scored")
        w0_ready = s_("w0_ready")
        u_scored = s_("u_scored")
        v1_ready = s_("v1_ready")
        w1_scored = s_("w1_scored")
        w1_ready = s_("w1_ready")
        o_scored = s_("o_scored")
        o_ready = s_("o_ready")
        o_stored = s_("o_stored")

        def after(n, u):
            return n * 2 + (u + 1)

        def at(n, v, u):
            return (n * LEVELS + v) * 2 + (u + 1)

        def at1(n, v, u):
            return (n * (LEVELS - 1) + (v - 1)) * 2 + (u + 1)

        def half(x, v, which):
            return x.rearrange("p k (b h i) -> p k b h i", h=2, i=1 << v)[:, :, :, which, :]

        with st.block() as block:
            @block.sync
            def _(sp):
                def duo(n, w, j):
                    if not early(n, 2):
                        sp.wait_ge(cross_scored, (n - 1) * 2)
                        sp.wait_ge(w0_scored, (n - 1) * 2)
                        sp.wait_ge(v1_ready, (n - 1) * 2)
                    for u in range(2):
                        sp.dma_start(src[:, w, u, :, :], unit_in[bass.ds(n * 2 + u, 1)]
                                     .rearrange("a p c t -> (a p) c t")).then_inc(src_loaded[w], 16)
                        sp.dma_start(val[:, w, u, :, :], unit_v[bass.ds(n * 2 + u, 1)]
                                     .rearrange("a p c t -> (a p) c t")).then_inc(val_loaded[w], 16)
                    if not early(n, 1):
                        store(n - 1)

                def store(n):
                    for u in range(2):
                        sp.wait_ge(o_ready, after(n, u))
                        sp.dma_start(unit_o[bass.ds(n * 2 + u, 1)].rearrange("a p c t -> (a p) c t"),
                                     osb[:, u, :, :, :].rearrange("p s h v -> p s (h v)")).then_inc(o_stored, 16)
                over_pairs(sp, DUOS, duo)
                store(DUOS - 1)
                sp.wait_ge(o_stored, 32 * DUOS)

            @block.gpsimd
            def _(pool):
                pool.memset(LT[:, :, :, :, :], 0.0).then_inc(masks_ready, 1)
                pool.memset(mask[:, :, :], 1.0).then_inc(masks_ready, 1)
                for v in range(LEVELS):
                    c = 1 << v
                    nb = P // (2 * c)
                    m = mask[:, v, :].rearrange("p (b i) -> p b i", b=nb)
                    pool.wait_ge(masks_ready, 2 * v + 2)
                    pool.affine_select(out=m, in_=m, compare_op=ALU.is_ge, fill=0.0, base=0,
                                       pattern=[[-2 * c, nb], [0, c]], channel_multiplier=1).then_inc(masks_ready, 1)
                    pool.wait_ge(masks_ready, 2 * v + 3)
                    pool.affine_select(out=m, in_=m, compare_op=ALU.is_ge, fill=0.0, base=c - 1,
                                       pattern=[[2 * c, nb], [0, c]], channel_multiplier=-1).then_inc(masks_ready, 1)

                def duo(n, w, j):
                    for u in range(2):
                        pool.wait_ge(diag_scored, after(n, u))
                        a = src[:, w, u, 2, :]
                        pool.tensor_tensor(src[:, w, u, 0:2, :], src[:, w, u, 0:2, :],
                                           a.unsqueeze(1).to_broadcast([P, 2, L]), ALU.mult).then_inc(decayed, 1)
                    for v in range(LEVELS):
                        c = 1 << v
                        nb = L // (2 * c)
                        for u in range(2):
                            tot = (src[:, w, u, 2, :] if v == 0 else total[:, u, (v - 1) % 2, 0:2 * nb]
                                   ).rearrange("p (b h) -> p b h", h=2)
                            if v == 0:
                                pool.wait_ge(decayed, after(n, u))
                            else:
                                pool.wait_ge(total_ready, at(n, v - 1, u))
                            pool.wait_ge(scored, at(n, v, u))
                            kq = src[:, w, u, 0:2, :].rearrange("p a (b h i) -> p a b h i", b=nb, h=2)[:, :, :, 1, :]
                            for x in range(2):
                                ins = pool.tensor_tensor(kq[:, x], kq[:, x],
                                                         tot[:, :, 0].unsqueeze(2).to_broadcast([P, nb, c]), ALU.mult)
                            ins.then_inc(kq_ready, 1)
                            kg = src[:, w, u, 3, :].rearrange("p (b h i) -> p b h i", b=nb, h=2)[:, :, 0, :]
                            pool.tensor_tensor(kg, kg, tot[:, :, 1].unsqueeze(2).to_broadcast([P, nb, c]), ALU.mult
                                               ).then_inc(kg_ready, 1)
                            pool.tensor_tensor(total[:, u, v % 2, 0:nb], tot[:, :, 0], tot[:, :, 1], ALU.mult
                                               ).then_inc(total_ready, 1)
                            pool.wait_ge(part_ready, at(n, v, u))
                            if v == 0:
                                pool.wait_ge(diag_ready, after(n, u))
                            else:
                                pool.wait_ge(bt_ready, at(n, v - 1, u))
                            bt = half(BT[:, u, :, :], v, 1)
                            pool.tensor_tensor(bt, bt, part[:, u, :, :].rearrange("p k (b i) -> p k b i", i=c), ALU.add
                                               ).then_inc(bt_ready, 1)
                over_pairs(pool, DUOS, duo)

            @block.tensor
            def _(pe):
                pe.wait_ge(masks_ready, 2 * LEVELS + 2)

                def level_scores(n, w, v, u):
                    if v == 0:
                        pe.wait_ge(decayed, after(n, u))
                        pe.wait_ge(diag_ready, after(n, u))
                    else:
                        pe.wait_ge(kq_ready, at(n, v - 1, u))
                        pe.wait_ge(kg_ready, at(n, v - 1, u))
                        pe.wait_ge(lt_ready, at(n, v - 1, u))
                        pe.wait_ge(part_ready, at(n, v - 1, u))
                    for k in range(TAU):
                        h, s = divmod(k, 2)
                        rows, cols = slice(h * DK, (h + 1) * DK), slice(s * P, (s + 1) * P)
                        ins = pe.matmul(halves(u)[:, k, :, :].rearrange("p a (b i) -> p a b i", i=1 << v),
                                        src[rows, w, u, 3, cols], half(src[rows, w, u, 0:2, cols], v, 1),
                                        start=True, stop=True)
                    ins.then_inc(scored, 1)

                def level_first(n, v, u):
                    pe.wait_ge(lt_ready, at(n, v, u))
                    if v == 0:
                        if not early(n, 1):
                            pe.wait_ge(w1_ready, after(n - 1, u))
                        for k in range(TAU):
                            ins = pe.transpose(wp[:, u, k, :], LT[:, u, 0, k, :], ident[:, :])
                    else:
                        pe.wait_ge(t_ready, at(n, v - 1, u))
                        for k in range(TAU):
                            ins = pe.matmul(wp[:, u, k, :], LT[:, u, v, k, :], T[:, u, k, :], start=True, stop=True)
                    ins.then_inc(r_scored, 1)

                def level_second(n, v, u):
                    pe.wait_ge(r_ready, at1(n, v, u))
                    if v == 1 and not early(n, 1):
                        pe.wait_ge(o_ready, after(n - 1, u))
                    for k in range(TAU):
                        if v < LEVELS - 1:
                            pe.matmul(wp[:, u, k, :], X[:, u, k, :], R[:, u, k, :], start=True, stop=True)
                        ins = pe.matmul(dp[:, u, k, :], R[:, u, k, :], X[:, u, k, :], start=True, stop=True)
                    ins.then_inc(d_scored, 1)

                def duo(n, w, j):
                    pe.wait_ge(src_loaded[w], (j + 1) * 32)
                    for u in range(2):
                        if not early(n, 1):
                            pe.wait_ge(cross_ready, after(n - 1, u))
                        for k in range(TAU):
                            h, s = divmod(k, 2)
                            rows, cols = slice(h * DK, (h + 1) * DK), slice(s * P, (s + 1) * P)
                            ins = pe.matmul(diag(u)[:, k, :], src[rows, w, u, 3, cols], src[rows, w, u, 1, cols],
                                            start=True, stop=True)
                        ins.then_inc(diag_scored, 1)
                    for u in range(2):
                        level_scores(n, w, 0, u)
                    for v in range(LEVELS):
                        for u in range(2):
                            level_first(n, v, u)
                        if v < LEVELS - 1:
                            for u in range(2):
                                level_scores(n, w, v + 1, u)
                        if v > 0:
                            for u in range(2):
                                level_second(n, v, u)
                    pe.wait_ge(val_loaded[w], (j + 1) * 32)
                    for u in range(2):
                        pe.wait_ge(kq_ready, at(n, LEVELS - 1, u))
                        pe.wait_ge(kg_ready, at(n, LEVELS - 1, u))
                        pe.wait_ge(lt_ready, at(n, LEVELS - 1, u))
                        pe.wait_ge(part_ready, at(n, LEVELS - 1, u))
                        for h in range(2):
                            rows = slice(h * DK, (h + 1) * DK)
                            ins = pe.matmul(across(u)[:, h, :, :], src[rows, w, u, 3, 0:P], src[rows, w, u, 0:2, P:L],
                                            start=True, stop=True)
                        ins.then_inc(cross_scored, 1)
                        pe.wait_ge(t_ready, at(n, LEVELS - 1, u))
                        for h in range(2):
                            ins = pe.matmul(wp[:, u, h, :], X[:, u, 2 * h, :], val[:, w, u, 0, h * DV:(h + 1) * DV],
                                            start=True, stop=True)
                        ins.then_inc(w0_scored, 1)
                    for u in range(2):
                        pe.wait_ge(cross_ready, after(n, u))
                        pe.wait_ge(w0_ready, after(n, u))
                        for h in range(2):
                            ins = pe.matmul(wp[:, u, 2 + h, :], cross_[:, u, h, 0, :], W[:, u, 0, h, :],
                                            start=True, stop=True)
                        ins.then_inc(u_scored, 1)
                    for u in range(2):
                        pe.wait_ge(v1_ready, after(n, u))
                        for h in range(2):
                            ins = pe.matmul(wp[:, u, h, :], X[:, u, 2 * h + 1, :], V1[:, u, h, :],
                                            start=True, stop=True)
                        ins.then_inc(w1_scored, 1)
                    for u in range(2):
                        pe.wait_ge(w1_ready, after(n, u))
                        pe.wait_ge(bt_ready, at(n, LEVELS - 1, u))
                        pe.wait_ge(t_ready, at(n, LEVELS - 1, u))
                        for h in range(2):
                            pe.matmul(outputs(u)[:, 0, h, :], BT[:, u, 2 * h, :], W[:, u, 0, h, :], start=True, stop=True)
                            pe.matmul(outputs(u)[:, 1, h, :], BT[:, u, 2 * h + 1, :], W[:, u, 1, h, :],
                                      start=True, stop=False)
                            ins = pe.matmul(outputs(u)[:, 1, h, :], cross_[:, u, h, 1, :], W[:, u, 0, h, :],
                                            start=False, stop=True)
                        ins.then_inc(o_scored, 1)
                over_pairs(pe, DUOS, duo)

            @block.vector
            def _(dve):
                dve.wait_ge(masks_ready, 2 * LEVELS + 2)
                eye = ident[:, :].unsqueeze(1).to_broadcast([P, TAU, P])

                def cut_scores(n, v, u):
                    m = mask[:, v, :].rearrange("p (b i) -> p b i", i=1 << v).unsqueeze(1).to_broadcast(
                        [P, TAU, P >> (v + 1), 1 << v])
                    whole = mask[:, v, :].unsqueeze(1).to_broadcast([P, TAU, P // 2])
                    dve.wait_ge(scored, at(n, v, u))
                    dve.tensor_tensor(half(LT[:, u, v, :, :], v, 1),
                                      halves(u)[:, :, 0, :].rearrange("p k (b i) -> p k b i", i=1 << v), m,
                                      ALU.mult).then_inc(lt_ready, 1)
                    if v > 0:
                        dve.wait_ge(bt_ready, at(n, v - 1, u))
                    dve.tensor_tensor(part[:, u, :, :], halves(u)[:, :, 1, :], whole, ALU.mult).then_inc(part_ready, 1)

                def update(n, v, u):
                    if v == 0:
                        dve.wait_ge(lt_ready, at(n, 0, u))
                        dve.tensor_tensor(X[:, u, :, :], eye, LT[:, u, 0, :, :], ALU.subtract)
                        dve.wait_ge(r_scored, at(n, 0, u))
                        dve.tensor_tensor(T[:, u, :, :], eye, wp[:, u, :, :], ALU.subtract).then_inc(t_ready, 1)
                        return
                    dve.wait_ge(d_scored, at1(n, v, u))
                    if v < LEVELS - 1:
                        first = half(T[:, u, :, :], v, 0)
                        dve.tensor_tensor(first, first, half(wp[:, u, :, :], v, 0), ALU.subtract)
                    second = half(X[:, u, :, :], v, 1)
                    dve.tensor_tensor(second, second, half(dp[:, u, :, :], v, 1), ALU.subtract).then_inc(t_ready, 1)

                def duo(n, w, j):
                    for u in range(2):
                        dve.wait_ge(diag_scored, after(n, u))
                        if not early(n, 1):
                            dve.wait_ge(o_scored, after(n - 1, u))
                        dve.tensor_tensor(BT[:, u, :, :], diag(u), eye, ALU.mult).then_inc(diag_ready, 1)
                    for u in range(2):
                        cut_scores(n, 0, u)
                    for v in range(LEVELS):
                        if v < LEVELS - 1:
                            for u in range(2):
                                cut_scores(n, v + 1, u)
                        for u in range(2):
                            update(n, v, u)
                    for u in range(2):
                        dve.wait_ge(cross_scored, after(n, u))
                        dve.tensor_copy(cross_[:, u, :, :, :], across(u)).then_inc(cross_ready, 1)
                    for u in range(2):
                        dve.wait_ge(u_scored, after(n, u))
                        dve.wait_ge(val_loaded[w], (j + 1) * 32)
                        dve.tensor_tensor(V1[:, u, :, :], val[:, w, u, 1, :].rearrange("p (h v) -> p h v", h=2),
                                          wp[:, u, 2:4, :], ALU.subtract).then_inc(v1_ready, 1)
                over_pairs(dve, DUOS, duo)

            @block.scalar
            def _(act):
                def duo(n, w, j):
                    for v in range(1, LEVELS):
                        for u in range(2):
                            act.wait_ge(r_scored, at(n, v, u))
                            act.activation(R[:, u, :, :], wp[:, u, :, :], ACT.Copy).then_inc(r_ready, 1)
                    for u in range(2):
                        act.wait_ge(w0_scored, after(n, u))
                        act.activation(W[:, u, 0, :, :], wp[:, u, 0:2, :], ACT.Copy).then_inc(w0_ready, 1)
                    for u in range(2):
                        act.wait_ge(w1_scored, after(n, u))
                        act.activation(W[:, u, 1, :, :], wp[:, u, 0:2, :], ACT.Copy).then_inc(w1_ready, 1)
                    for u in range(2):
                        act.wait_ge(o_scored, after(n, u))
                        if not early(n, 1):
                            act.wait_ge(o_stored, n * 32)
                        act.activation(osb[:, u, :, :, :], outputs(u), ACT.Copy).then_inc(o_ready, 1)
                over_pairs(act, DUOS, duo)


def gate_stage(nc, name, X, XN, XNT, Y, ident, t, unit_o):
    EPS = 1e-6
    S = S_HEADS
    with Stage(nc, name) as st:
        wo = st.sb("wo", [P, S, D])
        whn = st.sb("whn", [P, S, DV])
        wu1 = st.sb("wu1", [P, R_AU])
        bu1 = st.sb("bu1", [R_AU, 1])
        wu2 = st.sb("wu2", [R_AU, D])
        bu2 = st.sb("bu2", [P, D])
        U1 = st.sb("U1", [R_AU, NT])
        o = st.sb("o", [P, 2, S, DV])
        sq = st.sb("sq", [P, 2, S, DV])
        ms = st.sb("ms", [P, 2, S])
        var = st.sb("var", [P, 2, S])
        rt = st.sb("rt", [P, TILES, S])
        rs = st.sb("rs", [P, 2, S])
        on = st.sb("on", [P, 2, S, DV])
        on2 = st.sb("on2", [P, 2, S, DV])
        oT = st.sb("oT", [P, 2, S, P])
        u1 = st.sb("u1", [R_AU, 2, P])
        gz = st.sb("gz", [P, TILES, D])
        gate = st.sb("gate", [P, TILES, D])
        gated = st.sb("gated", [P, 2, D])
        up_ = st.ps("up", [R_AU, 2, 512])
        tp = st.ps("tp", [P, S, P])
        gp = st.ps("gp", [P, 2, 512])
        op = st.ps("op", [P, 2, 512])
        loaded = st.sem("loaded")
        u_projected = st.sem("u_projected")
        u_ready = st.sem("u_ready")
        g_projected = st.sem("g_projected")
        gz_ready = st.sem("gz_ready")
        g_ready = st.sem("g_ready")
        o_loaded = [st.sem("o_loaded0"), st.sem("o_loaded1")]
        squared = st.sem("squared")
        ms_ready = st.sem("ms_ready")
        var_ready = st.sem("var_ready")
        rt_ready = st.sem("rt_ready")
        rs_ready = st.sem("rs_ready")
        on_ready = st.sem("on_ready")
        on2_ready = st.sem("on2_ready")
        turned = st.sem("turned")
        oT_ready = st.sem("oT_ready")
        projected = st.sem("projected")
        gated_ready = st.sem("gated_ready")
        y_ready = st.sem("y_ready")
        added = st.sem("added")
        C = 512

        with st.block() as block:
            @block.sync
            def _(sp):
                for dst, src in [(wo[:, :, :], t["L1_attn_w_out"].rearrange("(h v) d -> v h d", v=DV)),
                                 (whn[:, :, :].rearrange("p h v -> p (h v)"),
                                  t["L1_attn_w_hn"].rearrange("h v -> (h v)").partition_broadcast(P)),
                                 (wu1[:, :], t["L1_attn_w_u1"]), (bu1[:, :], column(t["L1_attn_b_u1"], 0, R_AU)),
                                 (wu2[:, :], t["L1_attn_w_u2"]), (bu2[:, :], t["L1_attn_b_u2"].partition_broadcast(P))]:
                    sp.dma_start(dst, src).then_inc(loaded, 16)
                ov = unit_o.rearrange("(b x) p s f -> b p s x f", x=PAIRS_H)

                def unit(n, u, j):
                    if not early(n, 2):
                        sp.wait_ge(on_ready, n - 1)
                    sp.dma_start(o[:, u, :, :].rearrange("p (x h) v -> p x (h v)", x=PAIRS_H),
                                 ov[bass.ds(j, 1), :, u, :, :].rearrange("b p x f -> (b p) x f")
                                 ).then_inc(o_loaded[u], 16)
                over_pairs(sp, TILES, unit)

            @block.gpsimd
            def _(pool):
                def unit(n, u, j):
                    pool.wait_ge(on_ready, n + 1)
                    if not early(n, 2):
                        pool.wait_ge(turned, n - 1)
                    pool.tensor_tensor(on2[:, u, :, :], on[:, u, :, :], whn[:, :, :], ALU.mult).then_inc(on2_ready, 1)
                pool.wait_ge(loaded, 96)
                over_pairs(pool, TILES, unit)

            @block.tensor
            def _(pe):
                pe.wait_ge(loaded, 96)
                for c in range(NT // C):
                    if c >= 2:
                        pe.wait_ge(u_ready, c - 1)
                    pe.matmul(up_[:, c % 2, :], wu1[:, :], XNT[:, c * C:(c + 1) * C], start=True, stop=True
                              ).then_inc(u_projected, 1)
                for n in range(TILES):
                    pe.wait_ge(u_ready, n // 4 + 1)
                    if n >= 2:
                        pe.wait_ge(gz_ready, n - 1)
                    pe.matmul(gp[:, n % 2, 0:D], U1[:, n * P:(n + 1) * P], wu2[:, :], start=True, stop=True
                              ).then_inc(g_projected, 1)

                def unit(n, u, j):
                    pe.wait_ge(on2_ready, n + 1)
                    if not early(n, 1):
                        pe.wait_ge(oT_ready, n)
                    for h in range(S):
                        ins = pe.transpose(tp[:, h, :], on2[:, u, h, :], ident[:, :])
                    ins.then_inc(turned, 1)
                    pe.wait_ge(oT_ready, n + 1)
                    if not early(n, 2):
                        pe.wait_ge(gated_ready, n - 1)
                    for h in range(S):
                        ins = pe.matmul(op[:, u, 0:D], oT[:, u, h, :], wo[:, h, :], start=(h == 0), stop=(h == S - 1))
                    ins.then_inc(projected, 1)
                over_pairs(pe, TILES, unit)

            @block.scalar
            def _(act):
                act.wait_ge(loaded, 96)
                for c in range(NT // C):
                    act.wait_ge(u_projected, c + 1)
                    act.activation(U1[:, c * C:(c + 1) * C], up_[:, c % 2, :], ACT.Silu, bias=bu1[:, 0:1]
                                   ).then_inc(u_ready, 1)
                act.wait_ge(gz_ready, TILES)
                act.activation(gate[:, :, :], gz[:, :, :], ACT.Sigmoid).then_inc(g_ready, 1)

                def squares(n, u, j):
                    act.wait_ge(o_loaded[u], (j + 1) * 16)
                    if not early(n, 2):
                        act.wait_ge(ms_ready, n - 1)
                    act.activation(sq[:, u, :, :], o[:, u, :, :], ACT.Square).then_inc(squared, 1)
                    act.wait_ge(var_ready, n + 1)
                    act.activation(rt[:, u, :], var[:, u, :], ACT.Sqrt).then_inc(rt_ready, 1)

                def unit(n, u, j):
                    if not (isinstance(n, int) and n == TILES - 1):
                        squares(n + 1, 1 - u, j + u)
                    act.wait_ge(turned, n + 1)
                    if not early(n, 2):
                        act.wait_ge(projected, n - 1)
                    act.activation(oT[:, u, :, :], tp[:, :, :], ACT.Copy).then_inc(oT_ready, 1)
                squares(0, 0, 0)
                over_pairs(act, TILES, unit)

            @block.vector
            def _(dve):
                dve.wait_ge(loaded, 96)
                for n in range(TILES):
                    dve.wait_ge(g_projected, n + 1)
                    dve.tensor_tensor(gz[:, n, :], gp[:, n % 2, 0:D], bu2[:, :], ALU.add).then_inc(gz_ready, 1)
                dve.wait_ge(g_ready, 1)

                def norm(n, u):
                    dve.wait_ge(squared, n + 1)
                    if not early(n, 2):
                        dve.wait_ge(var_ready, n - 1)
                        dve.wait_ge(rt_ready, n - 1)
                    dve.tensor_reduce(ms[:, u, :], sq[:, u, :, :], AX.X, ALU.add).then_inc(ms_ready, 1)
                    dve.wait_ge(ms_ready, n + 1)
                    dve.tensor_scalar(var[:, u, :], ms[:, u, :], 1.0 / DV, EPS, ALU.mult, ALU.add).then_inc(var_ready, 1)
                    dve.wait_ge(rt_ready, n + 1)
                    dve.reciprocal(rs[:, u, :], rt[:, u, :]).then_inc(rs_ready, 1)
                    dve.wait_ge(rs_ready, n + 1)
                    if not early(n, 2):
                        dve.wait_ge(on2_ready, n - 1)
                    dve.tensor_tensor(on[:, u, :, :], o[:, u, :, :], rs[:, u, :].unsqueeze(2).to_broadcast([P, S, DV]),
                                      ALU.mult).then_inc(on_ready, 1)

                def unit(n, u, j):
                    if not (isinstance(n, int) and n == TILES - 1):
                        norm(n + 1, 1 - u)
                    dve.wait_ge(projected, n + 1)
                    one = lambda a: a[:, bass.ds(n, 1), :].rearrange("p a d -> p (a d)")
                    dve.tensor_tensor(gated[:, u, :], op[:, u, 0:D], one(gate), ALU.mult).then_inc(gated_ready, 1)
                    dve.wait_ge(gated_ready, n + 1)
                    dve.tensor_tensor(one(Y), gated[:, u, :], one(XN), ALU.add).then_inc(y_ready, 1)
                    dve.wait_ge(y_ready, n + 1)
                    dve.tensor_tensor(one(X), one(X), one(Y), ALU.add).then_inc(added, 1)
                norm(0, 0)
                over_pairs(dve, TILES, unit)


def delta(nc, X, ident, t):
    unit_in = nc.dram_tensor("unit_in", [B * PAIRS_H, P, 4, L], F32, kind="Internal").ap()
    unit_v = nc.dram_tensor("unit_v", [B * PAIRS_H, P, 2, 2 * DV], F32, kind="Internal").ap()
    unit_o = nc.dram_tensor("unit_o", [B * PAIRS_H, P, 2, 2 * DV], F32, kind="Internal").ap()
    with ExitStack() as ctx:
        XN = ctx.enter_context(nc.sbuf_tensor("d_XN", [P, TILES, D], F32))
        XNT = ctx.enter_context(nc.sbuf_tensor("d_XNT", [P, NT], F32))
        norm_stage(nc, "dn", X, XNT, ident, XN=XN)
        with ExitStack() as early_part:
            HT = early_part.enter_context(nc.sbuf_tensor("d_HT", [P, NT], F32))
            norm_stage(nc, "dh", XN, HT, ident, eps=1e-6, centre=False, weight=t["L1_attn_w_norm_in"])
            conv_stage(nc, "dc", HT, t)
            SD = early_part.enter_context(nc.sbuf_tensor("d_SD", [P, PAIRS_H, B, L], F32))
            AUT = early_part.enter_context(nc.sbuf_tensor("d_AUT", [R_AU, NT], F32))
            spike_stage(nc, "ds", HT, SD, AUT, t)
            prepare_stage(nc, "dp", HT, SD, AUT, t, unit_in, unit_v)
        delta_stage(nc, "dd", ident, unit_in, unit_v, unit_o)
        Y = ctx.enter_context(nc.sbuf_tensor("d_Y", [P, TILES, D], F32))
        gate_stage(nc, "dg", X, XN, XNT, Y, ident, t, unit_o)
        norm_stage(nc, "df", Y, XNT, ident, eps=1e-6, centre=False, weight=t["L1_attn_w_ffn"])
        cut = [slice(s * P, (s + 1) * P) for s in range(F_FF // P)]
        experts_stage(nc, "de", X, XNT, ident, None, [t["L1_attn_w_ff1"][:, c] for c in cut],
                      [t["L1_attn_w_ff3"][:, c] for c in cut], [t["L1_attn_w_ff2"][c, :] for c in cut], 0, 1,
                      direct=True)

NAMES = ["x", "ctx_768", "L0_attn_Wqkv_w", "L0_attn_Wqkv_b", "L0_attn_out_w", "L0_attn_out_b", "L0_attn_W_static",
         "L0_attn_Lambda_raw", "L0_attn_Gamma", "L0_attn_gate_w1", "L0_attn_gate_b1", "L0_attn_gate_w2",
         "L0_attn_gate_b2", "L0_xattn_Wq", "L0_xattn_bq", "L0_xattn_Wk", "L0_xattn_bk", "L0_xattn_Wv", "L0_xattn_bv",
         "L0_xattn_Wo", "L0_xattn_bo", "L0_ffn_gate_w", "L0_ffn_gate_bias", "L0_ffn_expert_gate",
         "L0_ffn_expert_up", "L0_ffn_expert_down", "L0_ffn_shared_gate", "L0_ffn_shared_up",
         "L0_ffn_shared_down", "L1_attn_w_norm_in", "L1_attn_conv_w", "L1_attn_conv_b", "L1_attn_wq",
         "L1_attn_wk", "L1_attn_wv", "L1_attn_w_out", "L1_attn_w_spike", "L1_attn_w_au", "L1_attn_b_au",
         "L1_attn_w_ad", "L1_attn_b_ad", "L1_attn_alpha_spike", "L1_attn_w_beta", "L1_attn_b_beta",
         "L1_attn_beta_spike", "L1_attn_w_hn", "L1_attn_w_u1", "L1_attn_b_u1", "L1_attn_w_u2", "L1_attn_b_u2",
         "L1_attn_w_ffn", "L1_attn_w_ff1", "L1_attn_w_ff3", "L1_attn_w_ff2", "L1_xattn_Wq", "L1_xattn_bq",
         "L1_xattn_Wk", "L1_xattn_bk", "L1_xattn_Wv", "L1_xattn_bv", "L1_xattn_Wo", "L1_xattn_bo",
         "L1_xattn_scale", "L1_ffn_gate_w", "L1_ffn_we_gate", "L1_ffn_we_up", "L1_ffn_we_down",
         "L1_ffn_ws_gate", "L1_ffn_ws_up", "L1_ffn_ws_down"]


def decoder(nc, t, out):
    def dram(name, shape, dt=F32):
        return nc.dram_tensor(name, shape, dt, kind="Internal").ap()

    with ExitStack() as ctx:
        X = ctx.enter_context(nc.sbuf_tensor("X", [P, TILES, D], F32))
        ident = ctx.enter_context(nc.sbuf_tensor("ident", [P, P], F32))
        setup_stage(nc, X, ident, t["x"])
        q_parts = dram("q_parts", [B, 3, P, L], BF16)
        k_self = dram("k_self", [B, 3, P, L], BF16)
        k_ctx = dram("k_ctx", [B, 3, P, LC], BF16)
        v_self = dram("v_self", [B, H // HG, L, HG * HD])
        v_ctx = dram("v_ctx", [B, H // HG, LC, HG * HD])
        y_units = dram("y_units", [UNITS, L, HG * HD])

        with nc.sbuf_tensor("XT", [P, NT], F32) as XT:
            norm_stage(nc, "n0", X, XT, ident)
            w, bias = t["L0_attn_Wqkv_w"], t["L0_attn_Wqkv_b"]
            project_stage(nc, "q0", XT, w, bias, HD ** -0.5, q_parts, 0)
            project_stage(nc, "k0", XT, w, bias, 1.0, k_self, P)
            value_stage(nc, "v0", XT, w, bias, v_self)
            attention_stage(nc, "s0", q_parts, k_self, v_self, y_units, ident, L, H // HG, causal=True)
            mix_stage(nc, "m0", X, XT, ident, t, y_units)
        cross(nc, "c0", X, ident, t, "L0_xattn", q_parts, k_ctx, v_ctx, y_units, clip=True)
        moe0(nc, X, ident, t)
        delta(nc, X, ident, t)
        cross(nc, "c1", X, ident, t, "L1_xattn", q_parts, k_ctx, v_ctx, y_units, clip=False)
        moe1(nc, X, ident, t)
        with Stage(nc, "store") as st:
            stored = st.sem("stored")
            with st.block() as block:
                @block.sync
                def _(sp):
                    sp.dma_start(out.rearrange("b (s p) d -> p (b s) d", p=P), X[:, :, :]).then_inc(stored, 16)
                    sp.wait_ge(stored, 16)


def kernel(**inputs):
    import numpy as _np
    import concourse.bacc as _bacc
    from concourse import mybir as _mybir
    from concourse.bass_utils import run_bass_kernel_spmd as _run

    nc = _bacc.Bacc("TRN2", target_bir_lowering=False, num_devices=1)
    arrays, t = {}, {}
    for name in NAMES:
        a = _np.ascontiguousarray(inputs[name])
        arrays[f"in_{name}_dram"] = a
        t[name] = nc.dram_tensor(f"in_{name}_dram", a.shape, _mybir.dt.from_np(a.dtype), kind="ExternalInput").ap()
    out = nc.dram_tensor("out_0_dram", (B, L, D), F32, kind="ExternalOutput").ap()
    decoder(nc, t, out)
    r = _run(nc, [arrays], core_ids=[0])
    return r.results[0]["out_0_dram"]
```
